# Optimizing a Trainium2 kernel written in Bass

```python
import numpy as np
import jax
import jax.numpy as jnp

def _softmax(x, axis=-1):
    return jax.nn.softmax(x, axis=axis)

def _gelu(x):
    return jax.nn.gelu(x, approximate=True)

def _silu(x):
    return jax.nn.silu(x)

def _sigmoid(x):
    return jax.nn.sigmoid(x)

def _layernorm(x, axis=-1, eps=1e-05):
    m = jnp.mean(x, axis=axis, keepdims=True)
    v = jnp.var(x, axis=axis, keepdims=True)
    return (x - m) / jnp.sqrt(v + eps)

def _scatter_add(tgt, idx, src, axis=0):
    return tgt.at[idx].add(src)

def _segment_sum(src, seg, n):
    return jax.ops.segment_sum(src, seg, n)
kernel_name = 'mk_flamingo_gated_d2_seqx_r8_75bba5'

def setup_inputs(seed: int=0):
    np.random.seed(seed)
    _w = jnp.asarray

    def _rec_inputs():
        import jax
        import jax.numpy as jnp
        _rk = jax.random.key(seed)
        x = 4.136e-05 + 0.9999 * jax.random.normal(jax.random.fold_in(_rk, 1), (4, 256, 256), jnp.float32)
        _lenS = 256 - jax.random.randint(jax.random.fold_in(_rk, 7), (4,), 0, max(1, 256 // 4) + 1, jnp.int32)
        _lenS2 = 256 - jax.random.randint(jax.random.fold_in(_rk, 8), (4,), 0, max(1, 256 // 4) + 1, jnp.int32)
        _ctx_1024P = jax.random.normal(jax.random.fold_in(_rk, 11), (4, 16, 128), jnp.float32)
        _ctx_1024c = jax.random.dirichlet(jax.random.fold_in(_rk, 511), 0.3 * jnp.ones((16,), jnp.float32), (4, 256))
        _ctx_1024t = jnp.einsum('bsk,bkd->bsd', _ctx_1024c, _ctx_1024P)
        _ctx_1024t = _ctx_1024t * jax.lax.rsqrt(jnp.mean(jnp.square(_ctx_1024t)) + 1e-12) * 0.953939
        ctx_1024 = -0.000292821 + 1.00034 * (_ctx_1024t + 0.3 * jax.random.normal(jax.random.fold_in(_rk, 611), (4, 256, 128), jnp.float32))
        fside_BxSx2_0 = jax.random.uniform(jax.random.fold_in(_rk, 12), (4, 256, 2), jnp.float32, 0.0, 0.999707)
        _g = jax.random.normal(jax.random.fold_in(_rk, 9001), (2, 2), jnp.float32)
        _g = jnp.sign(_g) * jnp.maximum(jnp.abs(_g), 1.0) + (_g == 0) * 1.0
        g_xattn = _g[0]
        g_ffn = _g[1]
        return (x, ctx_1024, fside_BxSx2_0, g_xattn, g_ffn)
    x, ctx_1024, fside_BxSx2_0, g_xattn, g_ffn = _rec_inputs()

    def _L0_xattn_setup():
        import jax, jax.numpy as jnp
        import numpy as np
        import math
        B, L, DM = (2, 256, 128)
        DS, DC, EXP = (16, 4, 2)
        DI = EXP * DM
        DR = math.ceil(DM / 16)
        DT_MIN, DT_MAX, DT_FLOOR = (0.001, 0.1, 0.0001)

        def _ssm_forward(hidden_states, z, in_proj_w, conv_w, conv_b, x_proj_w, dt_proj_w, dt_proj_b, A_log, D):
            b = hidden_states.shape[0]
            x = jnp.einsum('ed,bld->bel', in_proj_w, hidden_states)
            xp = jnp.pad(x, ((0, 0), (0, 0), (DC - 1, 0)))
            xc = jax.lax.conv_general_dilated(xp, conv_w[:, None, :], window_strides=(1,), padding='VALID', dimension_numbers=('NCH', 'OIH', 'NCH'), feature_group_count=DI)
            u = jax.nn.silu(xc + conv_b[None, :, None])
            x_dbl = jnp.einsum('ke,bel->bkl', x_proj_w, u)
            dt_lo = x_dbl[:, :DR]
            Bm = x_dbl[:, DR:DR + DS]
            Cm = x_dbl[:, DR + DS:]
            delta = jax.nn.softplus(jnp.einsum('er,brl->bel', dt_proj_w, dt_lo) + dt_proj_b[None, :, None])
            A = -jnp.exp(A_log)

            def step(state, xs):
                d_t, B_t, C_t, u_t = xs
                dA = jnp.exp(d_t[..., None] * A)
                state = state * dA + (d_t * u_t)[..., None] * B_t[:, None, :]
                y_t = jnp.einsum('ben,bn->be', state, C_t)
                return (state, y_t)
            xs = (jnp.moveaxis(delta, -1, 0), jnp.moveaxis(Bm, -1, 0), jnp.moveaxis(Cm, -1, 0), jnp.moveaxis(u, -1, 0))
            state0 = jnp.zeros((b, DI, DS), delta.dtype)
            _, ys = jax.lax.scan(step, state0, xs)
            y = jnp.moveaxis(ys, 0, -1)
            y = y + D[None, :, None] * u
            y = y * jax.nn.silu(z)
            return jnp.swapaxes(y, 1, 2)
        key = jax.random.key(seed)
        ks = jax.random.split(key, 8)
        hidden_states = jax.random.normal(ks[0], (B, L, DM), jnp.float32)
        z = jax.random.normal(ks[1], (B, DI, L), jnp.float32)
        in_proj_w = jax.random.normal(ks[2], (DI, DM), jnp.float32) * DM ** (-0.5)
        conv_w = jax.random.normal(ks[3], (DI, DC), jnp.float32) * DC ** (-0.5)
        conv_b = jnp.zeros((DI,), jnp.float32)
        x_proj_w = jax.random.normal(ks[4], (DR + 2 * DS, DI), jnp.float32) * DI ** (-0.5)
        dt_std = DR ** (-0.5)
        dt_proj_w = jax.random.uniform(ks[5], (DI, DR), jnp.float32, -dt_std, dt_std)
        dt = jnp.exp(jax.random.uniform(ks[6], (DI,), jnp.float32) * (math.log(DT_MAX) - math.log(DT_MIN)) + math.log(DT_MIN))
        dt = jnp.clip(dt, DT_FLOOR)
        dt_proj_b = dt + jnp.log(-jnp.expm1(-dt))
        A_log = jnp.log(jnp.broadcast_to(jnp.arange(1, DS + 1, dtype=jnp.float32), (DI, DS)))
        D = jnp.ones((DI,), jnp.float32)
        return dict(hidden_states=hidden_states, z=z, in_proj_w=in_proj_w, conv_w=conv_w, conv_b=conv_b, x_proj_w=x_proj_w, dt_proj_w=dt_proj_w, dt_proj_b=dt_proj_b, A_log=A_log, D=D)
    _L0_xattn_all = _L0_xattn_setup()
    _L0_xattn_in = {k: v for k, v in _L0_xattn_all.items() if k in ('in_proj_w', 'conv_w', 'conv_b', 'x_proj_w', 'dt_proj_w', 'dt_proj_b', 'A_log', 'D')}
    del _L0_xattn_all

    def _L0_ffn_setup():
        import jax, jax.numpy as jnp
        import numpy as np
        GOLDEN_CENTER = 1.0 / np.e
        GOLDEN_LOWER = 0.5 - np.log(4.0 / 3.0)
        GOLDEN_UPPER = 0.5

        def _golden_weights(x, Wr, temperature):
            inh = jax.nn.sigmoid(x @ Wr / temperature)
            in_zone = (inh >= GOLDEN_LOWER) & (inh <= GOLDEN_UPPER)
            distance = jnp.abs(inh - GOLDEN_CENTER)
            weights = jnp.exp(-distance / 0.1) * in_zone.astype(x.dtype)
            wsum = jnp.sum(weights, axis=-1, keepdims=True)
            no_expert = wsum < 1e-08
            fb = jnp.exp(-distance / 0.3)
            _, top2 = jax.lax.top_k(fb, 2)
            fb_mask = jnp.sum(jax.nn.one_hot(top2, weights.shape[-1], dtype=x.dtype), axis=-2)
            fb_w = fb * fb_mask
            fb_w = fb_w / jnp.maximum(jnp.sum(fb_w, axis=-1, keepdims=True), 1e-08)
            weights = jnp.where(no_expert, fb_w, weights)
            weights = weights / jnp.maximum(jnp.sum(weights, axis=-1, keepdims=True), 1e-08)
            return weights
        key = jax.random.key(seed)
        ks = jax.random.split(key, 5)
        B, T, D, E, F = (2, 256, 256, 8, 256)
        s_in = 1.0 / np.sqrt(D)
        s_f = 1.0 / np.sqrt(F)
        return {'x': jax.random.normal(ks[0], (B, T, D), dtype=jnp.float32), 'Wg': jax.random.normal(ks[1], (E, D, F), dtype=jnp.float32) * s_in, 'Wu': jax.random.normal(ks[2], (E, D, F), dtype=jnp.float32) * s_in, 'Wd': jax.random.normal(ks[3], (E, F, D), dtype=jnp.float32) * s_f, 'Wr': jax.random.normal(ks[4], (D, E), dtype=jnp.float32) * s_in, 'temperature': jnp.ones((1,), dtype=jnp.float32)}
    _L0_ffn_all = _L0_ffn_setup()
    _L0_ffn_in = {k: v for k, v in _L0_ffn_all.items() if k in ('Wg', 'Wu', 'Wd', 'Wr', 'temperature')}
    del _L0_ffn_all

    def _L1_xattn_setup():
        import jax, jax.numpy as jnp
        import numpy as np
        DIM = 256
        CTX_DIM = 128
        N_HEADS = 32
        HEAD_DIM = DIM // N_HEADS
        POS_DIM = 2
        B, N, CTXN = (2, 256, 256)
        ROPE_BASE = 10000.0

        def apply_axial_rope(x, pos):
            b, n, h, d = x.shape
            p = pos.shape[-1]
            dpa = d // p
            half = dpa // 2
            freqs = ROPE_BASE ** (-jnp.arange(half, dtype=x.dtype) / half)
            ang = pos[..., :, None] * freqs
            cos = jnp.cos(ang)[:, :, None, :, :]
            sin = jnp.sin(ang)[:, :, None, :, :]
            xr = x.reshape(b, n, h, p, half, 2)
            x1, x2 = (xr[..., 0], xr[..., 1])
            out = jnp.stack([x1 * cos - x2 * sin, x1 * sin + x2 * cos], axis=-1)
            return out.reshape(b, n, h, d)
        key = jax.random.key(seed)
        ks = jax.random.split(key, 8)
        x = jax.random.normal(ks[0], (B, N, DIM), jnp.float32)
        ctx = jax.random.normal(ks[1], (B, CTXN, CTX_DIM), jnp.float32)
        pos_map = jax.random.uniform(ks[2], (B, N, POS_DIM), jnp.float32)
        ctx_pos_map = jax.random.uniform(ks[3], (B, CTXN, POS_DIM), jnp.float32)
        Wq = jax.random.normal(ks[4], (DIM, DIM), jnp.float32) / np.sqrt(DIM)
        Wkv = jax.random.normal(ks[5], (CTX_DIM, 2 * DIM), jnp.float32) / np.sqrt(CTX_DIM)
        Wout = jax.random.normal(ks[6], (DIM, DIM), jnp.float32) / np.sqrt(DIM)
        bout = jnp.zeros((DIM,), jnp.float32)
        return {'x': x, 'ctx': ctx, 'pos_map': pos_map, 'ctx_pos_map': ctx_pos_map, 'Wq': Wq, 'Wkv': Wkv, 'Wout': Wout, 'bout': bout}
    _L1_xattn_all = _L1_xattn_setup()
    _L1_xattn_in = {k: v for k, v in _L1_xattn_all.items() if k in ('Wq', 'Wkv', 'Wout', 'bout')}
    del _L1_xattn_all

    def _L1_ffn_setup():
        import jax, jax.numpy as jnp
        import numpy as np
        B, S, D, F, E, K = (2, 256, 256, 1024, 8, 2)
        key = jax.random.key(seed)
        k0, k1, k2, k3 = jax.random.split(key, 4)
        scale = lambda k, shape, fan_in: jax.random.normal(k, shape, jnp.float32) * fan_in ** (-0.5)
        return {'inputs': jax.random.normal(k0, (B, S, D), jnp.float32), 'gate_w': scale(k1, (D, E), D), 'gate_b': jnp.zeros((E,), jnp.float32), 'w1': scale(k2, (E, D, F), D), 'b1': jnp.zeros((E, F), jnp.float32), 'w2': scale(k3, (E, F, D), F), 'b2': jnp.zeros((E, D), jnp.float32)}
    _L1_ffn_all = _L1_ffn_setup()
    _L1_ffn_in = {k: v for k, v in _L1_ffn_all.items() if k in ('gate_w', 'gate_b', 'w1', 'b1', 'w2', 'b2')}
    del _L1_ffn_all
    return {'x': x, 'ctx_1024': ctx_1024, 'fside_BxSx2_0': fside_BxSx2_0, 'g_xattn': g_xattn, 'g_ffn': g_ffn, 'L0_xattn_in_proj_w': _L0_xattn_in['in_proj_w'], 'L0_xattn_conv_w': _L0_xattn_in['conv_w'], 'L0_xattn_conv_b': _L0_xattn_in['conv_b'], 'L0_xattn_x_proj_w': _L0_xattn_in['x_proj_w'], 'L0_xattn_dt_proj_w': _L0_xattn_in['dt_proj_w'], 'L0_xattn_dt_proj_b': _L0_xattn_in['dt_proj_b'], 'L0_xattn_A_log': _L0_xattn_in['A_log'], 'L0_xattn_D': _L0_xattn_in['D'], 'L0_ffn_Wg': _L0_ffn_in['Wg'], 'L0_ffn_Wu': _L0_ffn_in['Wu'], 'L0_ffn_Wd': _L0_ffn_in['Wd'], 'L0_ffn_Wr': _L0_ffn_in['Wr'], 'L0_ffn_temperature': _L0_ffn_in['temperature'], 'L1_xattn_Wq': _L1_xattn_in['Wq'], 'L1_xattn_Wkv': _L1_xattn_in['Wkv'], 'L1_xattn_Wout': _L1_xattn_in['Wout'], 'L1_xattn_bout': _L1_xattn_in['bout'], 'L1_ffn_gate_w': _L1_ffn_in['gate_w'], 'L1_ffn_gate_b': _L1_ffn_in['gate_b'], 'L1_ffn_w1': _L1_ffn_in['w1'], 'L1_ffn_b1': _L1_ffn_in['b1'], 'L1_ffn_w2': _L1_ffn_in['w2'], 'L1_ffn_b2': _L1_ffn_in['b2']}

def reference(x, ctx_1024, fside_BxSx2_0, g_xattn, g_ffn, L0_xattn_in_proj_w, L0_xattn_conv_w, L0_xattn_conv_b, L0_xattn_x_proj_w, L0_xattn_dt_proj_w, L0_xattn_dt_proj_b, L0_xattn_A_log, L0_xattn_D, L0_ffn_Wg, L0_ffn_Wu, L0_ffn_Wd, L0_ffn_Wr, L0_ffn_temperature, L1_xattn_Wq, L1_xattn_Wkv, L1_xattn_Wout, L1_xattn_bout, L1_ffn_gate_w, L1_ffn_gate_b, L1_ffn_w1, L1_ffn_b1, L1_ffn_w2, L1_ffn_b2):
    import jax
    import jax.numpy as jnp

    def _L0_xattn_ref(hidden_states, z, in_proj_w, conv_w, conv_b, x_proj_w, dt_proj_w, dt_proj_b, A_log, D):
        import jax, jax.numpy as jnp
        import numpy as np
        import math
        B, L, DM = (2, 256, 128)
        DS, DC, EXP = (16, 4, 2)
        DI = EXP * DM
        DR = math.ceil(DM / 16)
        DT_MIN, DT_MAX, DT_FLOOR = (0.001, 0.1, 0.0001)

        def _ssm_forward(hidden_states, z, in_proj_w, conv_w, conv_b, x_proj_w, dt_proj_w, dt_proj_b, A_log, D):
            b = hidden_states.shape[0]
            x = jnp.einsum('ed,bld->bel', in_proj_w, hidden_states)
            xp = jnp.pad(x, ((0, 0), (0, 0), (DC - 1, 0)))
            xc = jax.lax.conv_general_dilated(xp, conv_w[:, None, :], window_strides=(1,), padding='VALID', dimension_numbers=('NCH', 'OIH', 'NCH'), feature_group_count=DI)
            u = jax.nn.silu(xc + conv_b[None, :, None])
            x_dbl = jnp.einsum('ke,bel->bkl', x_proj_w, u)
            dt_lo = x_dbl[:, :DR]
            Bm = x_dbl[:, DR:DR + DS]
            Cm = x_dbl[:, DR + DS:]
            delta = jax.nn.softplus(jnp.einsum('er,brl->bel', dt_proj_w, dt_lo) + dt_proj_b[None, :, None])
            A = -jnp.exp(A_log)

            def step(state, xs):
                d_t, B_t, C_t, u_t = xs
                dA = jnp.exp(d_t[..., None] * A)
                state = state * dA + (d_t * u_t)[..., None] * B_t[:, None, :]
                y_t = jnp.einsum('ben,bn->be', state, C_t)
                return (state, y_t)
            xs = (jnp.moveaxis(delta, -1, 0), jnp.moveaxis(Bm, -1, 0), jnp.moveaxis(Cm, -1, 0), jnp.moveaxis(u, -1, 0))
            state0 = jnp.zeros((b, DI, DS), delta.dtype)
            _, ys = jax.lax.scan(step, state0, xs)
            y = jnp.moveaxis(ys, 0, -1)
            y = y + D[None, :, None] * u
            y = y * jax.nn.silu(z)
            return jnp.swapaxes(y, 1, 2)
        return _ssm_forward(hidden_states, z, in_proj_w, conv_w, conv_b, x_proj_w, dt_proj_w, dt_proj_b, A_log, D)

    def _L0_ffn_ref(x, Wg, Wu, Wd, Wr, temperature):
        import jax, jax.numpy as jnp
        import numpy as np
        GOLDEN_CENTER = 1.0 / np.e
        GOLDEN_LOWER = 0.5 - np.log(4.0 / 3.0)
        GOLDEN_UPPER = 0.5

        def _golden_weights(x, Wr, temperature):
            inh = jax.nn.sigmoid(x @ Wr / temperature)
            in_zone = (inh >= GOLDEN_LOWER) & (inh <= GOLDEN_UPPER)
            distance = jnp.abs(inh - GOLDEN_CENTER)
            weights = jnp.exp(-distance / 0.1) * in_zone.astype(x.dtype)
            wsum = jnp.sum(weights, axis=-1, keepdims=True)
            no_expert = wsum < 1e-08
            fb = jnp.exp(-distance / 0.3)
            _, top2 = jax.lax.top_k(fb, 2)
            fb_mask = jnp.sum(jax.nn.one_hot(top2, weights.shape[-1], dtype=x.dtype), axis=-2)
            fb_w = fb * fb_mask
            fb_w = fb_w / jnp.maximum(jnp.sum(fb_w, axis=-1, keepdims=True), 1e-08)
            weights = jnp.where(no_expert, fb_w, weights)
            weights = weights / jnp.maximum(jnp.sum(weights, axis=-1, keepdims=True), 1e-08)
            return weights
        weights = _golden_weights(x, Wr, temperature)
        gate = jnp.einsum('btd,edf->betf', x, Wg)
        up = jnp.einsum('btd,edf->betf', x, Wu)
        h = jax.nn.silu(gate) * up
        e_out = jnp.einsum('betf,efd->betd', h, Wd)
        out = jnp.einsum('bte,betd->btd', weights, e_out)
        return out

    def _L1_xattn_ref(x, ctx, pos_map, ctx_pos_map, Wq, Wkv, Wout, bout):
        import jax, jax.numpy as jnp
        import numpy as np
        DIM = 256
        CTX_DIM = 128
        N_HEADS = 32
        HEAD_DIM = DIM // N_HEADS
        POS_DIM = 2
        B, N, CTXN = (2, 256, 256)
        ROPE_BASE = 10000.0

        def apply_axial_rope(x, pos):
            b, n, h, d = x.shape
            p = pos.shape[-1]
            dpa = d // p
            half = dpa // 2
            freqs = ROPE_BASE ** (-jnp.arange(half, dtype=x.dtype) / half)
            ang = pos[..., :, None] * freqs
            cos = jnp.cos(ang)[:, :, None, :, :]
            sin = jnp.sin(ang)[:, :, None, :, :]
            xr = x.reshape(b, n, h, p, half, 2)
            x1, x2 = (xr[..., 0], xr[..., 1])
            out = jnp.stack([x1 * cos - x2 * sin, x1 * sin + x2 * cos], axis=-1)
            return out.reshape(b, n, h, d)
        b, n, _ = x.shape
        ctx_n = ctx.shape[1]
        q = (x @ Wq).reshape(b, n, N_HEADS, HEAD_DIM)
        k, v = jnp.split(ctx @ Wkv, 2, axis=-1)
        k = k.reshape(b, ctx_n, N_HEADS, HEAD_DIM)
        v = v.reshape(b, ctx_n, N_HEADS, HEAD_DIM)
        q = apply_axial_rope(q, pos_map)
        k = apply_axial_rope(k, ctx_pos_map)
        scale = 1.0 / np.sqrt(HEAD_DIM).astype(np.float32)
        logits = jnp.einsum('bqhd,bkhd->bhqk', q, k) * scale
        w = jax.nn.softmax(logits, axis=-1)
        attn = jnp.einsum('bhqk,bkhd->bqhd', w, v)
        attn = attn.reshape(b, n, N_HEADS * HEAD_DIM)
        return attn @ Wout + bout

    def _L1_ffn_ref(inputs, gate_w, gate_b, w1, b1, w2, b2):
        import jax, jax.numpy as jnp
        import numpy as np
        B, S, D, F, E, K = (2, 256, 256, 1024, 8, 2)
        x = inputs.reshape(-1, inputs.shape[-1])
        n = x.shape[0]
        gate_probs = jax.nn.softmax(x @ gate_w + gate_b, axis=-1)
        weights, selected = jax.lax.top_k(gate_probs, K)
        weights = weights / jnp.sum(weights, axis=-1, keepdims=True)
        comb = jnp.zeros((n, E), x.dtype).at[jnp.arange(n)[:, None], selected].set(weights)
        h = jax.nn.gelu(jnp.einsum('nd,edf->enf', x, w1) + b1[:, None, :])
        expert_out = jnp.einsum('enf,efd->end', h, w2) + b2[:, None, :]
        out = jnp.einsum('ne,end->nd', comb, expert_out)
        return out.reshape(inputs.shape[:-1] + (out.shape[-1],))
    x = x + jnp.tanh(g_xattn[0]) * _L0_xattn_ref(ctx_1024, _layernorm(x, axis=-1), L0_xattn_in_proj_w, L0_xattn_conv_w, L0_xattn_conv_b, L0_xattn_x_proj_w, L0_xattn_dt_proj_w, L0_xattn_dt_proj_b, L0_xattn_A_log, L0_xattn_D)
    x = x + jnp.tanh(g_ffn[0]) * _L0_ffn_ref(_layernorm(x, axis=-1), L0_ffn_Wg, L0_ffn_Wu, L0_ffn_Wd, L0_ffn_Wr, L0_ffn_temperature)
    x = x + jnp.tanh(g_xattn[1]) * _L1_xattn_ref(_layernorm(x, axis=-1), ctx_1024, fside_BxSx2_0, fside_BxSx2_0, L1_xattn_Wq, L1_xattn_Wkv, L1_xattn_Wout, L1_xattn_bout)
    x = x + jnp.tanh(g_ffn[1]) * _L1_ffn_ref(_layernorm(x, axis=-1), L1_ffn_gate_w, L1_ffn_gate_b, L1_ffn_w1, L1_ffn_b1, L1_ffn_w2, L1_ffn_b2)
    return x

_drawn_inputs = setup_inputs


def setup_inputs(seed=0):
    import zlib

    import numpy as np

    out = dict(_drawn_inputs(seed))
    spreads = {'g_ffn': (-1.0, 0.591),
     'L0_xattn_conv_b': (0.0, 0.1),
     'L0_xattn_D': (1.0, 0.2),
     'L1_xattn_bout': (0.0, 0.1),
     'L1_ffn_gate_b': (0.0, 0.1),
     'L1_ffn_b1': (0.0, 0.1),
     'L1_ffn_b2': (0.0, 0.1)}
    factors = {'L0_xattn_dt_proj_w': 2.763}
    for name, (base, spread) in spreads.items():
        noise = np.random.default_rng([zlib.crc32(name.encode()), seed]).standard_normal(out[name].shape)
        drawn = base * np.exp(spread * noise) if base else spread * noise
        out[name] = jnp.asarray(drawn.astype(out[name].dtype))
    for name, factor in factors.items():
        out[name] = (out[name] * factor).astype(out[name].dtype)
    return out
```

```python
from contextlib import ExitStack

import numpy as np

import concourse.bass as bass
from concourse import mybir

ALU = mybir.AluOpType
ACT = mybir.ActivationFunctionType
F32 = mybir.dt.float32
BF16 = mybir.dt.bfloat16
AX = mybir.AxisListType

P = 128
BATCH, SEQ, DM = 4, 256, 256
NT = BATCH * SEQ // P
TOK = BATCH * SEQ
CTX = 128
DI, DS, DC, DR = 256, 16, 4, 8
EXPERTS = 8
F0, F1 = 256, 1024
HEADS, HD = 32, 8
EPS = 1e-5
GOLDEN = 1.0 / np.e
LOWER, UPPER = 0.5 - np.log(4.0 / 3.0), 0.5
FAR = 1e36
TWO_PI = 2.0 * np.pi
ARENA = 42500
ROUND = 1.5 * 2.0 ** 23


def constants():
    ident = np.eye(P, dtype=np.float32)
    rows = np.zeros((96, 32, P), np.float32)
    for r in range(96):
        rows[r, r % 32, :] = 1.0
    before = np.zeros((P, EXPERTS, EXPERTS), np.float32)
    for e in range(EXPERTS):
        before[:, e, :e] = 1.0
    freq = np.zeros((2, P), np.float32)
    for p in range(P):
        freq[(p // 4) % 2, p] = np.float32(10000.0) ** np.float32(-((p // 2) % 2) / 2)
    return {"ident": ident, "rows": rows, "before": before, "freq": freq}


def program(nc, a, out, upto=99):
    ctx = ExitStack()
    with ctx:
        def sb(name, shape, dt=F32):
            return ctx.enter_context(nc.sbuf_tensor(name, shape, dt))

        def sem(name):
            return ctx.enter_context(nc.semaphore(name))

        ps = ctx.enter_context(nc.psum_tensor("ps", [P, 8, 512], F32))

        X = sb("X", [P, NT, DM])
        xn = sb("xn", [P, NT, DM])
        xnT = sb("xnT", [P, 2, TOK])
        ctxT = sb("ctxT", [P, TOK])
        ident = sb("ident", [P, P])
        before = sb("before", [P, EXPERTS, EXPERTS])
        freq = sb("freq", [2, P])
        stats = sb("stats", [P, NT, 6])
        meanvar = sb("meanvar", [P, NT, 2])
        vareps = sb("vareps", [P, NT])
        minushalf = sb("minushalf", [P, NT])
        rstd = sb("rstd", [P, NT])
        gates = sb("gates", [P, 4])
        tg = sb("tg", [P, 4])
        temp = sb("temp", [P, 1])
        halfrt = sb("halfrt", [P, 1])
        posT = sb("posT", [2, TOK])
        ones_row = sb("ones_row", [1, P])

        arena = sb("arena", [P, ARENA])

        class Region:
            def __init__(self):
                self.used = 0

            def __call__(self, name, shape, dt=F32):
                count = 1
                for d in shape[1:]:
                    count *= d
                words = count if dt == F32 else (count + 1) // 2
                view = arena[0:shape[0], self.used:self.used + words]
                self.used += words
                assert self.used <= ARENA, (name, self.used)
                if dt != F32:
                    view = view.bitcast(dt)
                if len(shape) > 2:
                    axes = "abcd"[:len(shape) - 1]
                    view = view.rearrange(f"p ({' '.join(axes)}) -> p {' '.join(axes)}",
                                          **dict(zip(axes, shape[1:])))
                return view

        ld_const, ld_x, ld_ctx, ld_ssm, ld_gate, ld_att, ld_pos = (
            sem("ld_const"), sem("ld_x"), sem("ld_ctx"), sem("ld_ssm"), sem("ld_gate"), sem("ld_att"), sem("ld_pos"))
        set_up = sem("set_up")
        stored = sem("stored")
        dve_order = sem("dve_order")
        act_order = sem("act_order")

        class LN:
            def __init__(self, n):
                self.stat, self.agg, self.var, self.rs, self.xn, self.tr, self.t = (
                    sem(f"ln{n}_stat"), sem(f"ln{n}_agg"), sem(f"ln{n}_var"), sem(f"ln{n}_rstd"), sem(f"ln{n}_xn"),
                    sem(f"ln{n}_transposed"), sem(f"ln{n}_xnT"))
        ln = [LN(n) for n in range(4)]

        def ln_dve(dve, s):
            for t in range(NT):
                nc.vector.bn_stats(stats[:, t, :], X[:, t, :]).then_inc(s.stat, 1)
            for t in range(NT):
                dve.wait_ge(s.stat, t + 1)
                nc.vector.bn_aggr(meanvar[:, t, :], stats[:, t, :]).then_inc(s.agg, 1)
            dve.wait_ge(s.agg, NT)
            nc.vector.tensor_scalar(vareps[:, :], meanvar[:, :, 1], EPS, None, ALU.add).then_inc(s.var, 1)
            dve.wait_ge(s.rs, 1)
            for t in range(NT):
                nc.vector.tensor_scalar(xn[:, t, :], X[:, t, :], meanvar[:, t, 0:1], rstd[:, t:t + 1],
                                        ALU.subtract, ALU.mult).then_inc(s.xn, 1)

        def ln_pool(pool, s):
            pool.wait_ge(s.var, 1)
            nc.gpsimd.tensor_tensor(rstd[:, :], vareps[:, :], minushalf[:, :], ALU.pow).then_inc(s.rs, 1)

        def ln_pe(pe, s):
            for th in range(2):
                pe.wait_ge(s.xn, 4 * th + 4)
                for c in range(2):
                    for q in range(4):
                        mm = nc.tensor.transpose(ps[:, 2 * th + c, q * P:(q + 1) * P],
                                                 xn[:, 4 * th + q, c * P:(c + 1) * P], ident[:, :])
                    mm.then_inc(s.tr, 1)

        def ln_act(act, s):
            for th in range(2):
                for c in range(2):
                    act.wait_ge(s.tr, 2 * th + c + 1)
                    nc.scalar.copy(xnT[:, c, th * 512:(th + 1) * 512], ps[:, 2 * th + c, :]).then_inc(s.t, 1)

        sbs = Region()

        ctx_in = sbs("ctx_in", [P, NT, CTX])
        in_w = sbs("in_w", [P, 2, CTX])
        x_w = sbs("x_w", [DR + 2 * DS, DI])
        dt_w = sbs("dt_w", [P, 2, DR])
        cols = sbs("cols", [P, 2, DC + 3])
        a_log = sbs("a_log", [P, 2, DS])
        neg_a = sbs("neg_a", [P, 2, DS])
        rows = sbs("rows", [96, 32, P])
        rows_bf = sbs("rows_bf", [96, 32, P], BF16)
        in_wT = sbs("in_wT", [P, DI])
        x_wT = sbs("x_wT", [P, 2, DR])
        bc_wT = sbs("bc_wT", [P, 2, 96])
        dt_wT = sbs("dt_wT", [DR, DI])
        diag = sbs("diag", [P, 2, P])
        xpad = sbs("xpad", [P, 2, BATCH, SEQ + DC - 1])
        conv = sbs("conv", [P, 2, TOK])
        u = sbs("u", [P, 2, TOK])
        dt_lo = sbs("dt_lo", [DR, TOK])
        t_abs = sbs("t_abs", [P, 2, TOK])
        t_exp = sbs("t_exp", [P, 2, TOK])
        delta = sbs("delta", [P, 2, TOK])
        du = sbs("du", [P, 2, TOK])
        bc = sbs("bc", [96, 3, TOK])
        bc3 = sbs("bc3", [96, TOK], BF16)
        dA = sbs("dA", [P, 2, 2, TOK])
        dBu = sbs("dBu", [P, 2, TOK])
        h = sbs("h", [P, 2, TOK])
        hC = sbs("hC", [P, 2, TOK])
        sz = t_abs[:, :, :].rearrange("p e (b l) -> p e b l", b=BATCH)
        gy = t_exp

        names = ["wT", "wTc", "ctxT_ps", "ctxT", "xin_ps", "xpad", "conv", "u", "xdbl_ps", "dt_lo", "bc_cp", "bc_r",
                 "bc3", "dt_ps", "v", "abs", "exp", "plus", "log", "delta", "du", "far", "na", "B", "C", "dA", "dBu", "scan",
                 "hC", "Y", "seed", "sz", "gy", "yT", "X1", "zero"]
        S = {n: sem("ssm_" + n) for n in names}

        def ssm_dve(dve):
            nc.vector.memset(xpad[:, :, :, 0:DC - 1], 0.0).then_inc(S["zero"], 1)
            dve.wait_ge(S["wT"], 1)
            nc.vector.tensor_copy(in_wT[:, :], ps[:, 4, 0:256]).then_inc(S["wTc"], 1)
            for k in range(2):
                src = ps[:, 5, k * 64:k * 64 + 40]
                nc.vector.tensor_copy(x_wT[:, k, :], src[:, 0:DR]).then_inc(S["wTc"], 1)
                nc.vector.tensor_copy(bc_wT[:, k, :].rearrange("p (r n) -> p r n", r=3),
                                      src[:, DR:40].unsqueeze(1).to_broadcast([P, 3, 32])).then_inc(S["wTc"], 1)
            nc.vector.tensor_copy(dt_wT[:, :], ps[0:DR, 6, 0:256]).then_inc(S["wTc"], 1)
            dve.wait_ge(ld_const, 16 * 5)
            nc.vector.tensor_copy(rows_bf[:, :, :], rows[:, :, :]).then_inc(S["wTc"], 1)
            for e in range(2):
                nc.vector.tensor_scalar(diag[:, e, :], ident[:, :], cols[:, e, DC + 2:DC + 3], None,
                                        ALU.mult).then_inc(S["wTc"], 1)
            for e in range(2):
                dve.wait_ge(S["xpad"], 2 * e + 2)
                o = conv[:, e, :].rearrange("p (b l) -> p b l", b=BATCH)
                for k in range(DC):
                    if k:
                        dve.wait_ge(S["conv"], DC * e + k)
                        nc.vector.scalar_tensor_tensor(o, xpad[:, e, :, k:k + SEQ], cols[:, e, k:k + 1], o,
                                                       ALU.mult, ALU.add).then_inc(S["conv"], 1)
                    else:
                        nc.vector.tensor_scalar(o, xpad[:, e, :, 0:SEQ], cols[:, e, 0:1], None,
                                                ALU.mult).then_inc(S["conv"], 1)
            dve.wait_ge(S["bc_cp"], 2)
            nc.vector.tensor_copy(bc3[0:32, :], bc[0:32, 0, :]).then_inc(S["bc3"], 1)
            hi = t_abs[0:96, 0, :].bitcast(BF16)[:, 0:TOK]
            lo = t_abs[0:96, 1, :].bitcast(BF16)[:, 0:TOK]
            nc.vector.tensor_copy(hi, bc[:, 0, :]).then_inc(S["bc_r"], 1)
            dve.wait_ge(S["bc_r"], 1)
            nc.vector.tensor_tensor(bc[:, 1, :], bc[:, 0, :], hi, ALU.subtract).then_inc(S["bc_r"], 1)
            dve.wait_ge(S["bc_r"], 2)
            nc.vector.tensor_copy(bc3[32:64, :], bc[32:64, 1, :]).then_inc(S["bc3"], 1)
            nc.vector.tensor_copy(lo, bc[:, 1, :]).then_inc(S["bc_r"], 1)
            dve.wait_ge(S["bc_r"], 3)
            nc.vector.tensor_tensor(bc[:, 2, :], bc[:, 1, :], lo, ALU.subtract).then_inc(S["bc_r"], 1)
            dve.wait_ge(S["bc_r"], 4)
            nc.vector.tensor_copy(bc3[64:96, :], bc[64:96, 2, :]).then_inc(S["bc3"], 1)
            for e in range(2):
                dve.wait_ge(S["v"], e + 1)
                nc.vector.tensor_scalar(delta[:, e, :], conv[:, e, :], 0.0, None, ALU.max).then_inc(S["plus"], 1)
                dve.wait_ge(S["exp"], e + 1)
                nc.vector.tensor_scalar(dBu[:, e, :], t_exp[:, e, :], 1.0, None, ALU.add).then_inc(S["plus"], 1)
                dve.wait_ge(S["plus"], 4 * e + 2)
                nc.vector.scalar_tensor_tensor(h[:, e, :], dBu[:, e, :], -1.0, t_exp[:, e, :],
                                               ALU.add, ALU.subtract).then_inc(S["plus"], 1)
                dve.wait_ge(S["plus"], 4 * e + 3)
                nc.vector.tensor_tensor(delta[:, e, :], delta[:, e, :], h[:, e, :], ALU.subtract).then_inc(S["plus"], 1)
                dve.wait_ge(S["plus"], 4 * e + 4)
                dve.wait_ge(S["log"], e + 1)
                nc.vector.tensor_tensor(delta[:, e, :], delta[:, e, :], hC[:, e, :], ALU.add).then_inc(S["delta"], 1)
                dve.wait_ge(S["delta"], e + 1)
                dve.wait_ge(S["u"], e + 1)
                nc.vector.tensor_tensor(du[:, e, :], delta[:, e, :], u[:, e, :], ALU.mult).then_inc(S["du"], 1)
                dve.wait_ge(S["du"], e + 1)
                nc.vector.memset(delta[:, e, :].rearrange("p (b l) -> p b l", b=BATCH)[:, :, 0:1],
                                 FAR).then_inc(S["far"], 1)
            dve.wait_ge(S["far"], 2)

            def step(n, s):
                psB = ps[:, 0:2, :].rearrange("p k n -> p (k n)")
                psC = ps[:, 2:4, :].rearrange("p k n -> p (k n)")
                dve.wait_ge(S["B"], n + 1)
                for e in range(2):
                    nc.vector.tensor_tensor(dBu[:, e, :], du[:, e, :], psB, ALU.mult).then_inc(S["dBu"], 1)
                for e in range(2):
                    dve.wait_ge(S["dBu"], 2 * n + e + 1)
                    dve.wait_ge(S["dA"], 2 * n + e + 1)
                    nc.vector.tensor_tensor_scan(h[:, e, :], dA[:, s, e, :], dBu[:, e, :], 0.0,
                                                 ALU.mult, ALU.add).then_inc(S["scan"], 1)
                dve.wait_ge(S["C"], n + 1)
                for e in range(2):
                    dve.wait_ge(S["scan"], 4 + 2 * n + e + 1)
                    dve.wait_ge(S["Y"], 2 * n + e + 1)
                    nc.vector.tensor_tensor(hC[:, e, :], h[:, e, :], psC, ALU.mult).then_inc(S["hC"], 1)

            dve.sem_inc(S["scan"], 4)
            with dve.Fori(0, DS // 2) as i:
                for s in range(2):
                    step(2 * i + s, s)
            for e in range(2):
                dve.wait_ge(S["Y"], 2 + 2 * DS)
                dve.wait_ge(S["sz"], e + 1)
                nc.vector.tensor_tensor(gy[:, e, :], ps[:, 4 + 2 * e:6 + 2 * e, :].rearrange("p k n -> p (k n)"),
                                        sz[:, e, :, :].rearrange("p b l -> p (b l)"), ALU.mult).then_inc(S["gy"], 1)
            for t in range(NT):
                dve.wait_ge(S["yT"], t // 2 + 1)
                nc.vector.scalar_tensor_tensor(X[:, t, :], ps[:, t // 2, (t % 2) * 256:(t % 2) * 256 + 256],
                                               tg[:, 0:1], X[:, t, :], ALU.mult, ALU.add).then_inc(S["X1"], 1)
            dve.wait_ge(S["X1"], NT)

        def ssm_pe(pe):
            pe.wait_ge(ld_const, 16 * 5)
            pe.wait_ge(ld_ssm, 16 * SSM_LOADS)
            for e in range(2):
                nc.tensor.transpose(ps[:, 4, e * P:(e + 1) * P], in_w[:, e, :], ident[:, :])
                nc.tensor.transpose(ps[:, 5, e * 64:e * 64 + 40], x_w[:, e * P:(e + 1) * P], ident[0:40, 0:40])
                mm = nc.tensor.transpose(ps[0:DR, 6, e * P:(e + 1) * P], dt_w[:, e, :], ident[:, :])
            mm.then_inc(S["wT"], 1)
            pe.wait_ge(ld_ctx, 16)
            for th in range(2):
                for q in range(4):
                    mm = nc.tensor.transpose(ps[:, 2 + th, q * P:(q + 1) * P], ctx_in[:, 4 * th + q, :], ident[:, :])
                mm.then_inc(S["ctxT_ps"], 1)
            pe.wait_ge(S["wTc"], 9)
            for e in range(2):
                for th in range(2):
                    if not e:
                        pe.wait_ge(S["ctxT"], th + 1)
                    nc.tensor.matmul(ps[:, 4 + 2 * e + th, :], in_wT[:, e * P:(e + 1) * P],
                                     ctxT[:, th * 512:(th + 1) * 512], start=True, stop=True).then_inc(S["xin_ps"], 1)
            pe.wait_ge(S["u"], 2)
            for th in range(2):
                for k in range(2):
                    nc.tensor.matmul(ps[0:96, th, :], bc_wT[:, k, :], u[:, k, th * 512:(th + 1) * 512],
                                     start=(k == 0), stop=(k == 1))
                for k in range(2):
                    mm = nc.tensor.matmul(ps[0:DR, 2 + th, :], x_wT[:, k, :], u[:, k, th * 512:(th + 1) * 512],
                                          start=(k == 0), stop=(k == 1))
                mm.then_inc(S["xdbl_ps"], 1)
            pe.wait_ge(S["dt_lo"], 2)
            for e in range(2):
                for th in range(2):
                    mm = nc.tensor.matmul(ps[:, 4 + 2 * e + th, :], dt_wT[:, e * P:(e + 1) * P],
                                          dt_lo[:, th * 512:(th + 1) * 512], start=True, stop=True)
                mm.then_inc(S["dt_ps"], 1)

            def spread(bank, row, done):
                for th in range(2):
                    mm = nc.tensor.matmul(ps[:, bank + th, :], rows_bf[:, row, :], bc3[:, th * 512:(th + 1) * 512],
                                          start=True, stop=True)
                mm.then_inc(done, 1)

            def add_y(e):
                for th in range(2):
                    mm = nc.tensor.matmul(ps[:, 4 + 2 * e + th, :], ident[:, :], hC[:, e, th * 512:(th + 1) * 512],
                                          start=False, stop=False, skip_group_check=True)
                mm.then_inc(S["Y"], 1)

            pe.wait_ge(S["bc3"], 3)
            spread(0, 0, S["B"])
            spread(2, DS, S["C"])
            pe.wait_ge(S["far"], 2)
            for e in range(2):
                for th in range(2):
                    mm = nc.tensor.matmul(ps[:, 4 + 2 * e + th, :], diag[:, e, :], u[:, e, th * 512:(th + 1) * 512],
                                          start=True, stop=False, skip_group_check=True)
                mm.then_inc(S["Y"], 1)

            def step(n, more=True):
                if more:
                    pe.wait_ge(S["dBu"], 2 * n + 2)
                    spread(0, n + 1, S["B"])
                pe.wait_ge(S["hC"], 2 * n + 1)
                add_y(0)
                pe.wait_ge(S["hC"], 2 * n + 2)
                if more:
                    spread(2, DS + n + 1, S["C"])
                add_y(1)

            with pe.Fori(0, DS - 1) as n:
                step(n)
            step(DS - 1, more=False)
            for b in range(BATCH):
                for lh in range(2):
                    for e in range(2):
                        if b == 0 and lh == 0:
                            pe.wait_ge(S["gy"], e + 1)
                        at = b * SEQ + lh * P
                        mm = nc.tensor.transpose(ps[:, b, lh * 256 + e * P:lh * 256 + (e + 1) * P],
                                                 gy[:, e, at:at + P], ident[:, :])
                mm.then_inc(S["yT"], 1)

        def ssm_act(act):
            act.wait_ge(ld_gate, 32 + 16)
            nc.scalar.activation(tg[:, :], gates[:, :], ACT.Tanh).then_inc(set_up, 1)
            act.wait_ge(ld_ssm, 16 * SSM_LOADS)
            nc.scalar.activation(a_log[:, :, :], a_log[:, :, :], ACT.Exp).then_inc(act_order, 1)
            act.wait_ge(act_order, 1)
            nc.scalar.mul(neg_a[:, :, :], a_log[:, :, :], -1.0).then_inc(S["na"], 1)
            for th in range(2):
                act.wait_ge(S["ctxT_ps"], th + 1)
                nc.scalar.copy(ctxT[:, th * 512:(th + 1) * 512], ps[:, 2 + th, :]).then_inc(S["ctxT"], 1)
            act.wait_ge(S["zero"], 1)
            for e in range(2):
                for th in range(2):
                    act.wait_ge(S["xin_ps"], 2 * e + th + 1)
                    nc.scalar.copy(xpad[:, e, 2 * th:2 * th + 2, DC - 1:],
                                   ps[:, 4 + 2 * e + th, :].rearrange("p (b l) -> p b l", b=2)).then_inc(S["xpad"], 1)
            for e in range(2):
                act.wait_ge(S["conv"], DC * e + DC)
                nc.scalar.activation(u[:, e, :], conv[:, e, :], ACT.Silu, bias=cols[:, e, DC:DC + 1]).then_inc(S["u"], 1)
            for th in range(2):
                act.wait_ge(S["xdbl_ps"], th + 1)
                nc.scalar.copy(dt_lo[:, th * 512:(th + 1) * 512], ps[0:DR, 2 + th, :]).then_inc(S["dt_lo"], 1)
                nc.scalar.copy(bc[:, 0, th * 512:(th + 1) * 512], ps[0:96, th, :]).then_inc(S["bc_cp"], 1)
            act.wait_ge(S["bc_r"], 4)
            for e in range(2):
                act.wait_ge(S["dt_ps"], e + 1)
                nc.scalar.activation(conv[:, e, :], ps[:, 4 + 2 * e:6 + 2 * e, :].rearrange("p k n -> p (k n)"),
                                     ACT.Identity, bias=cols[:, e, DC + 1:DC + 2]).then_inc(S["v"], 1)
                act.wait_ge(S["v"], e + 1)
                nc.scalar.activation(t_abs[:, e, :], conv[:, e, :], ACT.Abs).then_inc(S["abs"], 1)
                act.wait_ge(S["abs"], e + 1)
                nc.scalar.activation(t_exp[:, e, :], t_abs[:, e, :], ACT.Exp, scale=-1.0).then_inc(S["exp"], 1)
            for e in range(2):
                act.wait_ge(S["plus"], 4 * e + 2)
                nc.scalar.activation(hC[:, e, :], dBu[:, e, :], ACT.Ln).then_inc(S["log"], 1)
            act.wait_ge(S["far"], 2)
            with act.Fori(0, DS // 2) as i:
                for s in range(2):
                    for e in range(2):
                        act.wait_ge(S["scan"], 4 * i + 2 * s + e + 1)
                        nc.scalar.activation(dA[:, s, e, :], delta[:, e, :], ACT.Exp,
                                             scale=neg_a[:, e, bass.ds(2 * i + s, 1)]).then_inc(S["dA"], 1)
            act.wait_ge(ln[0].xn, NT)
            for e in range(2):
                nc.scalar.activation(sz[:, e, :, :], xn[:, e:NT:2, :], ACT.Silu).then_inc(S["sz"], 1)

        SSM_LOADS = 8

        pair_gt = sb("pair_gt", [P, NT, EXPERTS * EXPERTS])
        pair_eq = sb("pair_eq", [P, NT, EXPERTS * EXPERTS])
        before_all = sb("before_all", [P, NT, EXPERTS * EXPERTS])
        rank = sb("rank", [P, NT, EXPERTS])
        per_tile = sb("per_tile", [P, 4, NT])
        comb = sb("comb", [P, NT, EXPERTS])
        step_count = [0]

        def link(ins):
            step_count[0] += 1
            ins.then_inc(dve_order, 1)
            return step_count[0]

        def then(dve, ins):
            dve.wait_ge(dve_order, link(ins))

        def top2(dve, score, mask):
            v = nc.vector
            for t in range(NT):
                gt = pair_gt[:, t, :].rearrange("p (e j) -> p e j", e=EXPERTS)
                eq = pair_eq[:, t, :].rearrange("p (e j) -> p e j", e=EXPERTS)
                other = score[:, t, :].unsqueeze(1).to_broadcast([P, EXPERTS, EXPERTS])
                own = score[:, t, :].unsqueeze(2).to_broadcast([P, EXPERTS, EXPERTS])
                link(v.tensor_tensor(gt, other, own, ALU.is_gt))
                link(v.tensor_tensor(eq, other, own, ALU.is_equal))
            dve.wait_ge(dve_order, step_count[0])
            then(dve, v.tensor_tensor(pair_eq[:, :, :], pair_eq[:, :, :], before_all[:, :, :], ALU.mult))
            then(dve, v.tensor_tensor(pair_gt[:, :, :], pair_gt[:, :, :], pair_eq[:, :, :], ALU.add))
            then(dve, v.tensor_reduce(rank[:, :, :], pair_gt[:, :, :].rearrange("p t (e j) -> p t e j", e=EXPERTS),
                                      AX.X, ALU.add))
            then(dve, v.tensor_scalar(mask, rank[:, :, :], 2.0, None, ALU.is_lt))

        def by_tile(row):
            return per_tile[:, row, :].unsqueeze(2).to_broadcast([P, NT, EXPERTS])

        r0 = Region()
        golden = r0("golden", [P, 8, NT, EXPERTS])
        router0 = r0("router0", [P, 2, EXPERTS])
        gu_w = r0("gu_w", [P, 2, 2, 2, F0])
        d_w = r0("d_w", [P, 2, 2, DM])
        silu = r0("silu", [P, 2, 512])
        h0 = r0("h0", [P, 2, 2, 512])
        M = {n: sem("moe0_" + n) for n in ["router", "lg", "tanh", "dist", "exp", "comb", "w0", "w1", "gu", "silu", "h", "dn",
                                           "acc", "ready", "used"]}

        def gate0_pe(pe):
            pe.wait_ge(ln[1].t, 4)
            pe.wait_ge(M["router"], 16)
            for t in range(NT):
                for c in range(2):
                    mm = nc.tensor.matmul(ps[:, 7, t * EXPERTS:(t + 1) * EXPERTS], xnT[:, c, t * P:(t + 1) * P],
                                          router0[:, c, :], start=(c == 0), stop=(c == 1))
            mm.then_inc(M["lg"], 1)

        def gate0_act(act):
            th, dist, w, fb = (golden[:, k, :, :] for k in range(4))
            act.wait_ge(M["ready"], 1)
            act.wait_ge(M["lg"], 1)
            lg = ps[:, 7, 0:NT * EXPERTS].rearrange("p (t e) -> p t e", t=NT)
            nc.scalar.activation(th, lg, ACT.Tanh, scale=halfrt[:, :]).then_inc(M["tanh"], 1)
            act.wait_ge(M["dist"], 1)
            nc.scalar.activation(w, dist, ACT.Exp, scale=-10.0).then_inc(M["exp"], 1)
            nc.scalar.activation(fb, dist, ACT.Exp, scale=-1.0 / 0.3).then_inc(M["exp"], 1)

        def gate0_dve(dve):
            v = nc.vector
            th, dist, w, fb, inh, zone, tmp, msk = (golden[:, k, :, :] for k in range(8))
            dve.wait_ge(ld_gate, 48)
            then(dve, v.reciprocal(temp[:, :], temp[:, :]))
            v.tensor_scalar(halfrt[:, :], temp[:, :], 0.5, None, ALU.mult).then_inc(M["ready"], 1)
            for t in range(NT):
                link(v.tensor_copy(before_all[:, t, :], before[:, :, :].rearrange("p e j -> p (e j)")))
            dve.wait_ge(M["tanh"], 1)
            then(dve, v.tensor_scalar(inh, th, 0.5, 0.5, ALU.mult, ALU.add))
            then(dve, v.tensor_scalar(tmp, inh, float(GOLDEN), None, ALU.subtract))
            v.scalar_tensor_tensor(dist, tmp, -1.0, tmp, ALU.mult, ALU.max).then_inc(M["dist"], 1)
            then(dve, v.tensor_scalar(zone, inh, float(LOWER), None, ALU.is_ge))
            then(dve, v.scalar_tensor_tensor(zone, inh, float(UPPER), zone, ALU.is_le, ALU.mult))
            dve.wait_ge(M["exp"], 2)
            then(dve, v.tensor_tensor(w, w, zone, ALU.mult))
            then(dve, v.tensor_reduce(per_tile[:, 0, :], w, AX.X, ALU.add))
            then(dve, v.tensor_scalar(per_tile[:, 1, :], per_tile[:, 0, :], 1e-8, None, ALU.is_lt))
            top2(dve, fb, msk)
            then(dve, v.tensor_tensor(fb, fb, msk, ALU.mult))
            then(dve, v.tensor_reduce(per_tile[:, 2, :], fb, AX.X, ALU.add))
            then(dve, v.tensor_scalar(per_tile[:, 2, :], per_tile[:, 2, :], 1e-8, None, ALU.max))
            then(dve, v.reciprocal(per_tile[:, 3, :], per_tile[:, 2, :]))
            then(dve, v.tensor_tensor(fb, fb, by_tile(3), ALU.mult))
            then(dve, v.tensor_tensor(fb, fb, by_tile(1), ALU.mult))
            then(dve, v.tensor_scalar(per_tile[:, 1, :], per_tile[:, 1, :], -1.0, 1.0, ALU.mult, ALU.add))
            then(dve, v.tensor_tensor(w, w, by_tile(1), ALU.mult))
            then(dve, v.tensor_tensor(w, w, fb, ALU.add))
            then(dve, v.tensor_reduce(per_tile[:, 2, :], w, AX.X, ALU.add))
            then(dve, v.tensor_scalar(per_tile[:, 2, :], per_tile[:, 2, :], 1e-8, None, ALU.max))
            then(dve, v.reciprocal(per_tile[:, 3, :], per_tile[:, 2, :]))
            then(dve, v.tensor_scalar(per_tile[:, 3, :], per_tile[:, 3, :], tg[:, 2:3], None, ALU.mult))
            then(dve, v.tensor_tensor(comb[:, :, :], w, by_tile(3), ALU.mult))

        def moe0_sp(sp):
            def load(e, slot):
                one = bass.ds(e, 1)
                for k, n in enumerate(["L0_ffn_Wg", "L0_ffn_Wu"]):
                    sp.dma_start(gu_w[:, slot, k, :, :], a[n][one, :, :].rearrange("o (k p) f -> p (o k) f", p=P)
                                 ).then_inc(M[f"w{slot}"], 16)
                sp.dma_start(d_w[:, slot, :, :], a["L0_ffn_Wd"][one, :, :].rearrange("o (k p) f -> p (o k) f", p=P)
                             ).then_inc(M[f"w{slot}"], 16)
            sp.wait_ge(S["X1"], NT)
            sp.dma_start(router0[:, :, :], a["L0_ffn_Wr"].rearrange("(k p) e -> p k e", p=P)).then_inc(M["router"], 16)
            for e in range(2):
                load(e, e)
            with sp.Fori(0, EXPERTS // 2 - 1) as i:
                for slot in range(2):
                    sp.wait_ge(M["dn"], 4 * i + 2 * slot + 4)
                    load(2 * i + slot + 2, slot)

        def moe0_pe(pe):
            def up(k, q, w_wait=None):
                slot, th = q // 2, q % 2
                if th == 0:
                    pe.wait_ge(M[f"w{slot}"], w_wait)
                for f in range(2):
                    pe.wait_ge(M["h"], 2 * k + f + 1)
                    for g in range(2):
                        for c in range(2):
                            mm = nc.tensor.matmul(ps[:, 2 * f + g, :], gu_w[:, slot, g, c, f * P:(f + 1) * P],
                                                  xnT[:, c, th * 512:(th + 1) * 512], start=(c == 0), stop=(c == 1))
                    mm.then_inc(M["gu"], 1)

            def down(k, q):
                slot, th = q // 2, q % 2
                pe.wait_ge(M["h"], 2 * k + 4)
                pe.wait_ge(M["acc"], 4 * k + 4)
                for t in range(4):
                    for f in range(2):
                        mm = nc.tensor.matmul(ps[:, 4 + 2 * th + t // 2, (t % 2) * 256:(t % 2) * 256 + 256],
                                              h0[:, th, f, t * P:(t + 1) * P], d_w[:, slot, f, :],
                                              start=(f == 0), stop=(f == 1))
                mm.then_inc(M["dn"], 1)

            def turn(i, last):
                for q in range(4):
                    if not (last and q == 3):
                        up(4 * i + q + 1, (q + 1) % 4, 48 * i + 48 * ((q + 1) // 4) + 48)
                    down(4 * i + q, q)

            pe.wait_ge(M["comb"], 1)
            pe.sem_inc(M["dn"], 2)
            up(0, 0, 48)
            with pe.Fori(0, EXPERTS // 2 - 1) as i:
                turn(i, False)
            turn(EXPERTS // 2 - 1, True)

        def moe0_act(act):
            with act.Fori(0, 2 * EXPERTS) as k:
                for f in range(2):
                    act.wait_ge(M["gu"], 2 * k + f + 1)
                    act.wait_ge(M["h"], 2 * k + f + 1)
                    nc.scalar.activation(silu[:, f, :], ps[:, 2 * f, :], ACT.Silu).then_inc(M["silu"], 1)

        def moe0_dve(dve):
            def hidden(k, q):
                for f in range(2):
                    dve.wait_ge(M["silu"], 2 * k + f + 1)
                    dve.wait_ge(M["dn"], k + 1)
                    nc.vector.tensor_tensor(h0[:, q % 2, f, :], silu[:, f, :], ps[:, 2 * f + 1, :],
                                            ALU.mult).then_inc(M["h"], 1)

            def add(i, q):
                th = q % 2
                dve.wait_ge(M["dn"], 4 * i + q + 3)
                dve.wait_ge(M["acc"], 8 + 16 * i + 4 * q - 4)
                for t in range(4):
                    tile = 4 * th + t
                    nc.vector.scalar_tensor_tensor(X[:, tile, :], ps[:, 4 + 2 * th + t // 2, (t % 2) * 256:(t % 2) * 256 + 256],
                                                   comb[:, tile, bass.ds(2 * i + q // 2, 1)], X[:, tile, :],
                                                   ALU.mult, ALU.add).then_inc(M["acc"], 1)

            def turn(i, last):
                for q in range(4):
                    if not (last and q == 3):
                        hidden(4 * i + q + 1, q + 1)
                    add(i, q)

            dve.sem_inc(M["h"], 2)
            dve.sem_inc(M["acc"], 8)
            nc.vector.memset(minushalf[:, :], -0.5).then_inc(M["comb"], 1)
            hidden(0, 0)
            with dve.Fori(0, EXPERTS // 2 - 1) as i:
                turn(i, False)
            turn(EXPERTS // 2 - 1, True)
            dve.wait_ge(M["acc"], 8 + 8 * EXPERTS)



        r1 = Region()
        wq = r1("wq", [P, 2, DM])
        wkv = r1("wkv", [P, 2 * DM])
        wout = r1("wout", [P, 2, DM])
        bout = r1("bout", [1, DM])
        wq_sw = r1("wq_sw", [P, 2, DM])
        wk_sw = r1("wk_sw", [P, DM])
        cos = r1("cos", [P, TOK])
        sin = r1("sin", [P, TOK])
        qa = r1("qa", [P, 3, HEADS, SEQ], BF16)
        ka = r1("ka", [P, 3, HEADS, SEQ], BF16)
        vv = r1("vv", [P, NT, DM])
        v_pad = r1("v_pad", [P, 2, 2, 4, 32])
        mx = r1("mx", [P, 2, 2, HEADS])
        m_parts = r1("m_parts", [32, 3, SEQ], BF16)
        m_rest = r1("m_rest", [32, 2, SEQ])
        probs = r1("probs", [P, 4, 2, 2, SEQ])
        o_rows = r1("o_rows", [P, 8, SEQ])
        recip16 = r1("recip16", [P, 16, 1])
        rope_a = probs[:, 0, :, :, :].rearrange("p a b c -> p (a b c)")
        rope_b = probs[:, 1, :, :, :].rearrange("p a b c -> p (a b c)")
        parts = [r1("parts0", [P, 3, TOK], BF16), r1("parts1", [P, 3, TOK], BF16)]
        attn, attnT = xn, xnT
        parts_d = nc.dram_tensor("parts_d", [2, 3, DM, TOK], BF16, kind="Internal").ap()
        max_d = nc.dram_tensor("max_d", [BATCH, 3, HEADS, SEQ], BF16, kind="Internal").ap()
        GROUPS = HEADS // 4
        T = {n: sem("att_" + n) for n in ["ang", "red", "sin", "cos", "w", "sw", "proj", "rope", "split", "part", "sent0",
                                          "sent1", "v_ps", "v", "rows", "zero", "qk0", "qk1", "qk2", "A", "max", "mT", "mrow",
                                          "msent", "mput", "B", "exp", "vpad", "pv", "o", "oT", "attn", "aT_ps", "aT",
                                          "out", "X3", "setv"]}

        def att_sp_weights(sp):
            sp.wait_ge(M["acc"], 8 + 8 * EXPERTS)
            sp.dma_start(wq[:, :, :], a["L1_xattn_Wq"].rearrange("(k p) n -> p k n", p=P)).then_inc(T["w"], 16)
            sp.dma_start(wkv[:, :], a["L1_xattn_Wkv"]).then_inc(T["w"], 16)
            sp.dma_start(wout[:, :, :], a["L1_xattn_Wout"].rearrange("(k p) n -> p k n", p=P)).then_inc(T["w"], 16)
            sp.dma_start(bout[:, :], a["L1_xattn_bout"].unsqueeze(0)).then_inc(T["w"], 16)

        def att_sp(sp):
            att_sp_weights(sp)
            for un in range(4):
                sp.wait_ge(T["part"], 3 * un + 3)
                dst = parts_d[1 - un // 2, :, (un % 2) * P:(un % 2 + 1) * P, :].rearrange("i p t -> p i t")
                sp.dma_start(dst, parts[un % 2]).then_inc(T[f"sent{un % 2}"], 16)
            sp.wait_ge(T["sent0"], 32)
            sp.wait_ge(T["sent1"], 32)
            sp.wait_ge(T["zero"], 3)

            def load(b):
                for k, rows_of in enumerate([qa, ka]):
                    for i in range(3):
                        for j in range(3):
                            r = (3 * i + j) * HD
                            src = parts_d[k, j if k else i, :, b * SEQ:(b + 1) * SEQ].rearrange("(h d) t -> d h t", d=HD)
                            sp.dma_start(rows_of[r:r + HD, b % 3, :, :], src).then_inc(T[f"qk{b % 3}"], 16)

            def put_max(b):
                sp.wait_ge(T["mrow"], b + 1)
                sp.dma_start(max_d[b].rearrange("i h t -> h i t"), m_parts).then_inc(T["msent"], 16)
                sp.wait_ge(T["msent"], 16 * (b + 1))
                sp.dma_start(qa[96:99, b % 3, :, :], max_d[b]).then_inc(T["mput"], 16)

            load(0)
            load(1)
            put_max(0)
            for b in range(1, BATCH):
                if b + 1 < BATCH:
                    if b >= 2:
                        sp.wait_ge(T["B"], 2 * GROUPS * (b - 1))
                    load(b + 1)
                put_max(b)

        def att_pe(pe):
            pe.wait_ge(ld_pos, 16)
            pe.wait_ge(ln[2].t, 4)
            for th in range(2):
                mm = nc.tensor.matmul(ps[:, th, :], freq[:, :], posT[:, th * 512:(th + 1) * 512], start=True, stop=True)
            mm.then_inc(T["ang"], 1)
            pe.wait_ge(T["sw"], 2)
            for un in range(4):
                base = 4 * (1 - un % 2)
                c = un % 2
                if un == 1:
                    pe.wait_ge(T["red"], 1)
                if un == 2:
                    pe.wait_ge(ln[2].t, 4)
                if un >= 2:
                    pe.wait_ge(T["rope"], 2 * un - 2)
                for k, w in enumerate([wkv[:, c * P:(c + 1) * P], wk_sw[:, c * P:(c + 1) * P]] if un < 2 else
                                      [wq[:, :, c * P:(c + 1) * P], wq_sw[:, :, c * P:(c + 1) * P]]):
                    for th in range(2):
                        o = ps[:, base + 2 * k + th, :]
                        cut = slice(th * 512, (th + 1) * 512)
                        if un < 2:
                            mm = nc.tensor.matmul(o, w, ctxT[:, cut], start=True, stop=True)
                        else:
                            for kk in range(2):
                                mm = nc.tensor.matmul(o, w[:, kk, :], xnT[:, kk, cut], start=(kk == 0), stop=(kk == 1))
                    mm.then_inc(T["proj"], 1)
            pe.wait_ge(T["rope"], 6)
            for t in range(NT):
                mm = nc.tensor.matmul(ps[:, 4 + t // 2, (t % 2) * 256:(t % 2) * 256 + 256], ctxT[:, t * P:(t + 1) * P],
                                      wkv[:, DM:2 * DM], start=True, stop=True)
                if t % 2:
                    mm.then_inc(T["v_ps"], 1)
            pe.wait_ge(T["rope"], 8)
            pe.wait_ge(T["v"], 4)

            def A(b, hd, par, n):
                pe.wait_ge(T["max"], n + 1)
                for qt in range(2):
                    mm = nc.tensor.matmul(ps[:, par, qt * 256:(qt + 1) * 256],
                                          one(qa[0:72, b % 3, :, qt * P:(qt + 1) * P], hd),
                                          one(ka[0:72, b % 3, :, :], hd), start=True, stop=True)
                mm.then_inc(T["A"], 1)

            def B(b, hd, pair, n):
                pe.wait_ge(T["exp"], n + 1)
                for j in range(2):
                    for kc in range(2):
                        mm = nc.tensor.matmul(ps[:, 2 + 2 * pair + j, kc * 256:(kc + 1) * 256],
                                              one(ka[0:99, b % 3, :, kc * P:(kc + 1) * P], hd + j),
                                              one(qa[0:99, b % 3, :, :], hd + j), start=True, stop=True)
                mm.then_inc(T["B"], 1)

            def PV(s, G):
                pe.wait_ge(T["exp"], 2 * G + 2 + 2)
                pe.wait_ge(T["vpad"], G + 1)
                pe.wait_ge(T["o"], G + 1)
                for kc in range(2):
                    for j in range(4):
                        mm = nc.tensor.matmul(ps[32 * j:32 * j + 32, 6, 0:256], v_pad[:, s, kc, j, :],
                                              probs[:, 2 * s + j // 2, j % 2, kc, :], start=(kc == 0), stop=(kc == 1),
                                              skip_group_check=True)
                mm.then_inc(T["pv"], 1)

            def max_rows(b):
                pe.wait_ge(T["max"], HEADS * (b + 1) + 2)
                for qt in range(2):
                    mm = nc.tensor.transpose(ps[0:32, 7, qt * P:(qt + 1) * P], mx[:, b % 2, qt, :], ident[:, :])
                mm.then_inc(T["mT"], 1)

            def turn(b, i, last):
                for s in range(2):
                    G = 8 * b + 2 * i + s
                    g = 2 * i + s
                    for p in range(2):
                        if b + 1 < BATCH:
                            for j in range(2):
                                A(b + 1, 4 * g + 2 * p + j, j, HEADS * (b + 1) + 4 * g + 2 * p + j)
                        if not (last and s == 1):
                            B(b, 4 * g + 4 + 2 * p, p, 2 * G + 2 + p)
                    PV(s, G)

            pe.sem_inc(T["pv"], 2)
            pe.wait_ge(T["qk0"], 16 * 18)
            with pe.Fori(0, HEADS // 2) as i:
                for j in range(2):
                    A(0, 2 * i + j, j, 2 * i + j)
            max_rows(0)
            for b in range(BATCH):
                pe.wait_ge(T["mput"], 16 * (b + 1))
                for p in range(2):
                    B(b, 2 * p, p, 16 * b + p)
                if b + 1 < BATCH:
                    pe.wait_ge(T[f"qk{(b + 1) % 3}"], 16 * 18 * ((b + 1) // 3 + 1))
                with pe.Fori(0, GROUPS // 2 - 1) as i:
                    turn(b, i, False)
                turn(b, GROUPS // 2 - 1, True)
                if b + 1 < BATCH:
                    max_rows(b + 1)
                for gg in range(GROUPS // 2):
                    pe.wait_ge(T["o"], 8 * b + 2 * gg + 2 + 1)
                    n = 4 * b + gg
                    if gg == 0:
                        if b + 1 < BATCH:
                            pe.wait_ge(T["mrow"], b + 2)
                    if n:
                        pe.wait_ge(T["attn"], n)
                    for qt in range(2):
                        for k in range(2):
                            mm = nc.tensor.transpose(ps[:, 7, (2 * qt + k) * P:(2 * qt + k + 1) * P],
                                                     o_rows[:, 2 * gg + k, qt * P:(qt + 1) * P], ident[:, :])
                    mm.then_inc(T["oT"], 1)
            for th in range(2):
                for c in range(2):
                    pe.wait_ge(T["attn"], 16)
                    for q in range(4):
                        mm = nc.tensor.transpose(ps[:, 2 * th + c, q * P:(q + 1) * P], attn[:, 4 * th + q, c * P:(c + 1) * P],
                                                 ident[:, :])
                    mm.then_inc(T["aT_ps"], 1)
            for t in range(NT):
                pe.wait_ge(T["aT"], 2 * (t // 4) + 2)
                o = ps[:, 4 + (t // 2) % 2 + 2 * (t // 4), (t % 2) * 256:(t % 2) * 256 + 256]
                for c in range(2):
                    nc.tensor.matmul(o, attnT[:, c, t * P:(t + 1) * P], wout[:, c, :], start=(c == 0), stop=False)
                mm = nc.tensor.matmul(o, ones_row[:, :], bout[:, :], start=False, stop=True)
                if t % 2:
                    mm.then_inc(T["out"], 1)

        def one(view, hd):
            if isinstance(hd, int):
                return view[:, hd, :]
            return view[:, bass.ds(hd, 1), :].rearrange("r o n -> r (o n)")

        def att_act(act):
            act.wait_ge(T["red"], 5)
            nc.scalar.activation(sin[:, :], cos[:, :], ACT.Sin).then_inc(T["sin"], 1)
            nc.scalar.activation(rope_b, cos[:, :], ACT.Abs).then_inc(T["sin"], 1)
            act.wait_ge(T["red"], 6)
            nc.scalar.activation(cos[:, :], rope_b, ACT.Sin).then_inc(T["cos"], 1)
            for k in range(4):
                act.wait_ge(T["v_ps"], k + 1)
                nc.scalar.copy(vv[:, 2 * k:2 * k + 2, :].rearrange("p a b -> p (a b)"), ps[:, 4 + k, :]).then_inc(T["v"], 1)
            act.sem_inc(T["exp"], 2)
            act.sem_inc(T["o"], 1)

            def exps(s, G):
                for p in range(2):
                    act.wait_ge(T["B"], 2 * G + p + 1)
                    act.wait_ge(T["pv"], G + 1)
                    nc.scalar.activation(probs[:, 2 * s + p, :, :, :].rearrange("p a b c -> p (a b c)"),
                                         ps[:, 2 + 2 * p:4 + 2 * p, :].rearrange("p a b -> p (a b)"), ACT.Exp,
                                         scale=float(1.0 / np.sqrt(np.float32(HD)))).then_inc(T["exp"], 1)

            def evac(g, G):
                act.wait_ge(T["pv"], G + 1 + 2)
                nc.scalar.copy(o_rows[:, bass.ds(g, 1), :].rearrange("p a b -> p (a b)"), ps[:, 6, 0:256]
                               ).then_inc(T["o"], 1)

            def turn(b, i, last):
                for s in range(2):
                    if not (last and s == 1):
                        exps((s + 1) % 2, 8 * b + 2 * i + s + 1)
                    evac(2 * i + s, 8 * b + 2 * i + s)

            for b in range(BATCH):
                exps(0, 8 * b)
                if b:
                    act.wait_ge(T["oT"], 4 * b)
                with act.Fori(0, GROUPS // 2 - 1) as i:
                    turn(b, i, False)
                turn(b, GROUPS // 2 - 1, True)
            for k in range(4):
                act.wait_ge(T["aT_ps"], k + 1)
                th, c = k // 2, k % 2
                nc.scalar.copy(attnT[:, c, th * 512:(th + 1) * 512], ps[:, k, :]).then_inc(T["aT"], 1)

        def att_dve(dve):
            v = nc.vector
            v.memset(qa[64:96, :, :, :].rearrange("p a b c -> p (a b c)"), 0.0).then_inc(T["zero"], 1)
            v.memset(ka[64:96, :, :, :].rearrange("p a b c -> p (a b c)"), 0.0).then_inc(T["zero"], 1)
            v.memset(ka[96:99, :, :, :].rearrange("p a b c -> p (a b c)"), -1.0).then_inc(T["zero"], 1)
            dve.wait_ge(T["w"], 64)
            for w, sw in ((wkv[:, 0:DM], wk_sw[:, :]), (wq.rearrange("p k n -> p (k n)"), wq_sw.rearrange("p k n -> p (k n)"))):
                src = w.rearrange("p (n two) -> p n two", two=2)
                dst = sw.rearrange("p (n two) -> p n two", two=2)
                link(v.tensor_scalar(dst[:, :, 0:1], src[:, :, 1:2], -1.0, None, ALU.mult))
                link(v.tensor_copy(dst[:, :, 1:2], src[:, :, 0:1]))
                dve.wait_ge(dve_order, step_count[0])
                dve.sem_inc(T["sw"], 1)
            dve.wait_ge(T["ang"], 1)
            ang = ps[:, 0:2, :].rearrange("p a b -> p (a b)")
            v.tensor_copy(rope_a, ang).then_inc(T["red"], 1)
            dve.wait_ge(T["red"], 1)
            v.tensor_scalar(rope_b, rope_a, float(1.0 / TWO_PI), ROUND, ALU.mult, ALU.add).then_inc(T["red"], 1)
            dve.wait_ge(T["red"], 2)
            v.tensor_scalar(rope_b, rope_b, ROUND, None, ALU.subtract).then_inc(T["red"], 1)
            dve.wait_ge(T["red"], 3)
            v.scalar_tensor_tensor(rope_a, rope_b, -6.28125, rope_a, ALU.mult, ALU.add).then_inc(T["red"], 1)
            dve.wait_ge(T["red"], 4)
            then(dve, v.scalar_tensor_tensor(rope_a, rope_b, -float(TWO_PI - 6.28125), rope_a, ALU.mult, ALU.add))
            v.tensor_scalar(cos[:, :], rope_a, 3.1415925, -3.1415925, ALU.min, ALU.max).then_inc(T["red"], 1)
            dve.wait_ge(T["sin"], 2)
            v.tensor_scalar(rope_b, rope_b, -1.0, float(np.pi / 2), ALU.mult, ALU.add).then_inc(T["red"], 1)
            dve.wait_ge(T["cos"], 1)
            for un in range(4):
                base = 4 * (1 - un % 2)
                pr = parts[un % 2]
                dve.wait_ge(T["proj"], 2 * un + 1)
                v.tensor_tensor(
                    rope_a, ps[:, base:base + 2, :].rearrange("p a b -> p (a b)"), cos[:, :], ALU.mult).then_inc(T["rope"], 1)
                dve.wait_ge(T["proj"], 2 * un + 2)
                v.tensor_tensor(rope_b, ps[:, base + 2:base + 4, :].rearrange("p a b -> p (a b)"), sin[:, :],
                                ALU.mult).then_inc(T["rope"], 1)
                dve.wait_ge(T["rope"], 2 * un + 2)
                then(dve, v.tensor_tensor(rope_a, rope_a, rope_b, ALU.add))
                if un >= 2:
                    dve.wait_ge(T[f"sent{un % 2}"], 16)
                v.tensor_copy(pr[:, 0, :], rope_a).then_inc(T["part"], 1)
                dve.wait_ge(T["part"], 3 * un + 1)
                then(dve, v.tensor_tensor(rope_b, rope_a, pr[:, 0, :], ALU.subtract))
                v.tensor_copy(pr[:, 1, :], rope_b).then_inc(T["part"], 1)
                dve.wait_ge(T["part"], 3 * un + 2)
                v.tensor_tensor(pr[:, 2, :], rope_b, pr[:, 1, :], ALU.subtract).then_inc(T["part"], 1)
                dve.wait_ge(T["part"], 3 * un + 3)
            dve.sem_inc(T["max"], 2)

            def head_max(slot, hd, par, n):
                dve.wait_ge(T["A"], n + 1)
                v.tensor_reduce(mx[:, slot, :, bass.ds(hd, 1)].rearrange("p a o -> p (a o)"),
                                ps[:, par, :].rearrange("p (a k) -> p a k", a=2), AX.X, ALU.max).then_inc(T["max"], 1)

            def max_split(b):
                dve.wait_ge(T["mT"], b + 1)
                if b:
                    dve.wait_ge(T["msent"], 16 * b)
                then(dve, v.tensor_copy(m_rest[:, 0, :], ps[0:32, 7, 0:256]))
                then(dve, v.tensor_copy(m_parts[:, 0, :], m_rest[:, 0, :]))
                then(dve, v.tensor_tensor(m_rest[:, 1, :], m_rest[:, 0, :], m_parts[:, 0, :], ALU.subtract))
                then(dve, v.tensor_copy(m_parts[:, 1, :], m_rest[:, 1, :]))
                v.tensor_tensor(m_parts[:, 2, :], m_rest[:, 1, :], m_parts[:, 1, :], ALU.subtract).then_inc(T["mrow"], 1)

            with dve.Fori(0, HEADS // 2) as i:
                for j in range(2):
                    head_max(0, 2 * i + j, j, 2 * i + j)
            max_split(0)
            for b in range(BATCH):
                if b + 1 < BATCH:
                    with dve.Fori(0, HEADS // 2) as i:
                        for j in range(2):
                            head_max((b + 1) % 2, 2 * i + j, j, HEADS * (b + 1) + 2 * i + j)
                    max_split(b + 1)
                for gg in range(GROUPS // 2):
                    dve.wait_ge(T["oT"], 4 * b + gg + 1)
                    o = ps[:, 7, :].rearrange("p (m c) -> p m c", c=32)
                    then(dve, v.reciprocal(recip16, o[:, :, HD:HD + 1]))
                    for qt in range(2):
                        dst = attn[:, 2 * b + qt, 64 * gg:64 * gg + 64].rearrange("p (m c) -> p m c", c=HD)
                        ins = v.tensor_tensor(dst, o[:, 8 * qt:8 * qt + 8, 0:HD],
                                              recip16[:, 8 * qt:8 * qt + 8, :].to_broadcast([P, 8, HD]), ALU.mult)
                        if qt == 0:
                            link(ins)
                    ins.then_inc(T["attn"], 1)
            for t in range(NT):
                dve.wait_ge(T["out"], t // 2 + 1)
                o = ps[:, 4 + (t // 2) % 2 + 2 * (t // 4), (t % 2) * 256:(t % 2) * 256 + 256]
                v.scalar_tensor_tensor(X[:, t, :], o, tg[:, 1:2], X[:, t, :], ALU.mult, ALU.add).then_inc(T["X3"], 1)
            dve.wait_ge(T["X3"], NT)

        def att_pool(pool):
            g = nc.gpsimd
            pool.wait_ge(T["zero"], 3)
            g.memset(v_pad.rearrange("p a b c d -> p (a b c d)"), 0.0).then_inc(T["setv"], 1)
            pool.wait_ge(T["setv"], 1)
            g.memset(v_pad[:, :, :, :, HD:HD + 1].rearrange("p a b c d -> p (a b c) d"), 1.0).then_inc(T["setv"], 1)
            pool.wait_ge(T["setv"], 2)
            pool.wait_ge(T["v"], 4)
            for b in range(BATCH):
                with pool.Fori(0, GROUPS // 2) as i:
                    for s in range(2):
                        pool.wait_ge(T["pv"], 8 * b + 2 * i + s + 1)
                        src = vv[:, 2 * b:2 * b + 2, bass.ds(32 * (2 * i + s), 32)]
                        for kc in range(2):
                            ins = g.tensor_copy(v_pad[:, s, kc, :, 0:HD], src[:, kc, :].rearrange("p (h d) -> p h d", d=HD))
                            if kc == 0:
                                ins.then_inc(T["setv"], 1)
                        ins.then_inc(T["vpad"], 1)


        r2 = Region()
        soft = r2("soft", [P, 5, NT, EXPERTS])
        router1 = r2("router1", [P, 2, EXPERTS])
        gate_b = r2("gate_b", [1, EXPERTS])
        b2_sb = r2("b2_sb", [EXPERTS, DM])
        b1_sb = r2("b1_sb", [P, 2, F1 // P])
        w1_sb = r2("w1_sb", [P, 2, 2, F1])
        w2_sb = r2("w2_sb", [P, 2, F1 // P, DM])
        h1 = r2("h1", [P, 2, F1 // P, 512])
        combT = r2("combT", [EXPERTS, TOK])
        N = {n: sem("moe1_" + n) for n in ["small", "lg", "max", "sub", "exp", "comb", "w0", "w1", "gu", "h", "dn",
                                           "acc", "cT_ps", "cT", "bias", "biased", "ready"]}
        HF = F1 // P

        def moe1_sp(sp):
            def load(e, slot):
                one = bass.ds(e, 1)
                sp.dma_start(w1_sb[:, slot, :, :], a["L1_ffn_w1"][one, :, :].rearrange("o (k p) f -> p (o k) f", p=P)
                             ).then_inc(N[f"w{slot}"], 16)
                sp.dma_start(w2_sb[:, slot, :, :], a["L1_ffn_w2"][one, :, :].rearrange("o (k p) f -> p (o k) f", p=P)
                             ).then_inc(N[f"w{slot}"], 16)
                sp.dma_start(b1_sb[:, slot, :], a["L1_ffn_b1"][one, :].rearrange("o (f p) -> p (o f)", p=P),
                             allow_slow_non_contiguous=True).then_inc(N[f"w{slot}"], 16)
            sp.wait_ge(T["X3"], NT)
            sp.dma_start(router1[:, :, :], a["L1_ffn_gate_w"].rearrange("(k p) e -> p k e", p=P)).then_inc(N["small"], 16)
            sp.dma_start(gate_b[:, :], a["L1_ffn_gate_b"].unsqueeze(0)).then_inc(N["small"], 16)
            sp.dma_start(b2_sb[:, :], a["L1_ffn_b2"]).then_inc(N["small"], 16)
            for e in range(2):
                load(e, e)
            with sp.Fori(0, EXPERTS // 2 - 1) as i:
                for slot in range(2):
                    sp.wait_ge(N["dn"], 4 * i + 2 * slot + 2)
                    load(2 * i + slot + 2, slot)

        def gate1_pe(pe):
            pe.wait_ge(ln[3].t, 4)
            pe.wait_ge(N["small"], 48)
            for t in range(NT):
                o = ps[:, 7, t * EXPERTS:(t + 1) * EXPERTS]
                for c in range(2):
                    nc.tensor.matmul(o, xnT[:, c, t * P:(t + 1) * P], router1[:, c, :], start=(c == 0), stop=False)
                mm = nc.tensor.matmul(o, ones_row[:, :], gate_b[:, :], start=False, stop=True)
            mm.then_inc(N["lg"], 1)

        def gate1_act(act):
            act.wait_ge(N["sub"], 1)
            nc.scalar.activation(soft[:, 1, :, :], soft[:, 0, :, :], ACT.Exp).then_inc(N["exp"], 1)

        def gate1_dve(dve):
            v = nc.vector
            lg, ex, msk = (soft[:, k, :, :] for k in range(3))
            dve.wait_ge(N["lg"], 1)
            then(dve, v.tensor_copy(lg, ps[:, 7, 0:NT * EXPERTS].rearrange("p (t e) -> p t e", t=NT)))
            then(dve, v.tensor_reduce(per_tile[:, 0, :], lg, AX.X, ALU.max))
            v.tensor_tensor(lg, lg, by_tile(0), ALU.subtract).then_inc(N["sub"], 1)
            dve.wait_ge(N["exp"], 1)
            then(dve, v.tensor_reduce(per_tile[:, 0, :], ex, AX.X, ALU.add))
            then(dve, v.reciprocal(per_tile[:, 1, :], per_tile[:, 0, :]))
            then(dve, v.tensor_tensor(ex, ex, by_tile(1), ALU.mult))
            top2(dve, ex, msk)
            then(dve, v.tensor_tensor(ex, ex, msk, ALU.mult))
            then(dve, v.tensor_reduce(per_tile[:, 2, :], ex, AX.X, ALU.add))
            then(dve, v.reciprocal(per_tile[:, 3, :], per_tile[:, 2, :]))
            then(dve, v.tensor_scalar(per_tile[:, 3, :], per_tile[:, 3, :], tg[:, 3:4], None, ALU.mult))
            v.tensor_tensor(comb[:, :, :], ex, by_tile(3), ALU.mult).then_inc(N["comb"], 1)

        def bias_pe(pe):
            pe.wait_ge(N["comb"], 1)
            for t in range(NT):
                mm = nc.tensor.transpose(ps[0:EXPERTS, 4 + t // 4, (t % 4) * P:(t % 4 + 1) * P], comb[:, t, :], ident[:, :])
            mm.then_inc(N["cT_ps"], 1)
            pe.wait_ge(N["cT"], 2)
            for t in range(NT):
                mm = nc.tensor.matmul(ps[:, 4 + t // 2, (t % 2) * 256:(t % 2) * 256 + 256], combT[:, t * P:(t + 1) * P],
                                      b2_sb[:, :], start=True, stop=True)
            mm.then_inc(N["bias"], 1)

        def bias_dve(dve):
            dve.wait_ge(N["bias"], 1)
            for t in range(NT):
                nc.vector.tensor_tensor(X[:, t, :], X[:, t, :], ps[:, 4 + t // 2, (t % 2) * 256:(t % 2) * 256 + 256],
                                        ALU.add).then_inc(N["acc"], 1)

        def bias_act(act):
            act.wait_ge(N["cT_ps"], 1)
            for k in range(2):
                nc.scalar.copy(combT[:, k * 512:(k + 1) * 512], ps[0:EXPERTS, 4 + k, :]).then_inc(N["cT"], 1)

        def moe1_pe(pe):
            def up(k, q, w_wait):
                slot, th = q // 2, q % 2
                if th == 0:
                    pe.wait_ge(N[f"w{slot}"], w_wait)
                for f in range(HF):
                    pe.wait_ge(N["h"], HF * k + f + 1)
                    for c in range(2):
                        mm = nc.tensor.matmul(ps[:, f % 4, :], w1_sb[:, slot, c, f * P:(f + 1) * P],
                                              xnT[:, c, th * 512:(th + 1) * 512], start=(c == 0), stop=(c == 1))
                    mm.then_inc(N["gu"], 1)

            def down(k, q):
                slot, th = q // 2, q % 2
                pe.wait_ge(N["h"], HF * k + HF + 4)
                pe.wait_ge(N["acc"], 4 * k + 4)
                for t in range(4):
                    for f in range(HF):
                        mm = nc.tensor.matmul(ps[:, 4 + 2 * th + t // 2, (t % 2) * 256:(t % 2) * 256 + 256],
                                              h1[:, th, f, t * P:(t + 1) * P], w2_sb[:, slot, f, :],
                                              start=(f == 0), stop=(f == HF - 1))
                mm.then_inc(N["dn"], 1)

            def turn(i, last):
                for q in range(4):
                    if not (last and q == 3):
                        up(4 * i + q + 1, (q + 1) % 4, 48 * i + 48 * ((q + 1) // 4) + 48)
                    down(4 * i + q, q)

            up(0, 0, 48)
            with pe.Fori(0, EXPERTS // 2 - 1) as i:
                turn(i, False)
            turn(EXPERTS // 2 - 1, True)

        def moe1_act(act):
            act.sem_inc(N["h"], 4)
            act.wait_ge(N["ready"], 1)
            with act.Fori(0, EXPERTS // 2) as i:
                for slot in range(2):
                    for th in range(2):
                        for f in range(HF):
                            act.wait_ge(N["gu"], 32 * i + 16 * slot + 8 * th + f + 1)
                            if f == 0:
                                act.wait_ge(N["ready"], 4 * i + 2 * slot + th + 1)
                            nc.scalar.activation(h1[:, th, f, :], ps[:, f % 4, :], ACT.Gelu_apprx_tanh,
                                                 bias=b1_sb[:, slot, f:f + 1]).then_inc(N["h"], 1)

        def moe1_dve(dve):
            dve.sem_inc(N["ready"], 2)
            with dve.Fori(0, EXPERTS) as e:
                for th in range(2):
                    dve.wait_ge(N["dn"], 2 * e + th + 1)
                    dve.wait_ge(N["acc"], 8 + 8 * e + 4 * th - 4)
                    for t in range(4):
                        tile = 4 * th + t
                        ins = nc.vector.scalar_tensor_tensor(
                            X[:, tile, :], ps[:, 4 + 2 * th + t // 2, (t % 2) * 256:(t % 2) * 256 + 256],
                            comb[:, tile, bass.ds(e, 1)], X[:, tile, :], ALU.mult, ALU.add)
                        ins.then_inc(N["acc"], 1)
                    dve.sem_inc(N["ready"], 1)
            dve.wait_ge(N["acc"], 8 + 8 * EXPERTS)

        block = ctx.enter_context(nc.Block())

        @block.sync
        def _(sp):
            sp.dma_start(ident[:, :], a["ident"]).then_inc(ld_const, 16)
            sp.dma_start(ctx_in[:, :, :], a["ctx_1024"].rearrange("b (h p) d -> p (b h) d", p=P)).then_inc(ld_ctx, 16)
            sp.dma_start(in_w[:, :, :], a["L0_xattn_in_proj_w"].rearrange("(e p) d -> p e d", p=P)).then_inc(ld_ssm, 16)
            sp.dma_start(x_w[:, :], a["L0_xattn_x_proj_w"]).then_inc(ld_ssm, 16)
            sp.dma_start(dt_w[:, :, :], a["L0_xattn_dt_proj_w"].rearrange("(e p) d -> p e d", p=P)).then_inc(ld_ssm, 16)
            sp.dma_start(cols[:, :, 0:DC], a["L0_xattn_conv_w"].rearrange("(e p) d -> p e d", p=P)).then_inc(ld_ssm, 16)
            for k, n in enumerate(["conv_b", "dt_proj_b", "D"]):
                sp.dma_start(cols[:, :, DC + k:DC + k + 1],
                             a["L0_xattn_" + n].rearrange("(e p o) -> p e o", p=P, o=1),
                             allow_slow_non_contiguous=True).then_inc(ld_ssm, 16)
            sp.dma_start(a_log[:, :, :], a["L0_xattn_A_log"].rearrange("(e p) d -> p e d", p=P)).then_inc(ld_ssm, 16)
            sp.dma_start(gates[:, 0:2], a["g_xattn"].unsqueeze(0).to_broadcast([P, 2])).then_inc(ld_gate, 16)
            sp.dma_start(gates[:, 2:4], a["g_ffn"].unsqueeze(0).to_broadcast([P, 2])).then_inc(ld_gate, 16)
            sp.dma_start(temp[:, :], a["L0_ffn_temperature"].unsqueeze(0).to_broadcast([P, 1])).then_inc(ld_gate, 16)
            sp.dma_start(rows[:, :, :], a["rows"]).then_inc(ld_const, 16)
            sp.dma_start(before[:, :, :], a["before"]).then_inc(ld_const, 16)
            sp.dma_start(freq[:, :], a["freq"]).then_inc(ld_const, 16)
            sp.dma_start(X[:, :, :], a["x"].rearrange("b (h p) d -> p (b h) d", p=P)).then_inc(ld_x, 16)
            sp.dma_start(posT[:, :], a["fside_BxSx2_0"].rearrange("b s a -> a (b s)"),
                         allow_slow_non_contiguous=True).then_inc(ld_pos, 16)
            sp.dma_start(ones_row[:, :], a["rows"][0:1, 0, :]).then_inc(ld_const, 16)
            if upto >= 2:
                moe0_sp(sp)
                sp.wait_ge(M["acc"], 8 + 8 * EXPERTS)
            if upto >= 3:
                att_sp(sp)
                sp.wait_ge(T["X3"], NT)
            if upto >= 4:
                moe1_sp(sp)
                sp.wait_ge(N["acc"], 8 + 8 * EXPERTS)
            sp.wait_ge(S["X1"], NT)
            sp.dma_start(out.rearrange("b (h p) d -> p (b h) d", p=P), X[:, :, :]).then_inc(stored, 16)
            sp.wait_ge(stored, 16)

        @block.vector
        def _(dve):
            nc.vector.memset(minushalf[:, :], -0.5).then_inc(set_up, 1)
            dve.wait_ge(ld_x, 16)
            ln_dve(dve, ln[0])
            ssm_dve(dve)
            if upto >= 2:
                ln_dve(dve, ln[1])
                gate0_dve(dve)
                moe0_dve(dve)
            if upto >= 3:
                ln_dve(dve, ln[2])
                att_dve(dve)
            if upto >= 4:
                ln_dve(dve, ln[3])
                gate1_dve(dve)
                bias_dve(dve)
                moe1_dve(dve)

        @block.gpsimd
        def _(pool):
            pool.wait_ge(set_up, 2)
            ln_pool(pool, ln[0])
            if upto >= 2:
                ln_pool(pool, ln[1])
            if upto >= 3:
                ln_pool(pool, ln[2])
                att_pool(pool)
            if upto >= 4:
                ln_pool(pool, ln[3])

        @block.scalar
        def _(act):
            ssm_act(act)
            if upto >= 2:
                ln_act(act, ln[1])
                gate0_act(act)
                moe0_act(act)
            if upto >= 3:
                ln_act(act, ln[2])
                att_act(act)
            if upto >= 4:
                ln_act(act, ln[3])
                gate1_act(act)
                bias_act(act)
                moe1_act(act)

        @block.tensor
        def _(pe):
            ssm_pe(pe)
            if upto >= 2:
                ln_pe(pe, ln[1])
                gate0_pe(pe)
                moe0_pe(pe)
            if upto >= 3:
                ln_pe(pe, ln[2])
                att_pe(pe)
            if upto >= 4:
                ln_pe(pe, ln[3])
                gate1_pe(pe)
                bias_pe(pe)
                moe1_pe(pe)


def kernel(_upto=99, **inputs):
    import concourse.bacc as bacc
    from concourse.bass_utils import run_bass_kernel_spmd as run

    nc = bacc.Bacc("TRN2", target_bir_lowering=False, num_devices=1)
    arrays, args = {}, {}
    for name, value in {**inputs, **constants()}.items():
        v = np.ascontiguousarray(value)
        arrays["in_" + name] = v
        args[name] = nc.dram_tensor("in_" + name, v.shape, mybir.dt.from_np(v.dtype), kind="ExternalInput").ap()
    out = nc.dram_tensor("out_x", (BATCH, SEQ, DM), F32, kind="ExternalOutput").ap()
    program(nc, args, out, _upto)
    return run(nc, [arrays], core_ids=[0]).results[0]["out_x"]
```

```python
from contextlib import ExitStack

import numpy as np

import concourse.bass as bass
from concourse import mybir

ALU = mybir.AluOpType
ACT = mybir.ActivationFunctionType
F32 = mybir.dt.float32
BF16 = mybir.dt.bfloat16
AX = mybir.AxisListType

P = 128
BATCH, SEQ, DM = 4, 256, 256
NT = BATCH * SEQ // P
TOK = BATCH * SEQ
CTX = 128
DI, DS, DC, DR = 256, 16, 4, 8
EXPERTS = 8
F0, F1 = 256, 1024
HEADS, HD = 32, 8
EPS = 1e-5
GOLDEN = 1.0 / np.e
LOWER, UPPER = 0.5 - np.log(4.0 / 3.0), 0.5
FAR = 1e36
SLOT_TILES = 2 * TOK // P + EXPERTS - 1
TWO_PI = 2.0 * np.pi
ARENA = 42400
ROUND = 1.5 * 2.0 ** 23


def constants():
    ident = np.eye(P, dtype=np.float32)
    rows = np.zeros((96, 32, P), np.float32)
    for r in range(96):
        rows[r, r % 32, :] = 1.0
    before = np.zeros((P, EXPERTS, EXPERTS), np.float32)
    for e in range(EXPERTS):
        before[:, e, :e] = 1.0
    freq = np.zeros((2, P), np.float32)
    for p in range(P):
        freq[(p // 4) % 2, p] = np.float32(10000.0) ** np.float32(-((p // 2) % 2) / 2)
    lower = np.triu(np.ones((P, P), np.float32), 1)
    tile_no = np.arange(SLOT_TILES, dtype=np.float32)[None, :]
    return {"ident": ident, "rows": rows, "before": before, "freq": freq, "lower": lower, "tile_no": tile_no}


def program(nc, a, out, upto=99):
    ctx = ExitStack()
    with ctx:
        def sb(name, shape, dt=F32):
            return ctx.enter_context(nc.sbuf_tensor(name, shape, dt))

        def sem(name):
            return ctx.enter_context(nc.semaphore(name))

        ps = ctx.enter_context(nc.psum_tensor("ps", [P, 8, 512], F32))

        X = sb("X", [P, NT, DM])
        xn = sb("xn", [P, NT, DM])
        xnT = sb("xnT", [P, 2, TOK])
        ctxT = sb("ctxT", [P, TOK])
        ident = sb("ident", [P, P])
        before = sb("before", [P, EXPERTS, EXPERTS])
        freq = sb("freq", [2, P])
        stats = sb("stats", [P, NT, 6])
        meanvar = sb("meanvar", [P, NT, 2])
        vareps = sb("vareps", [P, NT])
        minushalf = sb("minushalf", [P, NT])
        rstd = sb("rstd", [P, NT])
        gates = sb("gates", [P, 4])
        tg = sb("tg", [P, 4])
        temp = sb("temp", [P, 1])
        halfrt = sb("halfrt", [P, 1])
        posT = sb("posT", [2, TOK])
        ones_row = sb("ones_row", [1, P])

        arena = sb("arena", [P, ARENA])

        class Region:
            def __init__(self):
                self.used = 0

            def __call__(self, name, shape, dt=F32):
                count = 1
                for d in shape[1:]:
                    count *= d
                words = (count + 1) // 2 if dt == BF16 else count
                view = arena[0:shape[0], self.used:self.used + words]
                self.used += words
                assert self.used <= ARENA, (name, self.used)
                if dt != F32:
                    view = view.bitcast(dt)
                if len(shape) > 2:
                    axes = "abcd"[:len(shape) - 1]
                    view = view.rearrange(f"p ({' '.join(axes)}) -> p {' '.join(axes)}",
                                          **dict(zip(axes, shape[1:])))
                return view

        ld_const, ld_x, ld_ctx, ld_ssm, ld_gate, ld_att, ld_pos = (
            sem("ld_const"), sem("ld_x"), sem("ld_ctx"), sem("ld_ssm"), sem("ld_gate"), sem("ld_att"), sem("ld_pos"))
        set_up = sem("set_up")
        stored = sem("stored")
        dve_order = sem("dve_order")
        act_order = sem("act_order")

        L = {n: sem("ln_" + n) for n in ["stat", "agg", "var", "rstd", "xn", "xnT_ps", "xnT"]}

        def ln_dve(dve, n):
            for t in range(NT):
                nc.vector.bn_stats(stats[:, t, :], X[:, t, :]).then_inc(L["stat"], 1)
            for t in range(NT):
                dve.wait_ge(L["stat"], NT * n + t + 1)
                nc.vector.bn_aggr(meanvar[:, t, :], stats[:, t, :]).then_inc(L["agg"], 1)
            dve.wait_ge(L["agg"], NT * n + NT)
            nc.vector.tensor_scalar(vareps[:, :], meanvar[:, :, 1], EPS, None, ALU.add).then_inc(L["var"], 1)
            dve.wait_ge(L["rstd"], n + 1)
            for t in range(NT):
                nc.vector.tensor_scalar(xn[:, t, :], X[:, t, :], meanvar[:, t, 0:1], rstd[:, t:t + 1],
                                        ALU.subtract, ALU.mult).then_inc(L["xn"], 1)

        def ln_pool(pool, n):
            pool.wait_ge(L["var"], n + 1)
            nc.gpsimd.tensor_tensor(rstd[:, :], vareps[:, :], minushalf[:, :], ALU.pow).then_inc(L["rstd"], 1)

        def ln_pe(pe, n):
            for th in range(2):
                pe.wait_ge(L["xn"], NT * n + 4 * th + 4)
                for c in range(2):
                    for q in range(4):
                        mm = nc.tensor.transpose(ps[:, 2 * th + c, q * P:(q + 1) * P],
                                                 xn[:, 4 * th + q, c * P:(c + 1) * P], ident[:, :])
                    mm.then_inc(L["xnT_ps"], 1)

        def ln_act(act, n):
            for th in range(2):
                for c in range(2):
                    act.wait_ge(L["xnT_ps"], 4 * (n - 1) + 2 * th + c + 1)
                    nc.scalar.copy(xnT[:, c, th * 512:(th + 1) * 512], ps[:, 2 * th + c, :]).then_inc(L["xnT"], 1)

        sbs = Region()

        ctx_in = sbs("ctx_in", [P, NT, CTX])
        in_w = sbs("in_w", [P, 2, CTX])
        x_w = sbs("x_w", [DR + 2 * DS, DI])
        dt_w = sbs("dt_w", [P, 2, DR])
        cols = sbs("cols", [P, 2, DC + 3])
        a_log = sbs("a_log", [P, 2, DS])
        neg_a = sbs("neg_a", [P, 2, DS])
        rows = sbs("rows", [96, 32, P])
        rows_bf = sbs("rows_bf", [96, 32, P], BF16)
        in_wT = sbs("in_wT", [P, DI])
        x_wT = sbs("x_wT", [P, 2, DR])
        bc_wT = sbs("bc_wT", [P, 2, 96])
        dt_wT = sbs("dt_wT", [DR, DI])
        diag = sbs("diag", [P, 2, P])
        xpad = sbs("xpad", [P, 2, BATCH, SEQ + DC - 1])
        conv = sbs("conv", [P, 2, TOK])
        u = sbs("u", [P, 2, TOK])
        dt_lo = sbs("dt_lo", [DR, TOK])
        t_abs = sbs("t_abs", [P, 2, TOK])
        t_exp = sbs("t_exp", [P, 2, TOK])
        delta = sbs("delta", [P, 2, TOK])
        du = sbs("du", [P, 2, TOK])
        bc = sbs("bc", [96, 3, TOK])
        bc3 = sbs("bc3", [96, TOK], BF16)
        dA = sbs("dA", [P, 2, 2, TOK])
        dBu = sbs("dBu", [P, 2, TOK])
        h = sbs("h", [P, 2, TOK])
        hC = sbs("hC", [P, 2, TOK])
        sz = t_abs[:, :, :].rearrange("p e (b l) -> p e b l", b=BATCH)
        gy = t_exp

        names = ["wT", "wTc", "ctxT_ps", "ctxT", "xin_ps", "xpad", "conv", "u", "xdbl_ps", "dt_lo", "bc_cp", "bc_r",
                 "bc3", "dt_ps", "v", "abs", "exp", "plus", "log", "delta", "du", "far", "na", "B", "C", "dA", "dBu", "scan",
                 "hC", "Y", "seed", "sz", "gy", "yT", "X1", "zero"]
        S = {n: sem("ssm_" + n) for n in names}

        def ssm_dve(dve):
            nc.vector.memset(xpad[:, :, :, 0:DC - 1], 0.0).then_inc(S["zero"], 1)
            dve.wait_ge(S["wT"], 1)
            nc.vector.tensor_copy(in_wT[:, :], ps[:, 4, 0:256]).then_inc(S["wTc"], 1)
            for k in range(2):
                src = ps[:, 5, k * 64:k * 64 + 40]
                nc.vector.tensor_copy(x_wT[:, k, :], src[:, 0:DR]).then_inc(S["wTc"], 1)
                nc.vector.tensor_copy(bc_wT[:, k, :].rearrange("p (r n) -> p r n", r=3),
                                      src[:, DR:40].unsqueeze(1).to_broadcast([P, 3, 32])).then_inc(S["wTc"], 1)
            nc.vector.tensor_copy(dt_wT[:, :], ps[0:DR, 6, 0:256]).then_inc(S["wTc"], 1)
            dve.wait_ge(ld_const, 16 * 5)
            nc.vector.tensor_copy(rows_bf[:, :, :], rows[:, :, :]).then_inc(S["wTc"], 1)
            for e in range(2):
                nc.vector.tensor_scalar(diag[:, e, :], ident[:, :], cols[:, e, DC + 2:DC + 3], None,
                                        ALU.mult).then_inc(S["wTc"], 1)
            for e in range(2):
                dve.wait_ge(S["xpad"], 2 * e + 2)
                o = conv[:, e, :].rearrange("p (b l) -> p b l", b=BATCH)
                for k in range(DC):
                    if k:
                        dve.wait_ge(S["conv"], DC * e + k)
                        nc.vector.scalar_tensor_tensor(o, xpad[:, e, :, k:k + SEQ], cols[:, e, k:k + 1], o,
                                                       ALU.mult, ALU.add).then_inc(S["conv"], 1)
                    else:
                        nc.vector.tensor_scalar(o, xpad[:, e, :, 0:SEQ], cols[:, e, 0:1], None,
                                                ALU.mult).then_inc(S["conv"], 1)
            dve.wait_ge(S["bc_cp"], 2)
            nc.vector.tensor_copy(bc3[0:32, :], bc[0:32, 0, :]).then_inc(S["bc3"], 1)
            hi = t_abs[0:96, 0, :].bitcast(BF16)[:, 0:TOK]
            lo = t_abs[0:96, 1, :].bitcast(BF16)[:, 0:TOK]
            nc.vector.tensor_copy(hi, bc[:, 0, :]).then_inc(S["bc_r"], 1)
            dve.wait_ge(S["bc_r"], 1)
            nc.vector.tensor_tensor(bc[:, 1, :], bc[:, 0, :], hi, ALU.subtract).then_inc(S["bc_r"], 1)
            dve.wait_ge(S["bc_r"], 2)
            nc.vector.tensor_copy(bc3[32:64, :], bc[32:64, 1, :]).then_inc(S["bc3"], 1)
            nc.vector.tensor_copy(lo, bc[:, 1, :]).then_inc(S["bc_r"], 1)
            dve.wait_ge(S["bc_r"], 3)
            nc.vector.tensor_tensor(bc[:, 2, :], bc[:, 1, :], lo, ALU.subtract).then_inc(S["bc_r"], 1)
            dve.wait_ge(S["bc_r"], 4)
            nc.vector.tensor_copy(bc3[64:96, :], bc[64:96, 2, :]).then_inc(S["bc3"], 1)
            for e in range(2):
                dve.wait_ge(S["v"], e + 1)
                nc.vector.tensor_scalar(delta[:, e, :], conv[:, e, :], 0.0, None, ALU.max).then_inc(S["plus"], 1)
                dve.wait_ge(S["exp"], e + 1)
                nc.vector.tensor_scalar(dBu[:, e, :], t_exp[:, e, :], 1.0, None, ALU.add).then_inc(S["plus"], 1)
                dve.wait_ge(S["plus"], 4 * e + 2)
                nc.vector.scalar_tensor_tensor(h[:, e, :], dBu[:, e, :], -1.0, t_exp[:, e, :],
                                               ALU.add, ALU.subtract).then_inc(S["plus"], 1)
                dve.wait_ge(S["plus"], 4 * e + 3)
                nc.vector.tensor_tensor(delta[:, e, :], delta[:, e, :], h[:, e, :], ALU.subtract).then_inc(S["plus"], 1)
                dve.wait_ge(S["plus"], 4 * e + 4)
                dve.wait_ge(S["log"], e + 1)
                nc.vector.tensor_tensor(delta[:, e, :], delta[:, e, :], hC[:, e, :], ALU.add).then_inc(S["delta"], 1)
                dve.wait_ge(S["delta"], e + 1)
                dve.wait_ge(S["u"], e + 1)
                nc.vector.tensor_tensor(du[:, e, :], delta[:, e, :], u[:, e, :], ALU.mult).then_inc(S["du"], 1)
                dve.wait_ge(S["du"], e + 1)
                nc.vector.memset(delta[:, e, :].rearrange("p (b l) -> p b l", b=BATCH)[:, :, 0:1],
                                 FAR).then_inc(S["far"], 1)
            dve.wait_ge(S["far"], 2)

            def step(n, s):
                psB = ps[:, 0:2, :].rearrange("p k n -> p (k n)")
                psC = ps[:, 2:4, :].rearrange("p k n -> p (k n)")
                dve.wait_ge(S["B"], n + 1)
                for e in range(2):
                    nc.vector.tensor_tensor(dBu[:, e, :], du[:, e, :], psB, ALU.mult).then_inc(S["dBu"], 1)
                for e in range(2):
                    dve.wait_ge(S["dBu"], 2 * n + e + 1)
                    dve.wait_ge(S["dA"], 2 * n + e + 1)
                    nc.vector.tensor_tensor_scan(h[:, e, :], dA[:, s, e, :], dBu[:, e, :], 0.0,
                                                 ALU.mult, ALU.add).then_inc(S["scan"], 1)
                dve.wait_ge(S["C"], n + 1)
                for e in range(2):
                    dve.wait_ge(S["scan"], 4 + 2 * n + e + 1)
                    dve.wait_ge(S["Y"], 2 * n + e + 1)
                    nc.vector.tensor_tensor(hC[:, e, :], h[:, e, :], psC, ALU.mult).then_inc(S["hC"], 1)

            dve.sem_inc(S["scan"], 4)
            with dve.Fori(0, DS // 2) as i:
                for s in range(2):
                    step(2 * i + s, s)
            for e in range(2):
                dve.wait_ge(S["Y"], 2 + 2 * DS)
                dve.wait_ge(S["sz"], e + 1)
                nc.vector.tensor_tensor(gy[:, e, :], ps[:, 4 + 2 * e:6 + 2 * e, :].rearrange("p k n -> p (k n)"),
                                        sz[:, e, :, :].rearrange("p b l -> p (b l)"), ALU.mult).then_inc(S["gy"], 1)
            for t in range(NT):
                dve.wait_ge(S["yT"], t // 2 + 1)
                nc.vector.scalar_tensor_tensor(X[:, t, :], ps[:, t // 2, (t % 2) * 256:(t % 2) * 256 + 256],
                                               tg[:, 0:1], X[:, t, :], ALU.mult, ALU.add).then_inc(S["X1"], 1)
            dve.wait_ge(S["X1"], NT)

        def ssm_pe(pe):
            pe.wait_ge(ld_const, 16 * 5)
            pe.wait_ge(ld_ssm, 16 * SSM_LOADS)
            for e in range(2):
                nc.tensor.transpose(ps[:, 4, e * P:(e + 1) * P], in_w[:, e, :], ident[:, :])
                nc.tensor.transpose(ps[:, 5, e * 64:e * 64 + 40], x_w[:, e * P:(e + 1) * P], ident[0:40, 0:40])
                mm = nc.tensor.transpose(ps[0:DR, 6, e * P:(e + 1) * P], dt_w[:, e, :], ident[:, :])
            mm.then_inc(S["wT"], 1)
            pe.wait_ge(ld_ctx, 16)
            for th in range(2):
                for q in range(4):
                    mm = nc.tensor.transpose(ps[:, 2 + th, q * P:(q + 1) * P], ctx_in[:, 4 * th + q, :], ident[:, :])
                mm.then_inc(S["ctxT_ps"], 1)
            pe.wait_ge(S["wTc"], 9)
            for e in range(2):
                for th in range(2):
                    if not e:
                        pe.wait_ge(S["ctxT"], th + 1)
                    nc.tensor.matmul(ps[:, 4 + 2 * e + th, :], in_wT[:, e * P:(e + 1) * P],
                                     ctxT[:, th * 512:(th + 1) * 512], start=True, stop=True).then_inc(S["xin_ps"], 1)
            pe.wait_ge(S["u"], 2)
            for th in range(2):
                for k in range(2):
                    nc.tensor.matmul(ps[0:96, th, :], bc_wT[:, k, :], u[:, k, th * 512:(th + 1) * 512],
                                     start=(k == 0), stop=(k == 1))
                for k in range(2):
                    mm = nc.tensor.matmul(ps[0:DR, 2 + th, :], x_wT[:, k, :], u[:, k, th * 512:(th + 1) * 512],
                                          start=(k == 0), stop=(k == 1))
                mm.then_inc(S["xdbl_ps"], 1)
            pe.wait_ge(S["dt_lo"], 2)
            for e in range(2):
                for th in range(2):
                    mm = nc.tensor.matmul(ps[:, 4 + 2 * e + th, :], dt_wT[:, e * P:(e + 1) * P],
                                          dt_lo[:, th * 512:(th + 1) * 512], start=True, stop=True)
                mm.then_inc(S["dt_ps"], 1)

            def spread(bank, row, done):
                for th in range(2):
                    mm = nc.tensor.matmul(ps[:, bank + th, :], rows_bf[:, row, :], bc3[:, th * 512:(th + 1) * 512],
                                          start=True, stop=True)
                mm.then_inc(done, 1)

            def add_y(e):
                for th in range(2):
                    mm = nc.tensor.matmul(ps[:, 4 + 2 * e + th, :], ident[:, :], hC[:, e, th * 512:(th + 1) * 512],
                                          start=False, stop=False, skip_group_check=True)
                mm.then_inc(S["Y"], 1)

            pe.wait_ge(S["bc3"], 3)
            spread(0, 0, S["B"])
            spread(2, DS, S["C"])
            pe.wait_ge(S["far"], 2)
            for e in range(2):
                for th in range(2):
                    mm = nc.tensor.matmul(ps[:, 4 + 2 * e + th, :], diag[:, e, :], u[:, e, th * 512:(th + 1) * 512],
                                          start=True, stop=False, skip_group_check=True)
                mm.then_inc(S["Y"], 1)

            def step(n, more=True):
                if more:
                    pe.wait_ge(S["dBu"], 2 * n + 2)
                    spread(0, n + 1, S["B"])
                pe.wait_ge(S["hC"], 2 * n + 1)
                add_y(0)
                pe.wait_ge(S["hC"], 2 * n + 2)
                if more:
                    spread(2, DS + n + 1, S["C"])
                add_y(1)

            with pe.Fori(0, DS - 1) as n:
                step(n)
            step(DS - 1, more=False)
            for b in range(BATCH):
                for lh in range(2):
                    for e in range(2):
                        if b == 0 and lh == 0:
                            pe.wait_ge(S["gy"], e + 1)
                        at = b * SEQ + lh * P
                        mm = nc.tensor.transpose(ps[:, b, lh * 256 + e * P:lh * 256 + (e + 1) * P],
                                                 gy[:, e, at:at + P], ident[:, :])
                mm.then_inc(S["yT"], 1)

        def ssm_act(act):
            act.wait_ge(ld_gate, 32 + 16)
            nc.scalar.activation(tg[:, :], gates[:, :], ACT.Tanh).then_inc(set_up, 1)
            act.wait_ge(ld_ssm, 16 * SSM_LOADS)
            nc.scalar.activation(a_log[:, :, :], a_log[:, :, :], ACT.Exp).then_inc(act_order, 1)
            act.wait_ge(act_order, 1)
            nc.scalar.mul(neg_a[:, :, :], a_log[:, :, :], -1.0).then_inc(S["na"], 1)
            for th in range(2):
                act.wait_ge(S["ctxT_ps"], th + 1)
                nc.scalar.copy(ctxT[:, th * 512:(th + 1) * 512], ps[:, 2 + th, :]).then_inc(S["ctxT"], 1)
            act.wait_ge(S["zero"], 1)
            for e in range(2):
                for th in range(2):
                    act.wait_ge(S["xin_ps"], 2 * e + th + 1)
                    nc.scalar.copy(xpad[:, e, 2 * th:2 * th + 2, DC - 1:],
                                   ps[:, 4 + 2 * e + th, :].rearrange("p (b l) -> p b l", b=2)).then_inc(S["xpad"], 1)
            for e in range(2):
                act.wait_ge(S["conv"], DC * e + DC)
                nc.scalar.activation(u[:, e, :], conv[:, e, :], ACT.Silu, bias=cols[:, e, DC:DC + 1]).then_inc(S["u"], 1)
            for th in range(2):
                act.wait_ge(S["xdbl_ps"], th + 1)
                nc.scalar.copy(dt_lo[:, th * 512:(th + 1) * 512], ps[0:DR, 2 + th, :]).then_inc(S["dt_lo"], 1)
                nc.scalar.copy(bc[:, 0, th * 512:(th + 1) * 512], ps[0:96, th, :]).then_inc(S["bc_cp"], 1)
            act.wait_ge(S["bc_r"], 4)
            for e in range(2):
                act.wait_ge(S["dt_ps"], e + 1)
                nc.scalar.activation(conv[:, e, :], ps[:, 4 + 2 * e:6 + 2 * e, :].rearrange("p k n -> p (k n)"),
                                     ACT.Identity, bias=cols[:, e, DC + 1:DC + 2]).then_inc(S["v"], 1)
                act.wait_ge(S["v"], e + 1)
                nc.scalar.activation(t_abs[:, e, :], conv[:, e, :], ACT.Abs).then_inc(S["abs"], 1)
                act.wait_ge(S["abs"], e + 1)
                nc.scalar.activation(t_exp[:, e, :], t_abs[:, e, :], ACT.Exp, scale=-1.0).then_inc(S["exp"], 1)
            for e in range(2):
                act.wait_ge(S["plus"], 4 * e + 2)
                nc.scalar.activation(hC[:, e, :], dBu[:, e, :], ACT.Ln).then_inc(S["log"], 1)
            act.wait_ge(S["far"], 2)
            with act.Fori(0, DS // 2) as i:
                for s in range(2):
                    for e in range(2):
                        act.wait_ge(S["scan"], 4 * i + 2 * s + e + 1)
                        nc.scalar.activation(dA[:, s, e, :], delta[:, e, :], ACT.Exp,
                                             scale=neg_a[:, e, bass.ds(2 * i + s, 1)]).then_inc(S["dA"], 1)
            act.wait_ge(L["xn"], NT)
            for e in range(2):
                nc.scalar.activation(sz[:, e, :, :], xn[:, e:NT:2, :], ACT.Silu).then_inc(S["sz"], 1)

        SSM_LOADS = 8

        pair_gt = sb("pair_gt", [P, NT, EXPERTS * EXPERTS])
        pair_eq = sb("pair_eq", [P, NT, EXPERTS * EXPERTS])
        before_all = sb("before_all", [P, NT, EXPERTS * EXPERTS])
        rank = sb("rank", [P, NT, EXPERTS])
        per_tile = sb("per_tile", [P, 4, NT])
        comb = sb("comb", [P, NT, EXPERTS])
        step_count = [0]

        def link(ins):
            step_count[0] += 1
            ins.then_inc(dve_order, 1)
            return step_count[0]

        def then(dve, ins):
            dve.wait_ge(dve_order, link(ins))

        def top2(dve, score, mask):
            v = nc.vector
            for t in range(NT):
                gt = pair_gt[:, t, :].rearrange("p (e j) -> p e j", e=EXPERTS)
                eq = pair_eq[:, t, :].rearrange("p (e j) -> p e j", e=EXPERTS)
                other = score[:, t, :].unsqueeze(1).to_broadcast([P, EXPERTS, EXPERTS])
                own = score[:, t, :].unsqueeze(2).to_broadcast([P, EXPERTS, EXPERTS])
                link(v.tensor_tensor(gt, other, own, ALU.is_gt))
                link(v.tensor_tensor(eq, other, own, ALU.is_equal))
            dve.wait_ge(dve_order, step_count[0])
            then(dve, v.tensor_tensor(pair_eq[:, :, :], pair_eq[:, :, :], before_all[:, :, :], ALU.mult))
            then(dve, v.tensor_tensor(pair_gt[:, :, :], pair_gt[:, :, :], pair_eq[:, :, :], ALU.add))
            then(dve, v.tensor_reduce(rank[:, :, :], pair_gt[:, :, :].rearrange("p t (e j) -> p t e j", e=EXPERTS),
                                      AX.X, ALU.add))
            then(dve, v.tensor_scalar(mask, rank[:, :, :], 2.0, None, ALU.is_lt))

        def by_tile(row):
            return per_tile[:, row, :].unsqueeze(2).to_broadcast([P, NT, EXPERTS])

        r0 = Region()
        golden = r0("golden", [P, 8, NT, EXPERTS])
        router0 = r0("router0", [P, 2, EXPERTS])
        gu_w = r0("gu_w", [P, 2, 2, 2, F0])
        d_w = r0("d_w", [P, 2, 2, DM])
        silu = r0("silu", [P, 2, 512])
        h0 = r0("h0", [P, 2, 2, 512])
        M = {n: sem("moe0_" + n) for n in ["router", "lg", "tanh", "dist", "exp", "comb", "w0", "w1", "gu", "silu", "h", "dn",
                                           "acc", "ready", "used"]}

        def gate0_pe(pe):
            pe.wait_ge(L["xnT"], 4)
            pe.wait_ge(M["router"], 16)
            for t in range(NT):
                for c in range(2):
                    mm = nc.tensor.matmul(ps[:, 7, t * EXPERTS:(t + 1) * EXPERTS], xnT[:, c, t * P:(t + 1) * P],
                                          router0[:, c, :], start=(c == 0), stop=(c == 1))
            mm.then_inc(M["lg"], 1)

        def gate0_act(act):
            th, dist, w, fb = (golden[:, k, :, :] for k in range(4))
            act.wait_ge(M["ready"], 1)
            act.wait_ge(M["lg"], 1)
            lg = ps[:, 7, 0:NT * EXPERTS].rearrange("p (t e) -> p t e", t=NT)
            nc.scalar.activation(th, lg, ACT.Tanh, scale=halfrt[:, :]).then_inc(M["tanh"], 1)
            act.wait_ge(M["dist"], 1)
            nc.scalar.activation(w, dist, ACT.Exp, scale=-10.0).then_inc(M["exp"], 1)
            nc.scalar.activation(fb, dist, ACT.Exp, scale=-1.0 / 0.3).then_inc(M["exp"], 1)

        def gate0_dve(dve):
            v = nc.vector
            th, dist, w, fb, inh, zone, tmp, msk = (golden[:, k, :, :] for k in range(8))
            dve.wait_ge(ld_gate, 48)
            then(dve, v.reciprocal(temp[:, :], temp[:, :]))
            v.tensor_scalar(halfrt[:, :], temp[:, :], 0.5, None, ALU.mult).then_inc(M["ready"], 1)
            for t in range(NT):
                link(v.tensor_copy(before_all[:, t, :], before[:, :, :].rearrange("p e j -> p (e j)")))
            dve.wait_ge(M["tanh"], 1)
            then(dve, v.tensor_scalar(inh, th, 0.5, 0.5, ALU.mult, ALU.add))
            then(dve, v.tensor_scalar(tmp, inh, float(GOLDEN), None, ALU.subtract))
            v.scalar_tensor_tensor(dist, tmp, -1.0, tmp, ALU.mult, ALU.max).then_inc(M["dist"], 1)
            then(dve, v.tensor_scalar(zone, inh, float(LOWER), None, ALU.is_ge))
            then(dve, v.scalar_tensor_tensor(zone, inh, float(UPPER), zone, ALU.is_le, ALU.mult))
            dve.wait_ge(M["exp"], 2)
            then(dve, v.tensor_tensor(w, w, zone, ALU.mult))
            then(dve, v.tensor_reduce(per_tile[:, 0, :], w, AX.X, ALU.add))
            then(dve, v.tensor_scalar(per_tile[:, 1, :], per_tile[:, 0, :], 1e-8, None, ALU.is_lt))
            top2(dve, fb, msk)
            then(dve, v.tensor_tensor(fb, fb, msk, ALU.mult))
            then(dve, v.tensor_reduce(per_tile[:, 2, :], fb, AX.X, ALU.add))
            then(dve, v.tensor_scalar(per_tile[:, 2, :], per_tile[:, 2, :], 1e-8, None, ALU.max))
            then(dve, v.reciprocal(per_tile[:, 3, :], per_tile[:, 2, :]))
            then(dve, v.tensor_tensor(fb, fb, by_tile(3), ALU.mult))
            then(dve, v.tensor_tensor(fb, fb, by_tile(1), ALU.mult))
            then(dve, v.tensor_scalar(per_tile[:, 1, :], per_tile[:, 1, :], -1.0, 1.0, ALU.mult, ALU.add))
            then(dve, v.tensor_tensor(w, w, by_tile(1), ALU.mult))
            then(dve, v.tensor_tensor(w, w, fb, ALU.add))
            then(dve, v.tensor_reduce(per_tile[:, 2, :], w, AX.X, ALU.add))
            then(dve, v.tensor_scalar(per_tile[:, 2, :], per_tile[:, 2, :], 1e-8, None, ALU.max))
            then(dve, v.reciprocal(per_tile[:, 3, :], per_tile[:, 2, :]))
            then(dve, v.tensor_scalar(per_tile[:, 3, :], per_tile[:, 3, :], tg[:, 2:3], None, ALU.mult))
            then(dve, v.tensor_tensor(comb[:, :, :], w, by_tile(3), ALU.mult))

        def moe0_sp(sp):
            def load(e, slot):
                one = bass.ds(e, 1)
                for k, n in enumerate(["L0_ffn_Wg", "L0_ffn_Wu"]):
                    sp.dma_start(gu_w[:, slot, k, :, :], a[n][one, :, :].rearrange("o (k p) f -> p (o k) f", p=P)
                                 ).then_inc(M[f"w{slot}"], 16)
                sp.dma_start(d_w[:, slot, :, :], a["L0_ffn_Wd"][one, :, :].rearrange("o (k p) f -> p (o k) f", p=P)
                             ).then_inc(M[f"w{slot}"], 16)
            sp.wait_ge(S["X1"], NT)
            sp.dma_start(router0[:, :, :], a["L0_ffn_Wr"].rearrange("(k p) e -> p k e", p=P)).then_inc(M["router"], 16)
            for e in range(2):
                load(e, e)
            with sp.Fori(0, EXPERTS // 2 - 1) as i:
                for slot in range(2):
                    sp.wait_ge(M["dn"], 4 * i + 2 * slot + 4)
                    load(2 * i + slot + 2, slot)

        def moe0_pe(pe):
            def up(k, q, w_wait=None):
                slot, th = q // 2, q % 2
                if th == 0:
                    pe.wait_ge(M[f"w{slot}"], w_wait)
                for f in range(2):
                    pe.wait_ge(M["h"], 2 * k + f + 1)
                    for g in range(2):
                        for c in range(2):
                            mm = nc.tensor.matmul(ps[:, 2 * f + g, :], gu_w[:, slot, g, c, f * P:(f + 1) * P],
                                                  xnT[:, c, th * 512:(th + 1) * 512], start=(c == 0), stop=(c == 1))
                    mm.then_inc(M["gu"], 1)

            def down(k, q):
                slot, th = q // 2, q % 2
                pe.wait_ge(M["h"], 2 * k + 4)
                pe.wait_ge(M["acc"], 4 * k + 4)
                for t in range(4):
                    for f in range(2):
                        mm = nc.tensor.matmul(ps[:, 4 + 2 * th + t // 2, (t % 2) * 256:(t % 2) * 256 + 256],
                                              h0[:, th, f, t * P:(t + 1) * P], d_w[:, slot, f, :],
                                              start=(f == 0), stop=(f == 1))
                mm.then_inc(M["dn"], 1)

            def turn(i, last):
                for q in range(4):
                    if not (last and q == 3):
                        up(4 * i + q + 1, (q + 1) % 4, 48 * i + 48 * ((q + 1) // 4) + 48)
                    down(4 * i + q, q)

            pe.wait_ge(M["comb"], 1)
            pe.sem_inc(M["dn"], 2)
            up(0, 0, 48)
            with pe.Fori(0, EXPERTS // 2 - 1) as i:
                turn(i, False)
            turn(EXPERTS // 2 - 1, True)

        def moe0_act(act):
            with act.Fori(0, 2 * EXPERTS) as k:
                for f in range(2):
                    act.wait_ge(M["gu"], 2 * k + f + 1)
                    act.wait_ge(M["h"], 2 * k + f + 1)
                    nc.scalar.activation(silu[:, f, :], ps[:, 2 * f, :], ACT.Silu).then_inc(M["silu"], 1)

        def moe0_dve(dve):
            def hidden(k, q):
                for f in range(2):
                    dve.wait_ge(M["silu"], 2 * k + f + 1)
                    dve.wait_ge(M["dn"], k + 1)
                    nc.vector.tensor_tensor(h0[:, q % 2, f, :], silu[:, f, :], ps[:, 2 * f + 1, :],
                                            ALU.mult).then_inc(M["h"], 1)

            def add(i, q):
                th = q % 2
                dve.wait_ge(M["dn"], 4 * i + q + 3)
                dve.wait_ge(M["acc"], 8 + 16 * i + 4 * q - 4)
                for t in range(4):
                    tile = 4 * th + t
                    nc.vector.scalar_tensor_tensor(X[:, tile, :], ps[:, 4 + 2 * th + t // 2, (t % 2) * 256:(t % 2) * 256 + 256],
                                                   comb[:, tile, bass.ds(2 * i + q // 2, 1)], X[:, tile, :],
                                                   ALU.mult, ALU.add).then_inc(M["acc"], 1)

            def turn(i, last):
                for q in range(4):
                    if not (last and q == 3):
                        hidden(4 * i + q + 1, q + 1)
                    add(i, q)

            dve.sem_inc(M["h"], 2)
            dve.sem_inc(M["acc"], 8)
            nc.vector.memset(minushalf[:, :], -0.5).then_inc(M["comb"], 1)
            hidden(0, 0)
            with dve.Fori(0, EXPERTS // 2 - 1) as i:
                turn(i, False)
            turn(EXPERTS // 2 - 1, True)
            dve.wait_ge(M["acc"], 8 + 8 * EXPERTS)



        r1 = Region()
        wq = r1("wq", [P, 2, DM])
        wkv = r1("wkv", [P, 2 * DM])
        wout = r1("wout", [P, 2, DM])
        bout = r1("bout", [1, DM])
        wq_sw = r1("wq_sw", [P, 2, DM])
        wk_sw = r1("wk_sw", [P, DM])
        cos = r1("cos", [P, TOK])
        sin = r1("sin", [P, TOK])
        qa = r1("qa", [P, 3, HEADS, SEQ], BF16)
        ka = r1("ka", [P, 3, HEADS, SEQ], BF16)
        vv = r1("vv", [P, NT, DM])
        v_pad = r1("v_pad", [P, 2, 2, 4, 32])
        mx = r1("mx", [P, 2, 2, HEADS])
        minus_one = r1("minus_one", [3, SEQ], BF16)
        m_parts = r1("m_parts", [32, 3, SEQ], BF16)
        m_rest = r1("m_rest", [32, 2, SEQ])
        probs = r1("probs", [P, 4, 2, 2, SEQ])
        o_rows = r1("o_rows", [P, 8, SEQ])
        recip16 = r1("recip16", [P, 16, 1])
        rope_a = probs[:, 0, :, :, :].rearrange("p a b c -> p (a b c)")
        rope_b = probs[:, 1, :, :, :].rearrange("p a b c -> p (a b c)")
        parts = [r1("parts0", [P, 3, TOK], BF16), r1("parts1", [P, 3, TOK], BF16)]
        attn, attnT = xn, xnT
        parts_d = nc.dram_tensor("parts_d", [2, 3, DM, TOK], BF16, kind="Internal").ap()
        max_d = nc.dram_tensor("max_d", [BATCH, 3, HEADS, SEQ], BF16, kind="Internal").ap()
        GROUPS = HEADS // 4
        T = {n: sem("att_" + n) for n in ["ang", "red", "sin", "cos", "w", "sw", "proj", "rope", "split", "part", "sent0",
                                          "sent1", "v_ps", "v", "rows", "zero", "qk0", "qk1", "qk2", "A", "max", "mT", "mrow",
                                          "msent", "mput", "B", "exp", "vpad", "pv", "o", "oT", "attn", "aT_ps", "aT", "ones",
                                          "out", "X3", "setv"]}

        def att_sp_weights(sp):
            sp.wait_ge(M["acc"], 8 + 8 * EXPERTS)
            sp.dma_start(wq[:, :, :], a["L1_xattn_Wq"].rearrange("(k p) n -> p k n", p=P)).then_inc(T["w"], 16)
            sp.dma_start(wkv[:, :], a["L1_xattn_Wkv"]).then_inc(T["w"], 16)
            sp.dma_start(wout[:, :, :], a["L1_xattn_Wout"].rearrange("(k p) n -> p k n", p=P)).then_inc(T["w"], 16)
            sp.dma_start(bout[:, :], a["L1_xattn_bout"].unsqueeze(0)).then_inc(T["w"], 16)

        def att_sp(sp):
            att_sp_weights(sp)
            sp.wait_ge(T["zero"], 1)
            for slot in range(3):
                sp.dma_start(ka[72:75, slot, :, :], minus_one[:, :].unsqueeze(1).to_broadcast([3, HEADS, SEQ])
                             ).then_inc(T["ones"], 16)
            for un in range(4):
                sp.wait_ge(T["part"], 3 * un + 3)
                dst = parts_d[1 - un // 2, :, (un % 2) * P:(un % 2 + 1) * P, :].rearrange("i p t -> p i t")
                sp.dma_start(dst, parts[un % 2]).then_inc(T[f"sent{un % 2}"], 16)
            sp.wait_ge(T["sent0"], 32)
            sp.wait_ge(T["sent1"], 32)

            def load(b):
                for k, rows_of in enumerate([qa, ka]):
                    for i in range(3):
                        for j in range(3):
                            r = (3 * i + j) * HD
                            src = parts_d[k, j if k else i, :, b * SEQ:(b + 1) * SEQ].rearrange("(h d) t -> d h t", d=HD)
                            sp.dma_start(rows_of[r:r + HD, b % 3, :, :], src).then_inc(T[f"qk{b % 3}"], 16)

            def put_max(b):
                sp.wait_ge(T["mrow"], b + 1)
                sp.dma_start(max_d[b].rearrange("i h t -> h i t"), m_parts).then_inc(T["msent"], 16)
                sp.wait_ge(T["msent"], 16 * (b + 1))
                sp.dma_start(qa[72:75, b % 3, :, :], max_d[b]).then_inc(T["mput"], 16)

            load(0)
            load(1)
            put_max(0)
            for b in range(1, BATCH):
                if b + 1 < BATCH:
                    if b >= 2:
                        sp.wait_ge(T["B"], 2 * GROUPS * (b - 1))
                    load(b + 1)
                put_max(b)

        def att_pe(pe):
            pe.wait_ge(ld_pos, 16)
            pe.wait_ge(L["xnT"], 8)
            for th in range(2):
                mm = nc.tensor.matmul(ps[:, th, :], freq[:, :], posT[:, th * 512:(th + 1) * 512], start=True, stop=True)
            mm.then_inc(T["ang"], 1)
            pe.wait_ge(T["sw"], 2)
            for un in range(4):
                base = 4 * (1 - un % 2)
                c = un % 2
                if un == 1:
                    pe.wait_ge(T["red"], 1)
                if un == 2:
                    pe.wait_ge(L["xnT"], 8)
                if un >= 2:
                    pe.wait_ge(T["rope"], 2 * un - 2)
                for k, w in enumerate([wkv[:, c * P:(c + 1) * P], wk_sw[:, c * P:(c + 1) * P]] if un < 2 else
                                      [wq[:, :, c * P:(c + 1) * P], wq_sw[:, :, c * P:(c + 1) * P]]):
                    for th in range(2):
                        o = ps[:, base + 2 * k + th, :]
                        cut = slice(th * 512, (th + 1) * 512)
                        if un < 2:
                            mm = nc.tensor.matmul(o, w, ctxT[:, cut], start=True, stop=True)
                        else:
                            for kk in range(2):
                                mm = nc.tensor.matmul(o, w[:, kk, :], xnT[:, kk, cut], start=(kk == 0), stop=(kk == 1))
                    mm.then_inc(T["proj"], 1)
            pe.wait_ge(T["rope"], 6)
            for t in range(NT):
                mm = nc.tensor.matmul(ps[:, 4 + t // 2, (t % 2) * 256:(t % 2) * 256 + 256], ctxT[:, t * P:(t + 1) * P],
                                      wkv[:, DM:2 * DM], start=True, stop=True)
                if t % 2:
                    mm.then_inc(T["v_ps"], 1)
            pe.wait_ge(T["rope"], 8)
            pe.wait_ge(T["v"], 4)

            def A(b, hd, par, n):
                pe.wait_ge(T["max"], n + 1)
                for qt in range(2):
                    mm = nc.tensor.matmul(ps[:, par, qt * 256:(qt + 1) * 256],
                                          one(qa[0:72, b % 3, :, qt * P:(qt + 1) * P], hd),
                                          one(ka[0:72, b % 3, :, :], hd), start=True, stop=True)
                mm.then_inc(T["A"], 1)

            def B(b, hd, pair, n):
                pe.wait_ge(T["exp"], n + 1)
                for j in range(2):
                    for kc in range(2):
                        mm = nc.tensor.matmul(ps[:, 2 + 2 * pair + j, kc * 256:(kc + 1) * 256],
                                              one(ka[0:75, b % 3, :, kc * P:(kc + 1) * P], hd + j),
                                              one(qa[0:75, b % 3, :, :], hd + j), start=True, stop=True)
                mm.then_inc(T["B"], 1)

            def PV(s, G):
                pe.wait_ge(T["exp"], 2 * G + 2 + 2)
                pe.wait_ge(T["vpad"], G + 1)
                pe.wait_ge(T["o"], G + 1)
                for kc in range(2):
                    for j in range(4):
                        mm = nc.tensor.matmul(ps[32 * j:32 * j + 32, 6, 0:256], v_pad[:, s, kc, j, :],
                                              probs[:, 2 * s + j // 2, j % 2, kc, :], start=(kc == 0), stop=(kc == 1),
                                              skip_group_check=True)
                mm.then_inc(T["pv"], 1)

            def max_rows(b):
                pe.wait_ge(T["max"], HEADS * (b + 1) + 2)
                for qt in range(2):
                    mm = nc.tensor.transpose(ps[0:32, 7, qt * P:(qt + 1) * P], mx[:, b % 2, qt, :], ident[:, :])
                mm.then_inc(T["mT"], 1)

            def turn(b, i, last):
                for s in range(2):
                    G = 8 * b + 2 * i + s
                    g = 2 * i + s
                    for p in range(2):
                        if b + 1 < BATCH:
                            for j in range(2):
                                A(b + 1, 4 * g + 2 * p + j, j, HEADS * (b + 1) + 4 * g + 2 * p + j)
                        if not (last and s == 1):
                            B(b, 4 * g + 4 + 2 * p, p, 2 * G + 2 + p)
                    PV(s, G)

            pe.sem_inc(T["pv"], 2)
            pe.wait_ge(T["qk0"], 16 * 18)
            pe.wait_ge(T["ones"], 48)
            with pe.Fori(0, HEADS // 2) as i:
                for j in range(2):
                    A(0, 2 * i + j, j, 2 * i + j)
            max_rows(0)
            for b in range(BATCH):
                pe.wait_ge(T["mput"], 16 * (b + 1))
                for p in range(2):
                    B(b, 2 * p, p, 16 * b + p)
                if b + 1 < BATCH:
                    pe.wait_ge(T[f"qk{(b + 1) % 3}"], 16 * 18 * ((b + 1) // 3 + 1))
                with pe.Fori(0, GROUPS // 2 - 1) as i:
                    turn(b, i, False)
                turn(b, GROUPS // 2 - 1, True)
                if b + 1 < BATCH:
                    max_rows(b + 1)
                for gg in range(GROUPS // 2):
                    pe.wait_ge(T["o"], 8 * b + 2 * gg + 2 + 1)
                    n = 4 * b + gg
                    if gg == 0:
                        if b + 1 < BATCH:
                            pe.wait_ge(T["mrow"], b + 2)
                    if n:
                        pe.wait_ge(T["attn"], n)
                    for qt in range(2):
                        for k in range(2):
                            mm = nc.tensor.transpose(ps[:, 7, (2 * qt + k) * P:(2 * qt + k + 1) * P],
                                                     o_rows[:, 2 * gg + k, qt * P:(qt + 1) * P], ident[:, :])
                    mm.then_inc(T["oT"], 1)
            for th in range(2):
                for c in range(2):
                    pe.wait_ge(T["attn"], 16)
                    for q in range(4):
                        mm = nc.tensor.transpose(ps[:, 2 * th + c, q * P:(q + 1) * P], attn[:, 4 * th + q, c * P:(c + 1) * P],
                                                 ident[:, :])
                    mm.then_inc(T["aT_ps"], 1)
            for t in range(NT):
                pe.wait_ge(T["aT"], 2 * (t // 4) + 2)
                o = ps[:, 4 + (t // 2) % 2 + 2 * (t // 4), (t % 2) * 256:(t % 2) * 256 + 256]
                for c in range(2):
                    nc.tensor.matmul(o, attnT[:, c, t * P:(t + 1) * P], wout[:, c, :], start=(c == 0), stop=False)
                mm = nc.tensor.matmul(o, ones_row[:, :], bout[:, :], start=False, stop=True)
                if t % 2:
                    mm.then_inc(T["out"], 1)

        def one(view, hd):
            if isinstance(hd, int):
                return view[:, hd, :]
            return view[:, bass.ds(hd, 1), :].rearrange("r o n -> r (o n)")

        def att_act(act):
            act.wait_ge(T["red"], 5)
            nc.scalar.activation(sin[:, :], cos[:, :], ACT.Sin).then_inc(T["sin"], 1)
            nc.scalar.activation(rope_b, cos[:, :], ACT.Abs).then_inc(T["sin"], 1)
            act.wait_ge(T["red"], 6)
            nc.scalar.activation(cos[:, :], rope_b, ACT.Sin).then_inc(T["cos"], 1)
            for k in range(4):
                act.wait_ge(T["v_ps"], k + 1)
                nc.scalar.copy(vv[:, 2 * k:2 * k + 2, :].rearrange("p a b -> p (a b)"), ps[:, 4 + k, :]).then_inc(T["v"], 1)
            act.sem_inc(T["exp"], 2)
            act.sem_inc(T["o"], 1)

            def exps(s, G):
                for p in range(2):
                    act.wait_ge(T["B"], 2 * G + p + 1)
                    act.wait_ge(T["pv"], G + 1)
                    nc.scalar.activation(probs[:, 2 * s + p, :, :, :].rearrange("p a b c -> p (a b c)"),
                                         ps[:, 2 + 2 * p:4 + 2 * p, :].rearrange("p a b -> p (a b)"), ACT.Exp,
                                         scale=float(1.0 / np.sqrt(np.float32(HD)))).then_inc(T["exp"], 1)

            def evac(g, G):
                act.wait_ge(T["pv"], G + 1 + 2)
                nc.scalar.copy(o_rows[:, bass.ds(g, 1), :].rearrange("p a b -> p (a b)"), ps[:, 6, 0:256]
                               ).then_inc(T["o"], 1)

            def turn(b, i, last):
                for s in range(2):
                    if not (last and s == 1):
                        exps((s + 1) % 2, 8 * b + 2 * i + s + 1)
                    evac(2 * i + s, 8 * b + 2 * i + s)

            for b in range(BATCH):
                exps(0, 8 * b)
                if b:
                    act.wait_ge(T["oT"], 4 * b)
                with act.Fori(0, GROUPS // 2 - 1) as i:
                    turn(b, i, False)
                turn(b, GROUPS // 2 - 1, True)
            for k in range(4):
                act.wait_ge(T["aT_ps"], k + 1)
                th, c = k // 2, k % 2
                nc.scalar.copy(attnT[:, c, th * 512:(th + 1) * 512], ps[:, k, :]).then_inc(T["aT"], 1)

        def att_dve(dve):
            v = nc.vector
            v.memset(minus_one[:, :], -1.0).then_inc(T["zero"], 1)
            dve.wait_ge(T["w"], 64)
            for w, sw in ((wkv[:, 0:DM], wk_sw[:, :]), (wq.rearrange("p k n -> p (k n)"), wq_sw.rearrange("p k n -> p (k n)"))):
                src = w.rearrange("p (n two) -> p n two", two=2)
                dst = sw.rearrange("p (n two) -> p n two", two=2)
                link(v.tensor_scalar(dst[:, :, 0:1], src[:, :, 1:2], -1.0, None, ALU.mult))
                link(v.tensor_copy(dst[:, :, 1:2], src[:, :, 0:1]))
                dve.wait_ge(dve_order, step_count[0])
                dve.sem_inc(T["sw"], 1)
            dve.wait_ge(T["ang"], 1)
            ang = ps[:, 0:2, :].rearrange("p a b -> p (a b)")
            v.tensor_copy(rope_a, ang).then_inc(T["red"], 1)
            dve.wait_ge(T["red"], 1)
            v.tensor_scalar(rope_b, rope_a, float(1.0 / TWO_PI), ROUND, ALU.mult, ALU.add).then_inc(T["red"], 1)
            dve.wait_ge(T["red"], 2)
            v.tensor_scalar(rope_b, rope_b, ROUND, None, ALU.subtract).then_inc(T["red"], 1)
            dve.wait_ge(T["red"], 3)
            v.scalar_tensor_tensor(rope_a, rope_b, -6.28125, rope_a, ALU.mult, ALU.add).then_inc(T["red"], 1)
            dve.wait_ge(T["red"], 4)
            then(dve, v.scalar_tensor_tensor(rope_a, rope_b, -float(TWO_PI - 6.28125), rope_a, ALU.mult, ALU.add))
            v.tensor_scalar(cos[:, :], rope_a, 3.1415925, -3.1415925, ALU.min, ALU.max).then_inc(T["red"], 1)
            dve.wait_ge(T["sin"], 2)
            v.tensor_scalar(rope_b, rope_b, -1.0, float(np.pi / 2), ALU.mult, ALU.add).then_inc(T["red"], 1)
            dve.wait_ge(T["cos"], 1)
            for un in range(4):
                base = 4 * (1 - un % 2)
                pr = parts[un % 2]
                dve.wait_ge(T["proj"], 2 * un + 1)
                v.tensor_tensor(
                    rope_a, ps[:, base:base + 2, :].rearrange("p a b -> p (a b)"), cos[:, :], ALU.mult).then_inc(T["rope"], 1)
                dve.wait_ge(T["proj"], 2 * un + 2)
                v.tensor_tensor(rope_b, ps[:, base + 2:base + 4, :].rearrange("p a b -> p (a b)"), sin[:, :],
                                ALU.mult).then_inc(T["rope"], 1)
                dve.wait_ge(T["rope"], 2 * un + 2)
                then(dve, v.tensor_tensor(rope_a, rope_a, rope_b, ALU.add))
                if un >= 2:
                    dve.wait_ge(T[f"sent{un % 2}"], 16)
                v.tensor_copy(pr[:, 0, :], rope_a).then_inc(T["part"], 1)
                dve.wait_ge(T["part"], 3 * un + 1)
                then(dve, v.tensor_tensor(rope_b, rope_a, pr[:, 0, :], ALU.subtract))
                v.tensor_copy(pr[:, 1, :], rope_b).then_inc(T["part"], 1)
                dve.wait_ge(T["part"], 3 * un + 2)
                v.tensor_tensor(pr[:, 2, :], rope_b, pr[:, 1, :], ALU.subtract).then_inc(T["part"], 1)
                dve.wait_ge(T["part"], 3 * un + 3)
            dve.sem_inc(T["max"], 2)

            def head_max(slot, hd, par, n):
                dve.wait_ge(T["A"], n + 1)
                v.tensor_reduce(mx[:, slot, :, bass.ds(hd, 1)].rearrange("p a o -> p (a o)"),
                                ps[:, par, :].rearrange("p (a k) -> p a k", a=2), AX.X, ALU.max).then_inc(T["max"], 1)

            def max_split(b):
                dve.wait_ge(T["mT"], b + 1)
                if b:
                    dve.wait_ge(T["msent"], 16 * b)
                then(dve, v.tensor_copy(m_rest[:, 0, :], ps[0:32, 7, 0:256]))
                then(dve, v.tensor_copy(m_parts[:, 0, :], m_rest[:, 0, :]))
                then(dve, v.tensor_tensor(m_rest[:, 1, :], m_rest[:, 0, :], m_parts[:, 0, :], ALU.subtract))
                then(dve, v.tensor_copy(m_parts[:, 1, :], m_rest[:, 1, :]))
                v.tensor_tensor(m_parts[:, 2, :], m_rest[:, 1, :], m_parts[:, 1, :], ALU.subtract).then_inc(T["mrow"], 1)

            with dve.Fori(0, HEADS // 2) as i:
                for j in range(2):
                    head_max(0, 2 * i + j, j, 2 * i + j)
            max_split(0)
            for b in range(BATCH):
                if b + 1 < BATCH:
                    with dve.Fori(0, HEADS // 2) as i:
                        for j in range(2):
                            head_max((b + 1) % 2, 2 * i + j, j, HEADS * (b + 1) + 2 * i + j)
                    max_split(b + 1)
                for gg in range(GROUPS // 2):
                    dve.wait_ge(T["oT"], 4 * b + gg + 1)
                    o = ps[:, 7, :].rearrange("p (m c) -> p m c", c=32)
                    then(dve, v.reciprocal(recip16, o[:, :, HD:HD + 1]))
                    for qt in range(2):
                        dst = attn[:, 2 * b + qt, 64 * gg:64 * gg + 64].rearrange("p (m c) -> p m c", c=HD)
                        ins = v.tensor_tensor(dst, o[:, 8 * qt:8 * qt + 8, 0:HD],
                                              recip16[:, 8 * qt:8 * qt + 8, :].to_broadcast([P, 8, HD]), ALU.mult)
                        if qt == 0:
                            link(ins)
                    ins.then_inc(T["attn"], 1)
            for t in range(NT):
                dve.wait_ge(T["out"], t // 2 + 1)
                o = ps[:, 4 + (t // 2) % 2 + 2 * (t // 4), (t % 2) * 256:(t % 2) * 256 + 256]
                v.scalar_tensor_tensor(X[:, t, :], o, tg[:, 1:2], X[:, t, :], ALU.mult, ALU.add).then_inc(T["X3"], 1)
            dve.wait_ge(T["X3"], NT)

        def att_pool(pool):
            g = nc.gpsimd
            pool.wait_ge(T["zero"], 1)
            g.memset(v_pad.rearrange("p a b c d -> p (a b c d)"), 0.0).then_inc(T["setv"], 1)
            pool.wait_ge(T["setv"], 1)
            g.memset(v_pad[:, :, :, :, HD:HD + 1].rearrange("p a b c d -> p (a b c) d"), 1.0).then_inc(T["setv"], 1)
            pool.wait_ge(T["setv"], 2)
            pool.wait_ge(T["v"], 4)
            for b in range(BATCH):
                with pool.Fori(0, GROUPS // 2) as i:
                    for s in range(2):
                        pool.wait_ge(T["pv"], 8 * b + 2 * i + s + 1)
                        src = vv[:, 2 * b:2 * b + 2, bass.ds(32 * (2 * i + s), 32)]
                        for kc in range(2):
                            ins = g.tensor_copy(v_pad[:, s, kc, :, 0:HD], src[:, kc, :].rearrange("p (h d) -> p h d", d=HD))
                            if kc == 0:
                                ins.then_inc(T["setv"], 1)
                        ins.then_inc(T["vpad"], 1)


        r2 = Region()
        w1_sb = r2("w1_sb", [P, EXPERTS, 2, F1])
        w2_sb = r2("w2_sb", [P, EXPERTS, F1 // P, DM])
        router1 = r2("router1", [P, 2, EXPERTS])
        gate_b = r2("gate_b", [1, EXPERTS])
        b2_sb = r2("b2_sb", [EXPERTS, DM])
        b1_rows = r2("b1_rows", [EXPERTS * F1 // P, P])
        b1_sb = r2("b1_sb", [P, EXPERTS, F1 // P])
        lower = r2("lower", [P, P])
        ones = r2("ones", [P, P])
        tile_no = r2("tile_no", [1, SLOT_TILES])
        combT = r2("combT", [EXPERTS, TOK])
        soft = r2("soft", [P, 2, NT, EXPERTS])
        chosen = r2("chosen", [P, NT + 1, EXPERTS])
        place = r2("place", [P, NT + 1, EXPERTS])
        masked = r2("masked", [P, 2, NT, EXPERTS])
        hit = r2("hit", [P, 2, NT, EXPERTS])
        tiles = r2("tiles", [P, EXPERTS])
        in_front = r2("in_front", [P, EXPERTS, EXPERTS])
        first = r2("first", [P, EXPERTS])
        base = r2("base", [P, EXPERTS])
        slot_f = r2("slot_f", [P, 2, NT])
        slot_i = r2("slot_i", [P, 2, NT], mybir.dt.int32)
        pair_w = r2("pair_w", [P, 2, NT])
        reached = r2("reached", [1, SLOT_TILES, EXPERTS])
        owner_f = r2("owner_f", [1, SLOT_TILES])
        owner = r2("owner", [1, SLOT_TILES], mybir.dt.int32)
        xt_in = r2("xt_in", [P, DM])
        xt = r2("xt", [P, 2, P])
        pre = r2("pre", [P, F1])
        h1 = r2("h1", [P, F1 // P, P])
        y_sb = r2("y_sb", [P, DM])
        blank = sb("blank", [P, DM])
        got = [xn, xnT.rearrange("p k n -> p (k n)").rearrange("p (t d) -> p t d", t=NT)]
        slots_d = nc.dram_tensor("slots_d", [SLOT_TILES * P, DM], F32, kind="Internal").ap()
        y_d = nc.dram_tensor("y_d", [SLOT_TILES * P, DM], F32, kind="Internal").ap()
        NONE = 4096.0
        HF = F1 // P
        N = {n: sem("moe1_" + n) for n in ["small", "lg", "sub", "exp", "comb", "cT_ps", "cT", "bias", "acc", "blank",
                                           "blanked", "b1_ps", "b1", "chosen", "place_ps", "slots", "owner", "scattered",
                                           "w_ready", "xin", "xt_ps", "xt", "up", "pre", "hT", "hb", "h", "dn", "y",
                                           "y_out"] + [f"w{e}" for e in range(EXPERTS)] + [f"got{t}" for t in range(NT)]}

        def moe1_sp(sp):
            sp.wait_ge(T["X3"], NT)
            sp.dma_start(router1[:, :, :], a["L1_ffn_gate_w"].rearrange("(k p) e -> p k e", p=P)).then_inc(N["small"], 16)
            sp.dma_start(gate_b[:, :], a["L1_ffn_gate_b"].unsqueeze(0)).then_inc(N["small"], 16)
            sp.dma_start(b2_sb[:, :], a["L1_ffn_b2"]).then_inc(N["small"], 16)
            sp.dma_start(b1_rows[:, :], a["L1_ffn_b1"].rearrange("e (f p) -> (e f) p", p=P)).then_inc(N["small"], 16)
            sp.dma_start(lower[:, :], a["lower"]).then_inc(N["small"], 16)
            sp.dma_start(tile_no[:, :], a["tile_no"]).then_inc(N["small"], 16)
            for e in range(EXPERTS):
                sp.dma_start(w1_sb[:, e, :, :], a["L1_ffn_w1"][e].rearrange("(k p) f -> p k f", p=P)
                             ).then_inc(N[f"w{e}"], 16)
                sp.dma_start(w2_sb[:, e, :, :], a["L1_ffn_w2"][e].rearrange("(k p) f -> p k f", p=P)
                             ).then_inc(N[f"w{e}"], 16)
            for e in range(EXPERTS):
                sp.wait_ge(N[f"w{e}"], 32)
                sp.sem_inc(N["w_ready"], 1)
            sp.sem_inc(N["w_ready"], SLOT_TILES - EXPERTS)

        def gate1_pe(pe):
            pe.wait_ge(L["xnT"], 12)
            pe.wait_ge(N["small"], 96)
            for t in range(NT):
                o = ps[:, 7, t * EXPERTS:(t + 1) * EXPERTS]
                for c in range(2):
                    nc.tensor.matmul(o, xnT[:, c, t * P:(t + 1) * P], router1[:, c, :], start=(c == 0), stop=False)
                mm = nc.tensor.matmul(o, ones_row[:, :], gate_b[:, :], start=False, stop=True)
            mm.then_inc(N["lg"], 1)
            nc.tensor.transpose(ps[:, 6, 128:192], b1_rows[:, :], ident[0:64, 0:64]).then_inc(N["b1_ps"], 1)
            pe.wait_ge(N["chosen"], 2)
            nc.tensor.matmul(ps[:, 5, 0:(NT + 1) * EXPERTS], lower[:, :], chosen[:, :, :].rearrange("p t e -> p (t e)"),
                             start=True, stop=False, skip_group_check=True)
            for t in range(NT):
                mm = nc.tensor.matmul(ps[:, 5, (t + 1) * EXPERTS:(NT + 1) * EXPERTS].rearrange("p (t e) -> p t e", e=EXPERTS),
                                      ones[:, :], chosen[:, t:t + 1, :].to_broadcast([P, NT - t, EXPERTS]),
                                      start=False, stop=(t == NT - 1), skip_group_check=True)
            mm.then_inc(N["place_ps"], 1)

        def gate1_act(act):
            act.wait_ge(N["sub"], 1)
            nc.scalar.activation(soft[:, 1, :, :], soft[:, 0, :, :], ACT.Exp).then_inc(N["exp"], 1)

        def gate1_dve(dve):
            v = nc.vector
            lg, ex = (soft[:, k, :, :] for k in range(2))
            msk = chosen[:, 0:NT, :]
            v.memset(ones[:, :], 1.0).then_inc(N["chosen"], 1)
            link(v.memset(chosen[:, NT, :], 0.0))
            dve.wait_ge(N["lg"], 1)
            then(dve, v.tensor_copy(lg, ps[:, 7, 0:NT * EXPERTS].rearrange("p (t e) -> p t e", t=NT)))
            then(dve, v.tensor_reduce(per_tile[:, 0, :], lg, AX.X, ALU.max))
            v.tensor_tensor(lg, lg, by_tile(0), ALU.subtract).then_inc(N["sub"], 1)
            dve.wait_ge(N["exp"], 1)
            then(dve, v.tensor_reduce(per_tile[:, 0, :], ex, AX.X, ALU.add))
            then(dve, v.reciprocal(per_tile[:, 1, :], per_tile[:, 0, :]))
            then(dve, v.tensor_tensor(ex, ex, by_tile(1), ALU.mult))
            top2(dve, ex, msk)
            dve.sem_inc(N["chosen"], 1)
            then(dve, v.tensor_tensor(ex, ex, msk, ALU.mult))
            then(dve, v.tensor_reduce(per_tile[:, 2, :], ex, AX.X, ALU.add))
            then(dve, v.reciprocal(per_tile[:, 3, :], per_tile[:, 2, :]))
            then(dve, v.tensor_scalar(per_tile[:, 3, :], per_tile[:, 3, :], tg[:, 3:4], None, ALU.mult))
            link(v.tensor_tensor(comb[:, :, :], ex, by_tile(3), ALU.mult))
            dve.wait_ge(N["place_ps"], 1)
            then(dve, v.tensor_copy(place[:, :, :], ps[:, 5, 0:(NT + 1) * EXPERTS].rearrange("p (t e) -> p t e", e=EXPERTS)))
            then(dve, v.tensor_scalar(tiles[:, :], place[:, NT, :], 1.0 / P, 63.5 / P, ALU.mult, ALU.add))
            then(dve, v.tensor_scalar(tiles[:, :], tiles[:, :], ROUND, None, ALU.add))
            then(dve, v.tensor_scalar(tiles[:, :], tiles[:, :], ROUND, 1.0, ALU.subtract, ALU.max))
            then(dve, v.tensor_tensor(in_front[:, :, :], before[:, :, :],
                                      tiles[:, :].unsqueeze(1).to_broadcast([P, EXPERTS, EXPERTS]), ALU.mult))
            then(dve, v.tensor_reduce(first[:, :], in_front[:, :, :], AX.X, ALU.add))
            then(dve, v.tensor_scalar(base[:, :], first[:, :], float(P), None, ALU.mult))
            then(dve, v.tensor_tensor(place[:, 0:NT, :], place[:, 0:NT, :],
                                      base[:, :].unsqueeze(1).to_broadcast([P, NT, EXPERTS]), ALU.add))
            link(v.scalar_tensor_tensor(masked[:, 0, :, :], place[:, 0:NT, :], NONE, msk, ALU.subtract, ALU.mult))
            then(dve, v.tensor_tensor(masked[:, 1, :, :], place[:, 0:NT, :], msk, ALU.mult))
            link(v.tensor_reduce(slot_f[:, 0, :], masked[:, 0, :, :], AX.X, ALU.min))
            then(dve, v.tensor_reduce(slot_f[:, 1, :], masked[:, 1, :, :], AX.X, ALU.max))
            link(v.tensor_scalar(slot_i[:, 0, :], slot_f[:, 0, :], NONE, None, ALU.add))
            then(dve, v.tensor_copy(slot_i[:, 1, :], slot_f[:, 1, :]))
            dve.sem_inc(N["slots"], 1)
            then(dve, v.tensor_tensor(reached[:, :, :], first[0:1, :].unsqueeze(1).to_broadcast([1, SLOT_TILES, EXPERTS]),
                                      tile_no[:, :].unsqueeze(2).to_broadcast([1, SLOT_TILES, EXPERTS]), ALU.is_le))
            then(dve, v.tensor_reduce(owner_f[:, :], reached[:, :, :], AX.X, ALU.add))
            then(dve, v.tensor_scalar(owner[:, :], owner_f[:, :], -1.0, None, ALU.add))
            dve.sem_inc(N["owner"], 1)
            for k in range(2):
                link(v.tensor_tensor(hit[:, k, :, :], masked[:, k, :, :],
                                     slot_f[:, k, :].unsqueeze(2).to_broadcast([P, NT, EXPERTS]), ALU.is_equal))
            dve.wait_ge(dve_order, step_count[0])
            for k in range(2):
                link(v.tensor_tensor(hit[:, k, :, :], hit[:, k, :, :], comb[:, :, :], ALU.mult))
            dve.wait_ge(dve_order, step_count[0])
            for k in range(2):
                link(v.tensor_reduce(pair_w[:, k, :], hit[:, k, :, :], AX.X, ALU.add))
            dve.wait_ge(N["b1_ps"], 1)
            link(v.tensor_copy(b1_sb[:, :, :].rearrange("p e f -> p (e f)"), ps[:, 6, 128:192]))
            dve.wait_ge(dve_order, step_count[0])
            dve.sem_inc(N["comb"], 1)

        def bias_pe(pe):
            pe.wait_ge(N["comb"], 1)
            for t in range(NT):
                mm = nc.tensor.transpose(ps[0:EXPERTS, 4 + t // 4, (t % 4) * P:(t % 4 + 1) * P], comb[:, t, :], ident[:, :])
            mm.then_inc(N["cT_ps"], 1)
            pe.wait_ge(N["cT"], 2)
            for t in range(NT):
                mm = nc.tensor.matmul(ps[:, 4 + t // 2, (t % 2) * 256:(t % 2) * 256 + 256], combT[:, t * P:(t + 1) * P],
                                      b2_sb[:, :], start=True, stop=True)
            mm.then_inc(N["bias"], 1)

        def bias_dve(dve):
            dve.wait_ge(N["bias"], 1)
            for t in range(NT):
                nc.vector.tensor_tensor(X[:, t, :], X[:, t, :], ps[:, 4 + t // 2, (t % 2) * 256:(t % 2) * 256 + 256],
                                        ALU.add).then_inc(N["acc"], 1)

        def bias_act(act):
            act.wait_ge(N["cT_ps"], 1)
            for k in range(2):
                nc.scalar.copy(combT[:, k * 512:(k + 1) * 512], ps[0:EXPERTS, 4 + k, :]).then_inc(N["cT"], 1)

        def moe1_pool(pool):
            pool.wait_ge(N["blanked"], 16)
            pool.wait_ge(N["slots"], 1)
            for t in range(NT):
                for k in range(2):
                    nc.gpsimd.indirect_dma_start(slots_d[:, :], bass.IndirectOffsetOnAxis(ap=slot_i[:, k, t:t + 1], axis=0),
                                                 xn[:, t, :], None).then_inc(N["scattered"], 16)
            pool.wait_ge(N["y_out"], 16 * SLOT_TILES)
            pool.wait_ge(N["scattered"], 16 * 2 * NT)
            for t in range(NT):
                for k in range(2):
                    nc.gpsimd.indirect_dma_start(got[k][:, t, :], None, y_d[:, :],
                                                 bass.IndirectOffsetOnAxis(ap=slot_i[:, k, t:t + 1], axis=0)
                                                 ).then_inc(N[f"got{t}"], 16)

        def expert_of(tile, engine):
            return nc.values_load(owner[:, tile:tile + 1] if isinstance(tile, int) else owner[:, bass.ds(tile, 1)],
                                  engines=[engine], min_val=0, max_val=EXPERTS - 1,
                                  skip_runtime_bounds_check_because="a count of the experts, from 1, less one")

        def moe1_pe(pe):
            def rows_in(i):
                pe.wait_ge(N["xin"], 16 * i + 16)
                for c in range(2):
                    mm = nc.tensor.transpose(ps[:, 6, c * P:(c + 1) * P], xt_in[:, c * P:(c + 1) * P], ident[:, :])
                mm.then_inc(N["xt_ps"], 1)

            def up(i, e):
                pe.wait_ge(N["w_ready"], i + 1)
                pe.wait_ge(N["xt"], i + 1)
                for half in range(2):
                    for c in range(2):
                        mm = nc.tensor.matmul(ps[:, half, :], xt[:, c, :],
                                              w1_sb[:, bass.ds(e, 1), c, half * 512:(half + 1) * 512].rearrange("p o n -> p (o n)"),
                                              start=(c == 0), stop=(c == 1))
                    mm.then_inc(N["up"], 1)

            def turn_hidden(i):
                for half in range(2):
                    pe.wait_ge(N["pre"], 2 * i + half + 1)
                    for q in range(4):
                        f = 4 * half + q
                        mm = nc.tensor.transpose(ps[:, 2 + half, q * P:(q + 1) * P], pre[:, f * P:(f + 1) * P], ident[:, :])
                    mm.then_inc(N["hT"], 1)

            def down(i, e):
                pe.wait_ge(N["h"], 2 * i + 2)
                for f in range(HF):
                    mm = nc.tensor.matmul(ps[:, 4, 0:DM], h1[:, f, :],
                                          w2_sb[:, bass.ds(e, 1), f, :].rearrange("p o n -> p (o n)"),
                                          start=(f == 0), stop=(f == HF - 1))
                mm.then_inc(N["dn"], 1)

            pe.wait_ge(N["owner"], 1)
            pe.wait_ge(N["acc"], NT)
            rows_in(0)
            up(0, expert_of(0, mybir.EngineType.PE))
            rows_in(1)
            turn_hidden(0)

            def turn(i, ups, rows):
                e, e_next = expert_of(i, mybir.EngineType.PE), expert_of(i + 1, mybir.EngineType.PE) if ups else None
                if ups:
                    up(i + 1, e_next)
                if rows:
                    rows_in(i + 2)
                down(i, e)
                if ups:
                    turn_hidden(i + 1)

            with pe.Fori(0, SLOT_TILES - 2) as i:
                turn(i, True, True)
            turn(SLOT_TILES - 2, True, False)
            turn(SLOT_TILES - 1, False, False)

        def moe1_act(act):
            def load_rows(i):
                src = slots_d[i * P:(i + 1) * P, :] if isinstance(i, int) else slots_d[bass.ds(i * P, P), :]
                act.dma_start(xt_in[:, :], src).then_inc(N["xin"], 16)

            def copy_pre(i):
                for half in range(2):
                    act.wait_ge(N["up"], 2 * i + half + 1)
                    nc.scalar.copy(pre[:, half * 512:(half + 1) * 512], ps[:, half, :]).then_inc(N["pre"], 1)

            def gelu(i):
                for half in range(2):
                    act.wait_ge(N["hb"], 2 * i + half + 1)
                    part = h1[:, 4 * half:4 * half + 4, :]
                    nc.scalar.activation(part, part, ACT.Gelu_apprx_tanh).then_inc(N["h"], 1)

            def store(i):
                act.wait_ge(N["y"], i + 1)
                dst = y_d[i * P:(i + 1) * P, :] if isinstance(i, int) else y_d[bass.ds(i * P, P), :]
                act.dma_start(dst, y_sb[:, :]).then_inc(N["y_out"], 16)

            act.wait_ge(N["scattered"], 16 * 2 * NT)
            load_rows(0)
            act.wait_ge(N["xt_ps"], 1)
            load_rows(1)
            copy_pre(0)
            act.wait_ge(N["xt_ps"], 2)
            load_rows(2)
            gelu(0)
            with act.Fori(0, SLOT_TILES - 3) as i:
                copy_pre(i + 1)
                act.wait_ge(N["xt_ps"], i + 3)
                load_rows(i + 3)
                store(i)
                gelu(i + 1)
            for i in range(SLOT_TILES - 3, SLOT_TILES):
                if i + 1 < SLOT_TILES:
                    copy_pre(i + 1)
                store(i)
                if i + 1 < SLOT_TILES:
                    gelu(i + 1)

        def moe1_dve(dve):
            v = nc.vector

            def rows_out(i):
                dve.wait_ge(N["xt_ps"], i + 1)
                if not isinstance(i, int) or i:
                    dve.wait_ge(N["up"], 2 * i)
                v.tensor_copy(xt[:, :, :].rearrange("p c n -> p (c n)"), ps[:, 6, 0:DM]).then_inc(N["xt"], 1)

            def add_bias(i):
                e = expert_of(i, mybir.EngineType.DVE)
                if not isinstance(i, int) or i:
                    dve.wait_ge(N["dn"], i)
                for half in range(2):
                    dve.wait_ge(N["hT"], 2 * i + half + 1)
                    bias = b1_sb[:, bass.ds(e, 1), 4 * half:4 * half + 4].rearrange("p o f -> p (o f)")
                    v.tensor_tensor(h1[:, 4 * half:4 * half + 4, :],
                                    ps[:, 2 + half, :].rearrange("p (f n) -> p f n", f=4),
                                    bias.unsqueeze(2).to_broadcast([P, 4, P]), ALU.add).then_inc(N["hb"], 1)

            def result(i):
                if not isinstance(i, int) or i:
                    dve.wait_ge(N["y_out"], 16 * i)
                dve.wait_ge(N["dn"], i + 1)
                v.tensor_copy(y_sb[:, :], ps[:, 4, 0:DM]).then_inc(N["y"], 1)

            rows_out(0)
            rows_out(1)
            add_bias(0)
            rows_out(2)
            result(0)
            add_bias(1)
            with dve.Fori(1, SLOT_TILES - 2) as i:
                rows_out(i + 2)
                result(i)
                add_bias(i + 1)
            result(SLOT_TILES - 2)
            add_bias(SLOT_TILES - 1)
            result(SLOT_TILES - 1)
            for t in range(NT):
                dve.wait_ge(N[f"got{t}"], 32)
                v.scalar_tensor_tensor(X[:, t, :], got[0][:, t, :], pair_w[:, 0, t:t + 1], X[:, t, :],
                                       ALU.mult, ALU.add).then_inc(N["acc"], 1)
                dve.wait_ge(N["acc"], NT + 2 * t + 1)
                v.scalar_tensor_tensor(X[:, t, :], got[1][:, t, :], pair_w[:, 1, t:t + 1], X[:, t, :],
                                       ALU.mult, ALU.add).then_inc(N["acc"], 1)
            dve.wait_ge(N["acc"], 3 * NT)

        block = ctx.enter_context(nc.Block())

        @block.sync
        def _(sp):
            sp.dma_start(ident[:, :], a["ident"]).then_inc(ld_const, 16)
            sp.dma_start(ctx_in[:, :, :], a["ctx_1024"].rearrange("b (h p) d -> p (b h) d", p=P)).then_inc(ld_ctx, 16)
            sp.dma_start(in_w[:, :, :], a["L0_xattn_in_proj_w"].rearrange("(e p) d -> p e d", p=P)).then_inc(ld_ssm, 16)
            sp.dma_start(x_w[:, :], a["L0_xattn_x_proj_w"]).then_inc(ld_ssm, 16)
            sp.dma_start(dt_w[:, :, :], a["L0_xattn_dt_proj_w"].rearrange("(e p) d -> p e d", p=P)).then_inc(ld_ssm, 16)
            sp.dma_start(cols[:, :, 0:DC], a["L0_xattn_conv_w"].rearrange("(e p) d -> p e d", p=P)).then_inc(ld_ssm, 16)
            for k, n in enumerate(["conv_b", "dt_proj_b", "D"]):
                sp.dma_start(cols[:, :, DC + k:DC + k + 1],
                             a["L0_xattn_" + n].rearrange("(e p o) -> p e o", p=P, o=1),
                             allow_slow_non_contiguous=True).then_inc(ld_ssm, 16)
            sp.dma_start(a_log[:, :, :], a["L0_xattn_A_log"].rearrange("(e p) d -> p e d", p=P)).then_inc(ld_ssm, 16)
            sp.dma_start(gates[:, 0:2], a["g_xattn"].unsqueeze(0).to_broadcast([P, 2])).then_inc(ld_gate, 16)
            sp.dma_start(gates[:, 2:4], a["g_ffn"].unsqueeze(0).to_broadcast([P, 2])).then_inc(ld_gate, 16)
            sp.dma_start(temp[:, :], a["L0_ffn_temperature"].unsqueeze(0).to_broadcast([P, 1])).then_inc(ld_gate, 16)
            sp.dma_start(rows[:, :, :], a["rows"]).then_inc(ld_const, 16)
            sp.dma_start(before[:, :, :], a["before"]).then_inc(ld_const, 16)
            sp.dma_start(freq[:, :], a["freq"]).then_inc(ld_const, 16)
            sp.dma_start(X[:, :, :], a["x"].rearrange("b (h p) d -> p (b h) d", p=P)).then_inc(ld_x, 16)
            sp.dma_start(posT[:, :], a["fside_BxSx2_0"].rearrange("b s a -> a (b s)"),
                         allow_slow_non_contiguous=True).then_inc(ld_pos, 16)
            sp.dma_start(ones_row[:, :], a["rows"][0:1, 0, :]).then_inc(ld_const, 16)
            sp.wait_ge(N["blank"], 1)
            sp.dma_start(slots_d.rearrange("(k p) d -> p k d", p=P),
                         blank[:, :].unsqueeze(1).to_broadcast([P, SLOT_TILES, DM])).then_inc(N["blanked"], 16)
            if upto >= 2:
                moe0_sp(sp)
                sp.wait_ge(M["acc"], 8 + 8 * EXPERTS)
            if upto >= 3:
                att_sp(sp)
                sp.wait_ge(T["X3"], NT)
            if upto >= 4:
                moe1_sp(sp)
                sp.wait_ge(N["acc"], 3 * NT)
            sp.wait_ge(S["X1"], NT)
            sp.dma_start(out.rearrange("b (h p) d -> p (b h) d", p=P), X[:, :, :]).then_inc(stored, 16)
            sp.wait_ge(stored, 16)

        @block.vector
        def _(dve):
            nc.vector.memset(minushalf[:, :], -0.5).then_inc(set_up, 1)
            nc.vector.memset(blank[:, :], 0.0).then_inc(N["blank"], 1)
            dve.wait_ge(ld_x, 16)
            ln_dve(dve, 0)
            ssm_dve(dve)
            if upto >= 2:
                ln_dve(dve, 1)
                gate0_dve(dve)
                moe0_dve(dve)
            if upto >= 3:
                ln_dve(dve, 2)
                att_dve(dve)
            if upto >= 4:
                ln_dve(dve, 3)
                gate1_dve(dve)
                bias_dve(dve)
                moe1_dve(dve)

        @block.gpsimd
        def _(pool):
            pool.wait_ge(set_up, 2)
            ln_pool(pool, 0)
            if upto >= 2:
                ln_pool(pool, 1)
            if upto >= 3:
                ln_pool(pool, 2)
                att_pool(pool)
            if upto >= 4:
                ln_pool(pool, 3)
                moe1_pool(pool)

        @block.scalar
        def _(act):
            ssm_act(act)
            if upto >= 2:
                ln_act(act, 1)
                gate0_act(act)
                moe0_act(act)
            if upto >= 3:
                ln_act(act, 2)
                att_act(act)
            if upto >= 4:
                ln_act(act, 3)
                gate1_act(act)
                bias_act(act)
                moe1_act(act)

        @block.tensor
        def _(pe):
            ssm_pe(pe)
            if upto >= 2:
                ln_pe(pe, 1)
                gate0_pe(pe)
                moe0_pe(pe)
            if upto >= 3:
                ln_pe(pe, 2)
                att_pe(pe)
            if upto >= 4:
                ln_pe(pe, 3)
                gate1_pe(pe)
                bias_pe(pe)
                moe1_pe(pe)


def kernel(_upto=99, **inputs):
    import concourse.bacc as bacc
    from concourse.bass_utils import run_bass_kernel_spmd as run

    nc = bacc.Bacc("TRN2", target_bir_lowering=False, num_devices=1)
    arrays, args = {}, {}
    for name, value in {**inputs, **constants()}.items():
        v = np.ascontiguousarray(value)
        arrays["in_" + name] = v
        args[name] = nc.dram_tensor("in_" + name, v.shape, mybir.dt.from_np(v.dtype), kind="ExternalInput").ap()
    out = nc.dram_tensor("out_x", (BATCH, SEQ, DM), F32, kind="ExternalOutput").ap()
    program(nc, args, out, _upto)
    return run(nc, [arrays], core_ids=[0]).results[0]["out_x"]
```

```python
from contextlib import ExitStack

import numpy as np

import concourse.bass as bass
from concourse import mybir

ALU = mybir.AluOpType
ACT = mybir.ActivationFunctionType
F32 = mybir.dt.float32
BF16 = mybir.dt.bfloat16
F32R = mybir.dt.float32r
AX = mybir.AxisListType

P = 128
BATCH, SEQ, DM = 4, 256, 256
NT = BATCH * SEQ // P
TOK = BATCH * SEQ
CTX = 128
DI, DS, DC, DR = 256, 16, 4, 8
EXPERTS = 8
F0, F1 = 256, 1024
HEADS, HD = 32, 8
EPS = 1e-5
GOLDEN = 1.0 / np.e
LOWER, UPPER = 0.5 - np.log(4.0 / 3.0), 0.5
FAR = 1e36
SLOT_TILES = 2 * TOK // P + EXPERTS - 1
TWO_PI = 2.0 * np.pi
ARENA = 34208
TABLES = ARENA - 4352
SLOT_WORDS = 2 * 32 * 256 // 2
ROUND = 1.5 * 2.0 ** 23


def constants():
    ident = np.eye(P, dtype=np.float32)
    rows = np.tile(np.eye(32, dtype=np.float32), (3, 1))
    before = np.zeros((P, EXPERTS, EXPERTS), np.float32)
    for e in range(EXPERTS):
        before[:, e, :e] = 1.0
    freq = np.zeros((2, P), np.float32)
    for p in range(P):
        freq[(p // 4) % 2, p] = np.float32(10000.0) ** np.float32(-((p // 2) % 2) / 2)
    lower = np.triu(np.ones((P, P), np.float32), 1)
    part = np.arange(P, dtype=np.float32)[:, None]
    code = [2.0 * t + k + 1 for k in range(2) for t in range(NT)]
    tile = [float(t) for k in range(2) for t in range(NT)]
    numbers = np.concatenate([np.tile(np.arange(P, dtype=np.float32), (P, 1)), part, part + 2 * TOK + P,
                              np.tile(np.float32(code), (P, 1)), np.tile(np.float32(tile), (P, 1))], axis=1)
    return {"ident": ident, "rows": rows, "before": before, "freq": freq, "lower": lower, "numbers": numbers}


def program(nc, a, out):
    ctx = ExitStack()
    with ctx:
        def sb(name, shape, dt=F32):
            return ctx.enter_context(nc.sbuf_tensor(name, shape, dt))

        def sem(name):
            return ctx.enter_context(nc.semaphore(name))

        ps = ctx.enter_context(nc.psum_tensor("ps", [P, 8, 512], F32))

        X = sb("X", [P, NT, DM])
        with (nc.sbuf_tensor("up_r", [P, 2, 2, F1], F32R) as up_r,
              nc.sbuf_tensor("xt_r", [P, 2, 2, P], F32R) as xt_r):
            pass
        with (nc.sbuf_tensor("h_r", [P, 2, 2, 2, 512], F32R) as h_r,
              nc.sbuf_tensor("d_r", [P, 2, 2, DM], F32R) as d_r):
            pass
        xn = sb("xn", [P, NT, DM])
        xnT = sb("xnT", [P, 2, TOK])
        ctxT = sb("ctxT", [P, TOK])
        ident = sb("ident", [P, P])
        before = sb("before", [P, EXPERTS, EXPERTS])
        freq = sb("freq", [2, P])
        stats = sb("stats", [P, NT, 6])
        meanvar = sb("meanvar", [P, NT, 2])
        vareps = sb("vareps", [P, NT])
        minushalf = sb("minushalf", [P, NT])
        rstd = sb("rstd", [P, NT])
        gates = sb("gates", [P, 4])
        tg = sb("tg", [P, 4])
        temp = sb("temp", [P, 1])
        halfrt = sb("halfrt", [P, 1])
        posT = sb("posT", [2, TOK])
        ones_row = sb("ones_row", [1, P])

        arena = sb("arena", [P, ARENA])

        with (nc.sbuf_tensor("gu_r", [P, 2, 2, 2, 2, F0], F32R) as gu_r,
              nc.sbuf_tensor("xr", [P, 2, 2, TOK], F32R) as xr):
            pass
        arena_high = sb("arena_high", [P, SLOT_WORDS])

        class Region:
            def __init__(self, start=0, memory=None):
                self.used = start
                self.memory = arena if memory is None else memory

            def __call__(self, name, shape, dt=F32):
                count = 1
                for d in shape[1:]:
                    count *= d
                words = (count + 1) // 2 if dt == BF16 else count
                view = self.memory[0:shape[0], self.used:self.used + words]
                self.used += words
                assert self.used <= self.memory.shape[1], (name, self.used)
                if dt != F32:
                    view = view.bitcast(dt)
                if len(shape) > 2:
                    axes = "abcde"[:len(shape) - 1]
                    view = view.rearrange(f"p ({' '.join(axes)}) -> p {' '.join(axes)}",
                                          **dict(zip(axes, shape[1:])))
                return view

        top = Region(TABLES)
        cos = top("cos", [P, TOK])
        sin = top("sin", [P, TOK])
        wq = top("wq", [P, 2, DM])
        wkv = top("wkv", [P, 2 * DM])
        wout = top("wout", [P, 2, DM])
        wq_sw = top("wq_sw", [P, 2, DM])
        wk_sw = top("wk_sw", [P, DM])

        ld_const, ld_x, ld_ctx, ld_ssm, ld_gate, ld_att, ld_pos = (
            sem("ld_const"), sem("ld_x"), sem("ld_ctx"), sem("ld_ssm"), sem("ld_gate"), sem("ld_att"), sem("ld_pos"))
        set_up = sem("set_up")
        stored = sem("stored")
        dve_order = sem("dve_order")
        act_order = sem("act_order")

        L = {n: sem("ln_" + n) for n in ["stat", "agg", "var", "rstd", "xn", "xnT_ps", "xnT"]}

        def ln_dve(dve, n, early=False):
            ln_stats(dve, n, early)
            ln_scale(dve, n)

        def ln_tile_stats(dve, tiles):
            for t in tiles:
                nc.vector.bn_stats(stats[:, t, :], X[:, t, :]).then_inc(L["stat"], 1)

        def ln_stats(dve, n, early=False):
            if not early:
                ln_tile_stats(dve, range(NT))
            for t in range(NT):
                dve.wait_ge(L["stat"], NT * n + t + 1)
                nc.vector.bn_aggr(meanvar[:, t, :], stats[:, t, :]).then_inc(L["agg"], 1)
            dve.wait_ge(L["agg"], NT * n + NT)
            nc.vector.tensor_scalar(vareps[:, :], meanvar[:, :, 1], EPS, None, ALU.add).then_inc(L["var"], 1)

        def ln_scale(dve, n):
            dve.wait_ge(L["rstd"], n + 1)
            for t in range(NT):
                nc.vector.tensor_scalar(xn[:, t, :], X[:, t, :], meanvar[:, t, 0:1], rstd[:, t:t + 1],
                                        ALU.subtract, ALU.mult).then_inc(L["xn"], 1)

        def ln_pool(pool, n):
            pool.wait_ge(L["var"], n + 1)
            nc.gpsimd.tensor_tensor(rstd[:, :], vareps[:, :], minushalf[:, :], ALU.pow).then_inc(L["rstd"], 1)

        def ln_pe(pe, n):
            for th in range(2):
                pe.wait_ge(L["xn"], NT * n + 4 * th + 4)
                for c in range(2):
                    for q in range(4):
                        mm = nc.tensor.transpose(ps[:, 2 * th + c, q * P:(q + 1) * P],
                                                 xn[:, 4 * th + q, c * P:(c + 1) * P], ident[:, :])
                    mm.then_inc(L["xnT_ps"], 1)

        def ln_act(act, n):
            for th in range(2):
                for c in range(2):
                    act.wait_ge(L["xnT_ps"], 4 * (n - 1) + 2 * th + c + 1)
                    nc.scalar.copy(xnT[:, c, th * 512:(th + 1) * 512], ps[:, 2 * th + c, :]).then_inc(L["xnT"], 1)

        SSM_LOADS = 8
        sbs = Region()
        sbh = Region(0, arena_high)

        ctx_in = sbs("ctx_in", [P, NT, CTX])
        in_w = sbs("in_w", [P, 2, CTX])
        x_w = sbs("x_w", [DR + 2 * DS, DI])
        dt_w = sbs("dt_w", [P, 2, DR])
        cols = sbs("cols", [P, 2, DC + 3])
        a_log = sbs("a_log", [P, 2, DS])
        neg_a = sbs("neg_a", [P, 2, DS])
        rows = sbs("rows", [96, 32])
        rows_bf = sbs("rows_bf", [96, 32, P], BF16)
        in_wT = sbs("in_wT", [P, DI])
        x_wT = sbs("x_wT", [P, 2, 96 + DR])
        dt_wT = sbs("dt_wT", [DR, DI])
        diag = sbs("diag", [P, 2, P])
        xpad = sbs("xpad", [P, 2, BATCH, SEQ + DC - 1])
        conv = sbs("conv", [P, 2, TOK])
        u = sbs("u", [P, 2, TOK])
        dt_lo = sbs("dt_lo", [DR, TOK])
        t_abs = sbs("t_abs", [P, 2, TOK])
        t_exp = sbs("t_exp", [P, 2, TOK])
        delta = sbs("delta", [P, 2, TOK])
        du = sbs("du", [P, 2, TOK])
        bc = sbs("bc", [96, 3, TOK])
        bc3 = sbs("bc3", [96, TOK], BF16)
        dA = sbh("dA", [P, 2, 2, TOK])
        dBu = sbs("dBu", [P, 2, TOK])
        h = sbh("h", [P, 2, TOK])
        c_sb = sbs("c_sb", [P, 2, TOK])
        hC = sbh("hC", [P, 2, TOK])
        sz = t_abs[:, :, :].rearrange("p e (b l) -> p e b l", b=BATCH)
        gy = t_exp

        names = ["wT", "wTc", "ctxT_ps", "ctxT", "xin_ps", "xpad", "conv", "u", "xdbl_ps",
                    "dt_lo", "bc_cp", "bc_r", "bc3", "dt_ps", "v", "abs", "exp", "plus", "log",
                    "delta", "du", "far", "na", "B", "C", "dA", "dBu", "scan", "Y", "sz", "gy",
                    "yT", "X1", "zero", "rows", "C_sb", "hC0", "hC1"]
        S = {n: sem("ssm_" + n) for n in names}

        def ssm_dve(dve):
            nc.vector.memset(xpad[:, :, :, 0:DC - 1], 0.0).then_inc(S["zero"], 1)
            dve.wait_ge(S["wT"], 1)
            nc.vector.tensor_copy(in_wT[:, :], ps[:, 4, 0:256]).then_inc(S["wTc"], 1)
            for k in range(2):
                src = ps[:, 5, k * 64:k * 64 + 40]
                nc.vector.tensor_copy(x_wT[:, k, 96:96 + DR], src[:, 0:DR]).then_inc(S["wTc"], 1)
                nc.vector.tensor_copy(x_wT[:, k, 0:96].rearrange("p (r n) -> p r n", r=3),
                                      src[:, DR:40].unsqueeze(1).to_broadcast([P, 3, 32])).then_inc(S["wTc"], 1)
            nc.vector.tensor_copy(dt_wT[:, :], ps[0:DR, 6, 0:256]).then_inc(S["wTc"], 1)
            dve.wait_ge(ld_const, 16 * 4)
            for e in range(2):
                nc.vector.tensor_scalar(diag[:, e, :], ident[:, :], cols[:, e, DC + 2:DC + 3], None,
                                        ALU.mult).then_inc(S["wTc"], 1)
            dve.wait_ge(ld_x, 16)
            ln_stats(dve, 0)
            nc.vector.tensor_copy(rows_bf[:, :, :], rows[:, :].unsqueeze(2).to_broadcast([96, 32, P])).then_inc(S["rows"], 1)
            for e in range(2):
                dve.wait_ge(S["xpad"], 2 * e + 2)
                o = conv[:, e, :].rearrange("p (b l) -> p b l", b=BATCH)
                for k in range(DC):
                    if k:
                        dve.wait_ge(S["conv"], DC * e + k)
                        nc.vector.scalar_tensor_tensor(o, xpad[:, e, :, k:k + SEQ], cols[:, e, k:k + 1], o,
                                                       ALU.mult, ALU.add).then_inc(S["conv"], 1)
                    else:
                        nc.vector.tensor_scalar(o, xpad[:, e, :, 0:SEQ], cols[:, e, 0:1], None,
                                                ALU.mult).then_inc(S["conv"], 1)
            ln_scale(dve, 0)
            hi, lo = (c_sb[0:96, k, :].bitcast(BF16)[:, 0:TOK] for k in range(2))
            dve.wait_ge(S["bc_cp"], 2)
            nc.vector.tensor_copy(hi, bc[:, 0, :]).then_inc(S["bc_r"], 1)
            nc.vector.tensor_copy(bc3[0:32, :], bc[0:32, 0, :]).then_inc(S["bc3"], 1)
            dve.wait_ge(S["bc_r"], 1)
            nc.vector.tensor_tensor(bc[:, 1, :], bc[:, 0, :], hi, ALU.subtract).then_inc(S["bc_r"], 1)
            dve.wait_ge(S["bc_r"], 2)
            nc.vector.tensor_copy(lo, bc[:, 1, :]).then_inc(S["bc_r"], 1)
            nc.vector.tensor_copy(bc3[32:64, :], bc[32:64, 1, :]).then_inc(S["bc3"], 1)
            dve.wait_ge(S["bc_r"], 3)
            nc.vector.tensor_tensor(bc[:, 2, :], bc[:, 1, :], lo, ALU.subtract).then_inc(S["bc_r"], 1)
            dve.wait_ge(S["bc_r"], 4)
            nc.vector.tensor_copy(bc3[64:96, :], bc[64:96, 2, :]).then_inc(S["bc3"], 1)
            for e in range(2):
                dve.wait_ge(S["v"], e + 1)
                nc.vector.tensor_scalar(delta[:, e, :], conv[:, e, :], 0.0, None, ALU.max).then_inc(S["plus"], 1)
                dve.wait_ge(S["exp"], e + 1)
                nc.vector.tensor_scalar(dBu[:, e, :], t_exp[:, e, :], 1.0, None, ALU.add).then_inc(S["plus"], 1)
                dve.wait_ge(S["plus"], 4 * e + 2)
                nc.vector.scalar_tensor_tensor(h[:, e, :], dBu[:, e, :], -1.0, t_exp[:, e, :],
                                               ALU.add, ALU.subtract).then_inc(S["plus"], 1)
                dve.wait_ge(S["plus"], 4 * e + 3)
                nc.vector.tensor_tensor(delta[:, e, :], delta[:, e, :], h[:, e, :], ALU.subtract).then_inc(S["plus"], 1)
                dve.wait_ge(S["plus"], 4 * e + 4)
                dve.wait_ge(S["log"], e + 1)
                nc.vector.tensor_tensor(delta[:, e, :], delta[:, e, :], hC[:, e, :], ALU.add).then_inc(S["delta"], 1)
                dve.wait_ge(S["delta"], e + 1)
                dve.wait_ge(S["u"], e + 1)
                nc.vector.tensor_tensor(du[:, e, :], delta[:, e, :], u[:, e, :], ALU.mult).then_inc(S["du"], 1)
                dve.wait_ge(S["du"], e + 1)
                nc.vector.memset(delta[:, e, :].rearrange("p (b l) -> p b l", b=BATCH)[:, :, 0:1],
                                 FAR).then_inc(S["far"], 1)
            dve.wait_ge(S["far"], 2)

            def step(n, s):
                psB = ps[:, 0:2, :].rearrange("p k n -> p (k n)")
                psC = ps[:, 2:4, :].rearrange("p k n -> p (k n)")
                dve.wait_ge(S["B"], n + 1)
                dve.wait_ge(S["scan"], 4 + 2 * n)
                for e in range(2):
                    nc.vector.tensor_tensor(dBu[:, e, :], du[:, e, :], psB, ALU.mult).then_inc(S["dBu"], 1)
                for e in range(2):
                    dve.wait_ge(S["dBu"], 2 * n + e + 1)
                    dve.wait_ge(S["dA"], 2 * n + e + 1)
                    if e:
                        dve.wait_ge(S["hC1"], n + 1)
                    nc.vector.tensor_tensor_scan(h[:, e, :], dA[:, s, e, :], dBu[:, e, :], 0.0,
                                                 ALU.mult, ALU.add).then_inc(S["scan"], 1)
                dve.wait_ge(S["C_sb"], n + 1)
                dve.wait_ge(S["scan"], 4 + 2 * n + 1)
                dve.wait_ge(S["Y"], 2 * n + 1)
                nc.vector.tensor_tensor(hC[:, 0, :], h[:, 0, :], psC, ALU.mult).then_inc(S["hC0"], 1)

            dve.sem_inc(S["scan"], 4)
            with dve.Fori(0, DS // 2) as i:
                for s in range(2):
                    step(2 * i + s, s)
            for e in range(2):
                dve.wait_ge(S["Y"], 2 + 2 * DS)
                dve.wait_ge(S["sz"], e + 1)
                nc.vector.tensor_tensor(gy[:, e, :], ps[:, 4 + 2 * e:6 + 2 * e, :].rearrange("p k n -> p (k n)"),
                                        sz[:, e, :, :].rearrange("p b l -> p (b l)"), ALU.mult).then_inc(S["gy"], 1)
            for t in range(NT):
                dve.wait_ge(S["yT"], t // 2 + 1)
                nc.vector.scalar_tensor_tensor(X[:, t, :], ps[:, t // 2, (t % 2) * 256:(t % 2) * 256 + 256],
                                               tg[:, 0:1], X[:, t, :], ALU.mult, ALU.add).then_inc(S["X1"], 1)
            dve.wait_ge(S["X1"], NT)

        def ssm_pe(pe):
            pe.wait_ge(ld_const, 16 * 4)
            pe.wait_ge(ld_ssm, 16 * SSM_LOADS)
            for e in range(2):
                nc.tensor.transpose(ps[:, 4, e * P:(e + 1) * P], in_w[:, e, :], ident[:, :])
                nc.tensor.transpose(ps[:, 5, e * 64:e * 64 + 40], x_w[:, e * P:(e + 1) * P], ident[0:40, 0:40])
                mm = nc.tensor.transpose(ps[0:DR, 6, e * P:(e + 1) * P], dt_w[:, e, :], ident[:, :])
            mm.then_inc(S["wT"], 1)
            pe.wait_ge(ld_ctx, 16)
            for th in range(2):
                for q in range(4):
                    mm = nc.tensor.transpose(ps[:, 2 + th, q * P:(q + 1) * P], ctx_in[:, 4 * th + q, :], ident[:, :])
                mm.then_inc(S["ctxT_ps"], 1)
            angles_pe(pe)
            pe.wait_ge(S["wTc"], 8)
            for e in range(2):
                for th in range(2):
                    if not e:
                        pe.wait_ge(S["ctxT"], th + 1)
                    nc.tensor.matmul(ps[:, 4 + 2 * e + th, :], in_wT[:, e * P:(e + 1) * P],
                                     ctxT[:, th * 512:(th + 1) * 512], start=True, stop=True).then_inc(S["xin_ps"], 1)
            pe.wait_ge(S["u"], 2)
            pe.wait_ge(T["red"], 1)
            for th in range(2):
                for k in range(2):
                    mm = nc.tensor.matmul(ps[0:96 + DR, th, :], x_wT[:, k, :], u[:, k, th * 512:(th + 1) * 512],
                                          start=(k == 0), stop=(k == 1))
                mm.then_inc(S["xdbl_ps"], 1)
            pe.wait_ge(S["dt_lo"], 2)
            for e in range(2):
                for th in range(2):
                    mm = nc.tensor.matmul(ps[:, 4 + 2 * e + th, :], dt_wT[:, e * P:(e + 1) * P],
                                          dt_lo[:, th * 512:(th + 1) * 512], start=True, stop=True)
                mm.then_inc(S["dt_ps"], 1)

            def spread(bank, row, done):
                for th in range(2):
                    mm = nc.tensor.matmul(ps[:, bank + th, :], rows_bf[:, row, :], bc3[:, th * 512:(th + 1) * 512],
                                          start=True, stop=True)
                mm.then_inc(done, 1)

            def add_y(e):
                for th in range(2):
                    mm = nc.tensor.matmul(ps[:, 4 + 2 * e + th, :], ident[:, :], hC[:, e, th * 512:(th + 1) * 512],
                                          start=False, stop=False, skip_group_check=True)
                mm.then_inc(S["Y"], 1)

            pe.wait_ge(S["bc3"], 3)
            pe.wait_ge(S["rows"], 1)
            spread(0, 0, S["B"])
            spread(2, DS, S["C"])
            pe.wait_ge(S["far"], 2)
            for e in range(2):
                for th in range(2):
                    mm = nc.tensor.matmul(ps[:, 4 + 2 * e + th, :], diag[:, e, :], u[:, e, th * 512:(th + 1) * 512],
                                          start=True, stop=False, skip_group_check=True)
                mm.then_inc(S["Y"], 1)

            def step(n, more=True):
                if more:
                    pe.wait_ge(S["dBu"], 2 * n + 2)
                    spread(0, n + 1, S["B"])
                pe.wait_ge(S["hC0"], n + 1)
                add_y(0)
                if more:
                    pe.wait_ge(S["C_sb"], n + 1)
                    spread(2, DS + n + 1, S["C"])
                pe.wait_ge(S["hC1"], n + 2)
                add_y(1)

            with pe.Fori(0, DS - 1) as n:
                step(n)
            step(DS - 1, more=False)
            for b in range(BATCH):
                for lh in range(2):
                    for e in range(2):
                        if b == 0 and lh == 0:
                            pe.wait_ge(S["gy"], e + 1)
                        at = b * SEQ + lh * P
                        mm = nc.tensor.transpose(ps[:, b, lh * 256 + e * P:lh * 256 + (e + 1) * P],
                                                 gy[:, e, at:at + P], ident[:, :])
                mm.then_inc(S["yT"], 1)

        def ssm_pool(pool):
            pool.sem_inc(S["hC1"], 1)
            with pool.Fori(0, DS // 2) as i:
                for s in range(2):
                    n = 2 * i + s
                    pool.wait_ge(S["C_sb"], n + 1)
                    pool.wait_ge(S["scan"], 4 + 2 * n + 2)
                    pool.wait_ge(S["Y"], 2 * n + 2)
                    nc.gpsimd.tensor_tensor(hC[:, 1, :], h[:, 1, :], c_sb[:, s, :], ALU.mult).then_inc(S["hC1"], 1)

        def ssm_act(act):
            act.wait_ge(ld_gate, 32 + 16)
            nc.scalar.activation(tg[:, :], gates[:, :], ACT.Tanh).then_inc(set_up, 1)
            act.wait_ge(ld_ssm, 16 * SSM_LOADS)
            nc.scalar.activation(a_log[:, :, :], a_log[:, :, :], ACT.Exp).then_inc(act_order, 1)
            act.wait_ge(act_order, 1)
            nc.scalar.mul(neg_a[:, :, :], a_log[:, :, :], -1.0).then_inc(S["na"], 1)
            for th in range(2):
                act.wait_ge(S["ctxT_ps"], th + 1)
                nc.scalar.copy(ctxT[:, th * 512:(th + 1) * 512], ps[:, 2 + th, :]).then_inc(S["ctxT"], 1)
            angles_copy_act(act)
            act.wait_ge(S["zero"], 1)
            for e in range(2):
                for th in range(2):
                    act.wait_ge(S["xin_ps"], 2 * e + th + 1)
                    nc.scalar.copy(xpad[:, e, 2 * th:2 * th + 2, DC - 1:],
                                   ps[:, 4 + 2 * e + th, :].rearrange("p (b l) -> p b l", b=2)).then_inc(S["xpad"], 1)
            nc.scalar.preload_act_table(ACT.Silu)
            for e in range(2):
                act.wait_ge(S["conv"], DC * e + DC)
                nc.scalar.activation(u[:, e, :], conv[:, e, :], ACT.Silu, bias=cols[:, e, DC:DC + 1]).then_inc(S["u"], 1)
            for th in range(2):
                act.wait_ge(S["xdbl_ps"], th + 1)
                nc.scalar.copy(dt_lo[:, th * 512:(th + 1) * 512], ps[96:96 + DR, th, :]).then_inc(S["dt_lo"], 1)
                nc.scalar.copy(bc[:, 0, th * 512:(th + 1) * 512], ps[0:96, th, :]).then_inc(S["bc_cp"], 1)
            nc.scalar.preload_act_table(ACT.Exp)
            for e in range(2):
                act.wait_ge(S["dt_ps"], e + 1)
                nc.scalar.activation(conv[:, e, :], ps[:, 4 + 2 * e:6 + 2 * e, :].rearrange("p k n -> p (k n)"),
                                     ACT.Identity, bias=cols[:, e, DC + 1:DC + 2]).then_inc(S["v"], 1)
                act.wait_ge(S["v"], e + 1)
                nc.scalar.activation(t_abs[:, e, :], conv[:, e, :], ACT.Abs).then_inc(S["abs"], 1)
                act.wait_ge(S["abs"], e + 1)
                nc.scalar.activation(t_exp[:, e, :], t_abs[:, e, :], ACT.Exp, scale=-1.0).then_inc(S["exp"], 1)
            for e in range(2):
                act.wait_ge(S["plus"], 4 * e + 2)
                nc.scalar.activation(hC[:, e, :], dBu[:, e, :], ACT.Ln).then_inc(S["log"], 1)
            nc.scalar.preload_act_table(ACT.Exp)
            angles_abs_act(act)
            act.wait_ge(S["far"], 2)
            with act.Fori(0, DS // 2) as i:
                for s in range(2):
                    for e in range(2):
                        act.wait_ge(S["scan"], 4 * i + 2 * s + e + 1)
                        nc.scalar.activation(dA[:, s, e, :], delta[:, e, :], ACT.Exp,
                                             scale=neg_a[:, e, bass.ds(2 * i + s, 1)]).then_inc(S["dA"], 1)
                    act.wait_ge(S["hC1"], 2 * i + s + 1)
                    act.wait_ge(S["C"], 2 * i + s + 1)
                    nc.scalar.copy(c_sb[:, s, :], ps[:, 2:4, :].rearrange("p k n -> p (k n)")).then_inc(S["C_sb"], 1)
            angles_sin_act(act)
            act.wait_ge(L["xn"], NT)
            for e in range(2):
                nc.scalar.activation(sz[:, e, :, :], xn[:, e:NT:2, :], ACT.Silu).then_inc(S["sz"], 1)

        pair_gt = sb("pair_gt", [P, NT, EXPERTS * EXPERTS])
        pair_eq = sb("pair_eq", [P, NT, EXPERTS * EXPERTS])
        before_all = sb("before_all", [P, NT, EXPERTS * EXPERTS])
        rank = sb("rank", [P, NT, EXPERTS])
        per_tile = sb("per_tile", [P, 4, NT])
        comb = sb("comb", [P, NT, EXPERTS])
        step_count = [0]

        def link(ins):
            step_count[0] += 1
            ins.then_inc(dve_order, 1)
            return step_count[0]

        def then(dve, ins):
            dve.wait_ge(dve_order, link(ins))

        def top2(dve, score, mask):
            v = nc.vector
            for t in range(NT):
                gt = pair_gt[:, t, :].rearrange("p (e j) -> p e j", e=EXPERTS)
                eq = pair_eq[:, t, :].rearrange("p (e j) -> p e j", e=EXPERTS)
                other = score[:, t, :].unsqueeze(1).to_broadcast([P, EXPERTS, EXPERTS])
                own = score[:, t, :].unsqueeze(2).to_broadcast([P, EXPERTS, EXPERTS])
                link(v.tensor_tensor(gt, other, own, ALU.is_gt))
                link(v.tensor_tensor(eq, other, own, ALU.is_equal))
            dve.wait_ge(dve_order, step_count[0])
            then(dve, v.tensor_tensor(pair_eq[:, :, :], pair_eq[:, :, :], before_all[:, :, :], ALU.mult))
            then(dve, v.tensor_tensor(pair_gt[:, :, :], pair_gt[:, :, :], pair_eq[:, :, :], ALU.add))
            then(dve, v.tensor_reduce(rank[:, :, :], pair_gt[:, :, :].rearrange("p t (e j) -> p t e j", e=EXPERTS),
                                      AX.X, ALU.add))
            then(dve, v.tensor_scalar(mask, rank[:, :, :], 2.0, None, ALU.is_lt))

        def by_tile(row):
            return per_tile[:, row, :].unsqueeze(2).to_broadcast([P, NT, EXPERTS])

        r0 = Region()
        golden = r0("golden", [P, 8, NT, EXPERTS])
        router0 = r0("router0", [P, 2, EXPERTS])
        gu_w = r0("gu_w", [P, 2, 2, 2, F0])
        d_w = r0("d_w", [P, 2, 2, DM])
        silu = r0("silu", [P, 2, 512])
        h0 = r0("h0", [P, 2, 2, 512])
        M = {n: sem("moe0_" + n) for n in ["d0", "d1", "w_hi", "w_lo", "x_hi", "x_lo", "router", "lg", "tanh", "dist",
                    "exp", "w0", "w1", "gu", "silu", "h", "dn", "acc", "ready"]}

        def gate0_pe(pe):
            pe.wait_ge(M["router"], 16)
            for t in range(NT):
                if t % 4 == 0:
                    pe.wait_ge(L["xnT"], 2 * (t // 4) + 2)
                for c in range(2):
                    mm = nc.tensor.matmul(ps[:, 7, t * EXPERTS:(t + 1) * EXPERTS], xnT[:, c, t * P:(t + 1) * P],
                                          router0[:, c, :], start=(c == 0), stop=(c == 1))
            mm.then_inc(M["lg"], 1)

        def gate0_act(act):
            th, dist, w, fb = (golden[:, k, :, :] for k in range(4))
            split_x_act(act)
            high_act(act, 0, 32)
            nc.scalar.preload_act_table(ACT.Tanh)
            act.wait_ge(M["ready"], 1)
            act.wait_ge(M["lg"], 1)
            lg = ps[:, 7, 0:NT * EXPERTS].rearrange("p (t e) -> p t e", t=NT)
            nc.scalar.activation(th, lg, ACT.Tanh, scale=halfrt[:, :]).then_inc(M["tanh"], 1)
            nc.scalar.preload_act_table(ACT.Exp)
            act.wait_ge(M["dist"], 1)
            nc.scalar.activation(w, dist, ACT.Exp, scale=-10.0).then_inc(M["exp"], 1)
            nc.scalar.activation(fb, dist, ACT.Exp, scale=-1.0 / 0.3).then_inc(M["exp"], 1)

        def gate0_dve(dve):
            v = nc.vector
            th, dist, w, fb, inh, zone, tmp, msk = (golden[:, k, :, :] for k in range(8))
            dve.wait_ge(ld_gate, 48)
            then(dve, v.reciprocal(temp[:, :], temp[:, :]))
            v.tensor_scalar(halfrt[:, :], temp[:, :], 0.5, None, ALU.mult).then_inc(M["ready"], 1)
            for t in range(NT):
                link(v.tensor_copy(before_all[:, t, :], before[:, :, :].rearrange("p e j -> p (e j)")))
            dve.sem_inc(M["h"], 2)
            split_x_dve(dve)
            low_dve(dve, 0, 0)
            dve.wait_ge(M["tanh"], 1)
            then(dve, v.tensor_scalar(inh, th, 0.5, 0.5, ALU.mult, ALU.add))
            then(dve, v.tensor_scalar(tmp, inh, float(GOLDEN), None, ALU.subtract))
            v.scalar_tensor_tensor(dist, tmp, -1.0, tmp, ALU.mult, ALU.max).then_inc(M["dist"], 1)
            then(dve, v.tensor_scalar(zone, inh, float(LOWER), None, ALU.is_ge))
            then(dve, v.scalar_tensor_tensor(zone, inh, float(UPPER), zone, ALU.is_le, ALU.mult))
            dve.wait_ge(M["exp"], 2)
            then(dve, v.tensor_tensor(w, w, zone, ALU.mult))
            then(dve, v.tensor_reduce(per_tile[:, 0, :], w, AX.X, ALU.add))
            then(dve, v.tensor_scalar(per_tile[:, 1, :], per_tile[:, 0, :], 1e-8, None, ALU.is_lt))
            top2(dve, fb, msk)
            hidden0(dve, 0, 0)
            then(dve, v.tensor_tensor(fb, fb, msk, ALU.mult))
            then(dve, v.tensor_reduce(per_tile[:, 2, :], fb, AX.X, ALU.add))
            then(dve, v.tensor_scalar(per_tile[:, 2, :], per_tile[:, 2, :], 1e-8, None, ALU.max))
            then(dve, v.reciprocal(per_tile[:, 3, :], per_tile[:, 2, :]))
            then(dve, v.tensor_tensor(fb, fb, by_tile(3), ALU.mult))
            then(dve, v.tensor_tensor(fb, fb, by_tile(1), ALU.mult))
            then(dve, v.tensor_scalar(per_tile[:, 1, :], per_tile[:, 1, :], -1.0, 1.0, ALU.mult, ALU.add))
            then(dve, v.tensor_tensor(w, w, by_tile(1), ALU.mult))
            then(dve, v.tensor_tensor(w, w, fb, ALU.add))
            then(dve, v.tensor_reduce(per_tile[:, 2, :], w, AX.X, ALU.add))
            then(dve, v.tensor_scalar(per_tile[:, 2, :], per_tile[:, 2, :], 1e-8, None, ALU.max))
            then(dve, v.reciprocal(per_tile[:, 3, :], per_tile[:, 2, :]))
            then(dve, v.tensor_scalar(per_tile[:, 3, :], per_tile[:, 3, :], tg[:, 2:3], None, ALU.mult))
            then(dve, v.tensor_tensor(comb[:, :, :], w, by_tile(3), ALU.mult))

        def split_x_act(act):
            for c in range(2):
                act.wait_ge(L["xnT"], 3 + c)
                nc.scalar.copy(xr[:, 0, c, :], xnT[:, c, :]).then_inc(M["x_hi"], 1)

        def split_x_dve(dve):
            for c in range(2):
                dve.wait_ge(M["x_hi"], c + 1)
                nc.vector.tensor_tensor(xr[:, 1, c, :], xnT[:, c, :], xr[:, 0, c, :].bitcast(F32), ALU.subtract
                                        ).then_inc(M["x_lo"], 1)

        def high_act(act, slot, landed):
            act.wait_ge(M[f"w{slot}"], landed)
            nc.scalar.copy(gu_r[:, slot, 0, :, :, :].rearrange("p g c n -> p (g c n)"),
                           gu_w[:, slot, :, :, :].rearrange("p g c n -> p (g c n)")).then_inc(M["w_hi"], 1)

        def low_dve(dve, slot, e):
            dve.wait_ge(M["w_hi"], e + 1)
            nc.vector.tensor_tensor(gu_r[:, slot, 1, :, :, :].rearrange("p g c n -> p (g c n)"),
                                    gu_w[:, slot, :, :, :].rearrange("p g c n -> p (g c n)"),
                                    gu_r[:, slot, 0, :, :, :].rearrange("p g c n -> p (g c n)").bitcast(F32),
                                    ALU.subtract).then_inc(M["w_lo"], 1)

        X_SPLITS = 2

        def parts_done(e, th):
            return X_SPLITS + 3 * e + 2 + th

        def down_parts_act(act, k, q, e, landed):
            slot, th = q // 2, q % 2
            if th == 0:
                act.wait_ge(M[f"d{slot}"], landed)
                act.wait_ge(M["dn"], k + 2)
                nc.scalar.copy(d_r[:, 0, :, :].rearrange("p f n -> p (f n)"),
                               d_w[:, slot, :, :].rearrange("p f n -> p (f n)")).then_inc(M["x_hi"], 1)
            act.wait_ge(M["h"], 2 * k + 4)
            nc.scalar.copy(h_r[:, th, 0, :, :].rearrange("p f n -> p (f n)"),
                           h0[:, th, :, :].rearrange("p f n -> p (f n)")).then_inc(M["x_hi"], 1)

        def down_parts_dve(dve, q, e):
            slot, th = q // 2, q % 2
            if th == 0:
                dve.wait_ge(M["x_hi"], parts_done(e, 0) - 1)
                nc.vector.tensor_tensor(d_r[:, 1, :, :].rearrange("p f n -> p (f n)"),
                                        d_w[:, slot, :, :].rearrange("p f n -> p (f n)"),
                                        d_r[:, 0, :, :].rearrange("p f n -> p (f n)").bitcast(F32),
                                        ALU.subtract).then_inc(M["x_lo"], 1)
            dve.wait_ge(M["x_hi"], parts_done(e, th))
            nc.vector.tensor_tensor(h_r[:, th, 1, :, :].rearrange("p f n -> p (f n)"),
                                    h0[:, th, :, :].rearrange("p f n -> p (f n)"),
                                    h_r[:, th, 0, :, :].rearrange("p f n -> p (f n)").bitcast(F32),
                                    ALU.subtract).then_inc(M["x_lo"], 1)

        def moe0_sp(sp):
            def load_up(e, slot):
                one = bass.ds(e, 1)
                for k, n in enumerate(["L0_ffn_Wg", "L0_ffn_Wu"]):
                    sp.dma_start(gu_w[:, slot, k, :, :], a[n][one, :, :].rearrange("o (k p) f -> p (o k) f", p=P)
                                 ).then_inc(M[f"w{slot}"], 16)

            def load_down(e, slot):
                one = bass.ds(e, 1)
                sp.dma_start(d_w[:, slot, :, :], a["L0_ffn_Wd"][one, :, :].rearrange("o (k p) f -> p (o k) f", p=P)
                             ).then_inc(M[f"d{slot}"], 16)
            sp.wait_ge(S["yT"], BATCH)
            sp.dma_start(router0[:, :, :], a["L0_ffn_Wr"].rearrange("(k p) e -> p k e", p=P)).then_inc(M["router"], 16)
            for e in range(2):
                load_up(e, e)
                load_down(e, e)
            with sp.Fori(0, EXPERTS // 2 - 1) as i:
                for slot in range(2):
                    sp.wait_ge(M["w_lo"], 2 * i + slot + 1)
                    load_up(2 * i + slot + 2, slot)
                    sp.wait_ge(M["dn"], 4 * i + 2 * slot + 4)
                    load_down(2 * i + slot + 2, slot)

        def moe0_pe(pe):
            def up(k, q, w_wait=None):
                slot, th = q // 2, q % 2
                if th == 0:
                    pe.wait_ge(M["w_lo"], w_wait)
                for f in range(2):
                    pe.wait_ge(M["h"], 2 * k + f + 1)
                    for g in range(2):
                        for c in range(2):
                            for part, (wp, xp) in enumerate([(0, 0), (0, 1), (1, 0)]):
                                mm = nc.tensor.matmul(ps[:, 2 * f + g, :], gu_r[:, slot, wp, g, c, f * P:(f + 1) * P],
                                                      xr[:, xp, c, th * 512:(th + 1) * 512],
                                                      start=(c == 0 and part == 0), stop=(c == 1 and part == 2))
                    mm.then_inc(M["gu"], 1)

            def down(k, q, e):
                th = q % 2
                pe.wait_ge(M["x_lo"], parts_done(e, th))
                pe.wait_ge(M["acc"], 4 * k + 4)
                for t in range(4):
                    for f in range(2):
                        for part, (wp, hp) in enumerate([(0, 0), (0, 1), (1, 0)]):
                            mm = nc.tensor.matmul(ps[:, 4 + 2 * th + t // 2, (t % 2) * 256:(t % 2) * 256 + 256],
                                                  h_r[:, th, hp, f, t * P:(t + 1) * P], d_r[:, wp, f, :],
                                                  start=(f == 0 and part == 0), stop=(f == 1 and part == 2))
                mm.then_inc(M["dn"], 1)

            def turn(i, last):
                for q in range(4):
                    if not (last and q == 3):
                        up(4 * i + q + 1, (q + 1) % 4, 2 * i + (q + 1) // 2 + 1)
                    down(4 * i + q, q, 2 * i + q // 2)

            pe.wait_ge(M["tanh"], 1)
            pe.wait_ge(M["x_lo"], X_SPLITS)
            pe.sem_inc(M["dn"], 2)
            up(0, 0, 1)
            with pe.Fori(0, EXPERTS // 2 - 1) as i:
                turn(i, False)
            turn(EXPERTS // 2 - 1, True)

        def moe0_act(act):
            def turn(i, last):
                for q in range(4):
                    k = 4 * i + q
                    for f in range(2):
                        act.wait_ge(M["gu"], 2 * k + f + 1)
                        act.wait_ge(M["h"], 2 * k + f + 1)
                        nc.scalar.activation(silu[:, f, :], ps[:, 2 * f, :], ACT.Silu).then_inc(M["silu"], 1)
                    down_parts_act(act, k, q, 2 * i + q // 2, 16 * i + 16)
                    if q == 0:
                        high_act(act, 1, 32 * i + 32)
                    if q == 2 and not last:
                        high_act(act, 0, 32 * i + 64)

            nc.scalar.preload_act_table(ACT.Silu)
            with act.Fori(0, EXPERTS // 2 - 1) as i:
                turn(i, False)
            turn(EXPERTS // 2 - 1, True)

        def hidden0(dve, k, q):
            for f in range(2):
                dve.wait_ge(M["silu"], 2 * k + f + 1)
                dve.wait_ge(M["dn"], k + 1)
                nc.vector.tensor_tensor(h0[:, q % 2, f, :], silu[:, f, :], ps[:, 2 * f + 1, :],
                                        ALU.mult).then_inc(M["h"], 1)

        def moe0_dve(dve):
            def add(i, q):
                th = q % 2
                dve.wait_ge(M["dn"], 4 * i + q + 3)
                dve.wait_ge(M["acc"], 8 + 16 * i + 4 * q - 4)
                for t in range(4):
                    tile = 4 * th + t
                    nc.vector.scalar_tensor_tensor(X[:, tile, :], ps[:, 4 + 2 * th + t // 2, (t % 2) * 256:(t % 2) * 256 + 256],
                                                   comb[:, tile, bass.ds(2 * i + q // 2, 1)], X[:, tile, :],
                                                   ALU.mult, ALU.add).then_inc(M["acc"], 1)

            def turn(i, last):
                for q in range(4):
                    down_parts_dve(dve, q, 2 * i + q // 2)
                    if not (last and q == 3):
                        hidden0(dve, 4 * i + q + 1, q + 1)
                    if q == 0:
                        low_dve(dve, 1, 2 * i + 1)
                    if q == 2 and not last:
                        low_dve(dve, 0, 2 * i + 2)
                    add(i, q)
                    if last and q >= 2:
                        dve.wait_ge(M["acc"], 8 + 8 * EXPERTS - 4 * (3 - q))
                        ln_tile_stats(dve, range(4 * (q - 2), 4 * (q - 2) + 4))

            dve.sem_inc(M["acc"], 8)
            with dve.Fori(0, EXPERTS // 2 - 1) as i:
                turn(i, False)
            turn(EXPERTS // 2 - 1, True)
            dve.wait_ge(M["acc"], 8 + 8 * EXPERTS)

        r1 = Region()
        qk1 = r1("qk1", [P, 2, HEADS, SEQ], BF16)
        vv = r1("vv", [P, NT, DM])
        v_pad = r1("v_pad", [P, 2, 2, 4, 32])
        mx = r1("mx", [P, 2, 2, HEADS])
        minus_one = r1("minus_one", [3, SEQ], BF16)
        m_parts = r1("m_parts", [32, 3, SEQ], BF16)
        m_rest = r1("m_rest", [32, 2, SEQ])
        probs = r1("probs", [P, 4, 2, 2, SEQ])
        o_rows = r1("o_rows", [P, 2, SEQ])
        recip16 = r1("recip16", [P, 16, 1])
        bout = r1("bout", [1, DM])
        parts = [r1("parts0", [P, 3, TOK], BF16), r1("parts1", [P, 3, TOK], BF16)]
        qk_rows = [r1("qk0", [P, 2, HEADS, SEQ], BF16), qk1,
                   Region(0, arena_high)("qk2", [P, 2, HEADS, SEQ], BF16)]
        assert r1.used <= TABLES and r0.used <= SLOT_WORDS
        qa, ka = [x[:, 0, :, :] for x in qk_rows], [x[:, 1, :, :] for x in qk_rows]
        raw = probs.rearrange("p a b c d -> p (a b c d)").rearrange("p (u s t) -> p u s t", u=2, s=2)
        rope_a, rope_b = raw[:, 0, 0, :], raw[:, 0, 1, :]
        attn, attnT = xn, xnT
        parts_d = nc.dram_tensor("parts_d", [2, 3, DM, TOK], BF16, kind="Internal").ap()
        max_d = nc.dram_tensor("max_d", [BATCH, 3, HEADS, SEQ], BF16, kind="Internal").ap()
        GROUPS = HEADS // 4
        T = {n: sem("att_" + n) for n in ["recip", "unit0", "unit1", "ang", "red", "sin", "w", "sw", "proj", "rope",
                    "part", "sent0", "sent1", "qk0", "qk1", "qk2", "A", "max", "mT", "mrow",
                    "msent", "mput", "B", "exp", "vpad", "pv", "o", "oT", "attn", "aT_ps", "aT",
                    "bout", "blank", "kp", "swp", "raw", "kv", "out", "X3", "setv"]}

        def att_sp_weights(sp):
            sp.dma_start(wq[:, :, :], a["L1_xattn_Wq"].rearrange("(k p) n -> p k n", p=P)).then_inc(T["w"], 16)
            sp.dma_start(wkv[:, :], a["L1_xattn_Wkv"]).then_inc(T["w"], 16)
            sp.dma_start(wout[:, :, :], a["L1_xattn_Wout"].rearrange("(k p) n -> p k n", p=P)).then_inc(T["w"], 16)

        def store_parts(sp, un):
            dst = parts_d[1 - un // 2, :, (un % 2) * P:(un % 2 + 1) * P, :].rearrange("i p t -> p i t")
            sp.dma_start(dst, parts[un % 2]).then_inc(T[f"sent{un % 2}"], 16)

        def load_rows(sp, b, k, unit=None):
            heads = slice(0, HEADS) if unit is None else slice(unit * HEADS // 2, (unit + 1) * HEADS // 2)
            done = T[f"qk{b % 3}"] if unit is None else T[f"unit{unit}"]
            for i in range(3):
                for j in range(3):
                    r = (3 * i + j) * HD
                    src = parts_d[k, j if k else i, heads.start * HD:heads.stop * HD, b * SEQ:(b + 1) * SEQ]
                    sp.dma_start(qk_rows[b % 3][r:r + HD, k, heads, :], src.rearrange("(h d) t -> d h t", d=HD)
                                 ).then_inc(done, 16)

        def ones_of(sp, slot):
            sp.dma_start(ka[slot][72:75, :, :], minus_one[:, :].unsqueeze(1).to_broadcast([3, HEADS, SEQ])
                         ).then_inc(T[f"qk{slot}"], 16)

        def keys_sp(sp):
            sp.dma_start(bout[:, :], a["L1_xattn_bout"].unsqueeze(0)).then_inc(T["bout"], 16)
            sp.wait_ge(T["part"], 6)
            for un in range(2):
                store_parts(sp, un)
            sp.wait_ge(T["blank"], 1)
            ones_of(sp, 0)
            sp.wait_ge(T["sent0"], 16)
            sp.wait_ge(T["sent1"], 16)
            load_rows(sp, 0, 1)

        def att_sp(sp):
            for un in range(2, 4):
                sp.wait_ge(T["part"], 3 * un + 3)
                store_parts(sp, un)
                sp.wait_ge(T[f"sent{un % 2}"], 32)
                load_rows(sp, 0, 0, un % 2)

            def put_max(b):
                sp.wait_ge(T["mrow"], b + 1)
                sp.dma_start(max_d[b].rearrange("i h t -> h i t"), m_parts).then_inc(T["msent"], 16)
                sp.wait_ge(T["msent"], 16 * (b + 1))
                sp.dma_start(qa[b % 3][72:75, :, :], max_d[b]).then_inc(T["mput"], 16)

            sp.wait_ge(T["blank"], 2)
            ones_of(sp, 1)
            load_rows(sp, 1, 0)
            load_rows(sp, 1, 1)
            put_max(0)
            sp.wait_ge(T["blank"], 3)
            ones_of(sp, 2)
            load_rows(sp, 2, 0)
            load_rows(sp, 2, 1)
            put_max(1)
            sp.wait_ge(T["B"], 2 * GROUPS)
            none = blank[0:3, :].bitcast(BF16)[:, 0:SEQ]
            sp.dma_start(qa[0][72:75, :, :], none.unsqueeze(1).to_broadcast([3, HEADS, SEQ])).then_inc(T["qk0"], 16)
            load_rows(sp, 3, 0)
            load_rows(sp, 3, 1)
            put_max(2)
            sp.wait_ge(T["B"], 4 * GROUPS)
            for e in range(2):
                load_expert(sp, e)
            put_max(3)

        def angles_pe(pe):
            pe.wait_ge(ld_pos, 16)
            for th in range(2):
                mm = nc.tensor.matmul(ps[:, th, :], freq[:, :], posT[:, th * 512:(th + 1) * 512], start=True, stop=True)
            mm.then_inc(T["ang"], 1)

        def kv_pe(pe):
            pe.wait_ge(T["sw"], 1)
            for k, w in enumerate([wkv[:, 0:P], wk_sw[:, 0:P], wkv[:, P:2 * P], wk_sw[:, P:2 * P]]):
                if k >= 2:
                    pe.wait_ge(T["raw"], k - 1)
                for th in range(2):
                    mm = nc.tensor.matmul(ps[:, 4 + 2 * (k % 2) + th, :], w, ctxT[:, th * 512:(th + 1) * 512],
                                          start=True, stop=True)
                mm.then_inc(T["kv"], 1)
            for k in range(2):
                pe.wait_ge(T["raw"], k + 3)
                for t in range(4):
                    mm = nc.tensor.matmul(ps[:, 4 + 2 * k + t // 2, (t % 2) * 256:(t % 2) * 256 + 256],
                                          ctxT[:, (4 * k + t) * P:(4 * k + t + 1) * P], wkv[:, DM:2 * DM],
                                          start=True, stop=True)
                mm.then_inc(T["kv"], 1)

        def angles_copy_act(act):
            act.wait_ge(T["ang"], 1)
            nc.scalar.copy(sin[:, :], ps[:, 0:2, :].rearrange("p a b -> p (a b)")).then_inc(T["red"], 1)

        def angles_abs_act(act):
            act.wait_ge(T["red"], 7)
            nc.scalar.activation(cos[:, :], sin[:, :], ACT.Abs).then_inc(T["sin"], 1)

        def angles_sin_act(act):
            nc.scalar.activation(sin[:, :], sin[:, :], ACT.Sin).then_inc(T["sin"], 1)
            act.wait_ge(T["red"], 8)
            nc.scalar.activation(cos[:, :], cos[:, :], ACT.Sin).then_inc(T["sin"], 1)

        def kv_act(act):
            for k in range(6):
                act.wait_ge(T["kv"], k + 1)
                dst = raw[:, k // 2, k % 2, :] if k < 4 else vv[:, 4 * (k - 4):4 * (k - 4) + 4, :].rearrange("p a b -> p (a b)")
                nc.scalar.copy(dst, ps[:, 4 + 2 * (k % 2):6 + 2 * (k % 2), :].rearrange("p a b -> p (a b)")
                               ).then_inc(T["raw"], 1)

        def angles_pool(pool):
            g = nc.gpsimd
            pool.wait_ge(T["w"], 48)
            for w, sw in ((wkv[:, 0:DM], wk_sw[:, :]), (wq.rearrange("p k n -> p (k n)"), wq_sw.rearrange("p k n -> p (k n)"))):
                src = w.rearrange("p (n two) -> p n two", two=2)
                dst = sw.rearrange("p (n two) -> p n two", two=2)
                g.tensor_scalar(dst[:, :, 0:1], src[:, :, 1:2], -1.0, None, ALU.mult).then_inc(T["swp"], 1)
                g.tensor_copy(dst[:, :, 1:2], src[:, :, 0:1]).then_inc(T["swp"], 1)
            pool.wait_ge(T["swp"], 4)
            pool.sem_inc(T["sw"], 1)
            pool.wait_ge(T["red"], 1)
            g.tensor_scalar(cos[:, :], sin[:, :], float(1.0 / TWO_PI), ROUND, ALU.mult, ALU.add).then_inc(T["red"], 1)
            pool.wait_ge(T["red"], 2)
            g.tensor_scalar(cos[:, :], cos[:, :], ROUND, -6.28125, ALU.subtract, ALU.mult).then_inc(T["red"], 1)
            pool.wait_ge(T["red"], 3)
            g.tensor_tensor(sin[:, :], sin[:, :], cos[:, :], ALU.add).then_inc(T["red"], 1)
            pool.wait_ge(T["red"], 4)
            g.tensor_scalar(cos[:, :], cos[:, :], float((TWO_PI - 6.28125) / 6.28125), None, ALU.mult).then_inc(T["red"], 1)
            pool.wait_ge(T["red"], 5)
            g.tensor_tensor(sin[:, :], sin[:, :], cos[:, :], ALU.add).then_inc(T["red"], 1)
            pool.wait_ge(T["red"], 6)
            g.tensor_scalar(sin[:, :], sin[:, :], 3.1415925, -3.1415925, ALU.min, ALU.max).then_inc(T["red"], 1)
            pool.wait_ge(T["sin"], 1)
            g.tensor_scalar(cos[:, :], cos[:, :], -1.0, float(np.pi / 2), ALU.mult, ALU.add).then_inc(T["red"], 1)

        def blank_rows(pool, slot):
            nc.gpsimd.memset(qk_rows[slot][64:P, :, :, :].rearrange("p a b c -> p (a b c)").bitcast(F32), 0.0
                             ).then_inc(T["blank"], 1)
            pool.wait_ge(T["blank"], slot + 1)

        def keys_pool(pool):
            g = nc.gpsimd
            g.memset(minus_one[:, :], -1.0).then_inc(T["kp"], 1)
            pool.wait_ge(T["sin"], 3)
            for un in range(2):
                ra, rb, pr = raw[:, un, 0, :], raw[:, un, 1, :], parts[un]
                pool.wait_ge(T["raw"], 2 * un + 2)
                g.tensor_tensor(ra, ra, cos[:, :], ALU.mult).then_inc(T["kp"], 1)
                g.tensor_tensor(rb, rb, sin[:, :], ALU.mult).then_inc(T["kp"], 1)
                pool.wait_ge(T["kp"], 7 * un + 3)
                g.tensor_tensor(ra, ra, rb, ALU.add).then_inc(T["kp"], 1)
                pool.wait_ge(T["kp"], 7 * un + 4)
                g.tensor_copy(pr[:, 0, :], ra).then_inc(T["kp"], 1)
                pool.wait_ge(T["kp"], 7 * un + 5)
                g.tensor_tensor(rb, ra, pr[:, 0, :], ALU.subtract).then_inc(T["kp"], 1)
                pool.wait_ge(T["kp"], 7 * un + 6)
                g.tensor_copy(pr[:, 1, :], rb).then_inc(T["kp"], 1)
                pool.wait_ge(T["kp"], 7 * un + 7)
                g.tensor_tensor(pr[:, 2, :], rb, pr[:, 1, :], ALU.subtract).then_inc(T["kp"], 1)
            pool.wait_ge(T["kp"], 15)
            pool.sem_inc(T["part"], 6)
            blank_rows(pool, 0)

        def att_pe(pe):
            for un in range(2, 4):
                base, c = 4 * (un % 2), un % 2
                pe.wait_ge(L["xnT"], 8)
                for k, w in enumerate([wq, wq_sw]):
                    for th in range(2):
                        for kk in range(2):
                            mm = nc.tensor.matmul(ps[:, base + 2 * k + th, :], w[:, kk, c * P:(c + 1) * P],
                                                  xnT[:, kk, th * 512:(th + 1) * 512], start=(kk == 0), stop=(kk == 1))
                    mm.then_inc(T["proj"], 1)
            pe.wait_ge(T["rope"], 2)

            def A(b, hd, par, n):
                pe.wait_ge(T["max"], n + 1)
                for qt in range(2):
                    mm = nc.tensor.matmul(ps[:, par, qt * 256:(qt + 1) * 256],
                                          one(qa[b % 3][:, :, qt * P:(qt + 1) * P], hd),
                                          one(ka[b % 3][:, :, :], hd), start=True, stop=True)
                mm.then_inc(T["A"], 1)

            def B(b, hd, pair, n, js=(0, 1)):
                if js[0] == 0:
                    pe.wait_ge(T["exp"], n + 1)
                for j in js:
                    for kc in range(2):
                        mm = nc.tensor.matmul(ps[:, 2 + 2 * pair + j, kc * 256:(kc + 1) * 256],
                                              one(ka[b % 3][:, :, kc * P:(kc + 1) * P], hd + j),
                                              one(qa[b % 3][:, :, :], hd + j), start=True, stop=True)
                if js[-1] == 1:
                    mm.then_inc(T["B"], 1)

            def PV(s, G, kc):
                if kc == 0:
                    pe.wait_ge(T["exp"], 2 * G + 2 + 2)
                    pe.wait_ge(T["vpad"], G + 1)
                    pe.wait_ge(T["o"], G + 1)
                for j in range(4):
                    mm = nc.tensor.matmul(ps[32 * j:32 * j + 32, 6, 0:256], v_pad[:, s, kc, j, :],
                                          probs[:, 2 * s + j // 2, j % 2, kc, :], start=(kc == 0), stop=(kc == 1),
                                          skip_group_check=True)
                if kc == 1:
                    mm.then_inc(T["pv"], 1)

            def max_rows(b):
                pe.wait_ge(T["max"], HEADS * (b + 1) + 2)
                for qt in range(2):
                    mm = nc.tensor.transpose(ps[0:32, 7, qt * P:(qt + 1) * P], mx[:, b % 2, qt, :], ident[:, :])
                mm.then_inc(T["mT"], 1)

            def outputs(n, maxima=0):
                pe.wait_ge(T["o"], 2 * n + 2 + 1)
                pe.wait_ge(T["attn"], n + 1)
                if maxima:
                    pe.wait_ge(T["mrow"], maxima)
                for qt in range(2):
                    for k in range(2):
                        mm = nc.tensor.transpose(ps[:, 7, (2 * qt + k) * P:(2 * qt + k + 1) * P],
                                                 o_rows[:, k, qt * P:(qt + 1) * P], ident[:, :])
                mm.then_inc(T["oT"], 1)

            def turn(b, i, ahead, at, last):
                for s in range(2):
                    G = 8 * b + 2 * i + s
                    g = 2 * i + s
                    for p in range(2):
                        for j in range(2):
                            if ahead < BATCH:
                                hd = 4 * (at + s) + 2 * p + j
                                A(ahead, hd, j, HEADS * ahead + hd)
                            if not (last and s == 1):
                                B(b, 4 * g + 4 + 2 * p, p, 2 * G + 2 + p, [j])
                        PV(s, G, p)
                    if s == 0 and not (isinstance(i, int) and 4 * b + i == 0):
                        outputs(4 * b + i - 1, b + 2 if last and b + 1 < BATCH else 0)

            pe.sem_inc(T["pv"], 2)
            pe.wait_ge(T["qk0"], 16 * 10)
            for unit in range(2):
                pe.wait_ge(T[f"unit{unit}"], 16 * 9)
                with pe.Fori(unit * HEADS // 4, (unit + 1) * HEADS // 4) as i:
                    for j in range(2):
                        A(0, 2 * i + j, j, 2 * i + j)
            pe.wait_ge(T["rope"], 4)
            max_rows(0)
            pe.wait_ge(T["qk1"], 16 * 19)
            for hd in range(8):
                A(1, hd, hd % 2, HEADS + hd)
            pe.wait_ge(T["mput"], 16)
            for p in range(2):
                B(0, 2 * p, p, p)
            for b in range(BATCH):
                turn(b, 0, b + 1, 2, False)
                with pe.Fori(1, GROUPS // 2 - 1) as i:
                    turn(b, i, b + 1, 2 * i + 2, False)
                if b + 1 < BATCH:
                    pe.wait_ge(T["attn"], 4 * b + 2 + 1)
                    max_rows(b + 1)
                if b + 2 < BATCH:
                    pe.wait_ge(T[f"qk{(b + 2) % 3}"], 16 * (19 + 10 * ((b + 2) // 3)))
                turn(b, GROUPS // 2 - 1, b + 2, 0, True)
                if b + 1 < BATCH:
                    pe.wait_ge(T["mput"], 16 * (b + 2))
                    for p in range(2):
                        B(b + 1, 2 * p, p, 16 * (b + 1) + p)
            outputs(BATCH * GROUPS // 2 - 1)
            pe.wait_ge(T["bout"], 16)
            for th in range(2):
                for c in range(2):
                    pe.wait_ge(T["attn"], 16 + 1)
                    for q in range(4):
                        mm = nc.tensor.transpose(ps[:, 2 * th + c, q * P:(q + 1) * P], attn[:, 4 * th + q, c * P:(c + 1) * P],
                                                 ident[:, :])
                    mm.then_inc(T["aT_ps"], 1)
            for t in range(NT):
                pe.wait_ge(T["aT"], 2 * (t // 4) + 2)
                o = ps[:, 4 + (t // 2) % 2 + 2 * (t // 4), (t % 2) * 256:(t % 2) * 256 + 256]
                for c in range(2):
                    nc.tensor.matmul(o, attnT[:, c, t * P:(t + 1) * P], wout[:, c, :], start=(c == 0), stop=False)
                mm = nc.tensor.matmul(o, ones_row[:, :], bout[:, :], start=False, stop=True)
                if t % 2:
                    mm.then_inc(T["out"], 1)

        def one(view, hd):
            if isinstance(hd, int):
                return view[:, hd, :]
            return view[:, bass.ds(hd, 1), :].rearrange("r o n -> r (o n)")

        def att_act(act):
            nc.scalar.preload_act_table(ACT.Exp)
            act.sem_inc(T["exp"], 2)
            act.sem_inc(T["o"], 1)

            def exps(s, G):
                for p in range(2):
                    act.wait_ge(T["B"], 2 * G + p + 1)
                    act.wait_ge(T["pv"], G + 1)
                    nc.scalar.activation(probs[:, 2 * s + p, :, :, :].rearrange("p a b c -> p (a b c)"),
                                         ps[:, 2 + 2 * p:4 + 2 * p, :].rearrange("p a b -> p (a b)"), ACT.Exp,
                                         scale=float(1.0 / np.sqrt(np.float32(HD)))).then_inc(T["exp"], 1)

            def evac(s, G):
                act.wait_ge(T["pv"], G + 1 + 2)
                nc.scalar.copy(o_rows[:, s, :], ps[:, 6, 0:256]).then_inc(T["o"], 1)

            def turn(b, i, last):
                for s in range(2):
                    if not (last and s == 1):
                        exps((s + 1) % 2, 8 * b + 2 * i + s + 1)
                    if s == 0 and not (isinstance(i, int) and 4 * b + i == 0):
                        act.wait_ge(T["oT"], 4 * b + i)
                    evac(s, 8 * b + 2 * i + s)

            for b in range(BATCH):
                exps(0, 8 * b)
                turn(b, 0, False)
                with act.Fori(1, GROUPS // 2 - 1) as i:
                    turn(b, i, False)
                turn(b, GROUPS // 2 - 1, True)
            for k in range(4):
                act.wait_ge(T["aT_ps"], k + 1)
                th, c = k // 2, k % 2
                nc.scalar.copy(attnT[:, c, th * 512:(th + 1) * 512], ps[:, k, :]).then_inc(T["aT"], 1)

        def att_dve(dve):
            v = nc.vector
            dve.wait_ge(T["sin"], 3)
            dve.sem_inc(T["max"], 2)
            dve.wait_ge(T["part"], 6)
            for un in range(2, 4):
                base = 4 * (un % 2)
                pr = parts[un % 2]
                dve.wait_ge(T["proj"], 2 * un - 3)
                v.tensor_tensor(
                    rope_a, ps[:, base:base + 2, :].rearrange("p a b -> p (a b)"), cos[:, :], ALU.mult).then_inc(T["rope"], 1)
                dve.wait_ge(T["proj"], 2 * un - 2)
                v.tensor_tensor(rope_b, ps[:, base + 2:base + 4, :].rearrange("p a b -> p (a b)"), sin[:, :],
                                ALU.mult).then_inc(T["rope"], 1)
                dve.wait_ge(T["rope"], 2 * un - 2)
                then(dve, v.tensor_tensor(rope_a, rope_a, rope_b, ALU.add))
                dve.wait_ge(T[f"sent{un % 2}"], 16)
                v.tensor_copy(pr[:, 0, :], rope_a).then_inc(T["part"], 1)
                dve.wait_ge(T["part"], 3 * un + 1)
                then(dve, v.tensor_tensor(rope_b, rope_a, pr[:, 0, :], ALU.subtract))
                v.tensor_copy(pr[:, 1, :], rope_b).then_inc(T["part"], 1)
                dve.wait_ge(T["part"], 3 * un + 2)
                v.tensor_tensor(pr[:, 2, :], rope_b, pr[:, 1, :], ALU.subtract).then_inc(T["part"], 1)
                dve.wait_ge(T["part"], 3 * un + 3)

            def head_max(slot, hd, par, n):
                dve.wait_ge(T["A"], n + 1)
                at = slice(hd, hd + 1) if isinstance(hd, int) else bass.ds(hd, 1)
                v.tensor_reduce(mx[:, slot, :, at].rearrange("p a o -> p (a o)"),
                                ps[:, par, :].rearrange("p (a k) -> p a k", a=2), AX.X, ALU.max).then_inc(T["max"], 1)

            def max_split(b):
                dve.wait_ge(T["mT"], b + 1)
                if b:
                    dve.wait_ge(T["msent"], 16 * b)
                then(dve, v.tensor_copy(m_rest[:, 0, :], ps[0:32, 7, 0:256]))
                then(dve, v.tensor_copy(m_parts[:, 0, :], m_rest[:, 0, :]))
                then(dve, v.tensor_tensor(m_rest[:, 1, :], m_rest[:, 0, :], m_parts[:, 0, :], ALU.subtract))
                then(dve, v.tensor_copy(m_parts[:, 1, :], m_rest[:, 1, :]))
                v.tensor_tensor(m_parts[:, 2, :], m_rest[:, 1, :], m_parts[:, 1, :], ALU.subtract).then_inc(T["mrow"], 1)

            with dve.Fori(0, HEADS // 2) as i:
                for j in range(2):
                    head_max(0, 2 * i + j, j, 2 * i + j)
            max_split(0)
            def outputs(b, gg):
                dve.wait_ge(T["oT"], 4 * b + gg + 1)
                dve.wait_ge(T["attn"], 4 * b + gg + 1)
                o = ps[:, 7, :].rearrange("p (m c) -> p m c", c=32)
                v.reciprocal(recip16, o[:, :, HD:HD + 1]).then_inc(T["recip"], 1)
                dve.wait_ge(T["recip"], 4 * b + gg + 1)
                cols = slice(64 * gg, 64 * gg + 64) if isinstance(gg, int) else bass.ds(64 * gg, 64)
                for qt in range(2):
                    dst = attn[:, 2 * b + qt, cols].rearrange("p (m c) -> p m c", c=HD)
                    ins = v.tensor_tensor(dst, o[:, 8 * qt:8 * qt + 8, 0:HD],
                                          recip16[:, 8 * qt:8 * qt + 8, :].to_broadcast([P, 8, HD]), ALU.mult)
                ins.then_inc(T["attn"], 1)

            def turn(b, i, ahead, at):
                for half in range(2):
                    if ahead < BATCH:
                        for hd in range(4):
                            k = 4 * half + hd
                            head_max(ahead % 2, at + k, hd % 2, HEADS * ahead + at + k)
                    if half == 0:
                        if not isinstance(i, int) or i:
                            outputs(b, i - 1)
                        elif b:
                            outputs(b - 1, GROUPS // 2 - 1)

            dve.sem_inc(T["attn"], 1)
            for hd in range(8):
                head_max(1, hd, hd % 2, HEADS + hd)
            for b in range(BATCH):
                turn(b, 0, b + 1, 8)
                with dve.Fori(1, GROUPS // 2 - 1) as i:
                    turn(b, i, b + 1, 8 * i + 8)
                if b + 1 < BATCH:
                    max_split(b + 1)
                turn(b, GROUPS // 2 - 1, b + 2, 0)
            outputs(BATCH - 1, GROUPS // 2 - 1)
            for t in range(NT):
                dve.wait_ge(T["out"], t // 2 + 1)
                o = ps[:, 4 + (t // 2) % 2 + 2 * (t // 4), (t % 2) * 256:(t % 2) * 256 + 256]
                v.scalar_tensor_tensor(X[:, t, :], o, tg[:, 1:2], X[:, t, :], ALU.mult, ALU.add).then_inc(T["X3"], 1)
                if t % 2:
                    dve.wait_ge(T["X3"], t + 1)
                    ln_tile_stats(dve, range(t - 1, t + 1))

        def att_pool(pool):
            g = nc.gpsimd
            g.memset(v_pad.rearrange("p a b c d -> p (a b c d)"), 0.0).then_inc(T["setv"], 1)
            pool.wait_ge(T["setv"], 1)
            g.memset(v_pad[:, :, :, :, HD:HD + 1].rearrange("p a b c d -> p (a b c) d"), 1.0).then_inc(T["setv"], 1)
            pool.wait_ge(T["setv"], 2)
            pool.wait_ge(T["raw"], 6)
            for b in range(BATCH):
                with pool.Fori(0, GROUPS // 2) as i:
                    for s in range(2):
                        pool.wait_ge(T["pv"], 8 * b + 2 * i + s + 1)
                        src = vv[:, 2 * b:2 * b + 2, bass.ds(32 * (2 * i + s), 32)]
                        for kc in range(2):
                            ins = g.tensor_copy(v_pad[:, s, kc, :, 0:HD], src[:, kc, :].rearrange("p (h d) -> p h d", d=HD))
                            if kc == 0:
                                ins.then_inc(T["setv"], 1)
                        ins.then_inc(T["vpad"], 1)


        r2 = Region()
        w_sb = r2("w_sb", [P, EXPERTS, 2, 2 * F1])
        r2 = Region(0, arena_high)
        router1 = r2("router1", [P, 2, EXPERTS])
        gate_b = r2("gate_b", [1, EXPERTS])
        b2_sb = r2("b2_sb", [EXPERTS, DM])
        b1_rows = r2("b1_rows", [EXPERTS * F1 // P, P])
        b1_sb = r2("b1_sb", [P, EXPERTS, F1 // P])
        lower = r2("lower", [P, P])
        lower_b = r2("lower_b", [P, P], BF16)
        ones = r2("ones", [P, P], BF16)
        numbers = r2("numbers", [P, P + 2 + 4 * NT])
        count_up, part_no, spare_row = numbers[:, 0:P], numbers[:, P:P + 1], numbers[:, P + 1:P + 2]
        code_no, tile_of = numbers[:, P + 2:P + 2 + 2 * NT], numbers[:, P + 2 + 2 * NT:P + 2 + 4 * NT]
        combT = r2("combT", [EXPERTS, TOK])
        soft = r2("soft", [P, 2, NT, EXPERTS])
        chosen = r2("chosen", [P, NT + 1, EXPERTS], BF16)
        place = r2("place", [P, NT + 1, EXPERTS])
        masked = r2("masked", [P, 2, NT, EXPERTS])
        hit = r2("hit", [P, 2, NT, EXPERTS])
        tiles = r2("tiles", [P, EXPERTS])
        in_front = r2("in_front", [P, EXPERTS, EXPERTS])
        first = r2("first", [P, EXPERTS])
        base = r2("base", [P, EXPERTS])
        slot_f = r2("slot_f", [P, 2, NT])
        slot_hi = r2("slot_hi", [P, 2, NT])
        slot_lo = r2("slot_lo", [P, 2, NT])
        at_lo = r2("at_lo", [P, 2 * NT, P], BF16)
        at_hi = r2("at_hi", [P, 2 * NT, SLOT_TILES + 1])
        what = r2("what", [P, 2 * NT, 3, SLOT_TILES + 1], BF16)
        found = r2("found", [P, 3, SLOT_TILES + 1])
        goes_f = r2("goes_f", [P, 2, SLOT_TILES + 1])
        token_i = r2("token_i", [P, SLOT_TILES + 1], mybir.dt.int32)
        goes_i = r2("goes_i", [P, SLOT_TILES + 1], mybir.dt.int32)
        pair_w = r2("pair_w", [P, 2, NT])
        reached = r2("reached", [1, SLOT_TILES, EXPERTS])
        owner_f = r2("owner_f", [1, SLOT_TILES])
        owner = r2("owner", [1, SLOT_TILES], mybir.dt.int32)
        xt_in = r2("xt_in", [P, 2, DM])
        pre = r2("pre", [P, F1])
        h1 = r2("h1", [P, F1 // P, P])
        y_sb = r2("y_sb", [P, DM])
        blank = sb("blank", [P, DM])
        got = [xn[:, :, :], xnT.rearrange("p k n -> p (k n)").rearrange("p (c d) -> p c d", c=NT)]
        xn_d = nc.dram_tensor("xn_d", [TOK, DM], F32, kind="Internal").ap()
        y_d = nc.dram_tensor("y_d", [2 * TOK + P, DM], F32, kind="Internal").ap()
        NONE = 4096.0
        HF = F1 // P
        N = {n: sem("moe1_" + n) for n in ["xn_d", "what", "found_ps", "small", "lg", "sub", "exp", "comb", "cT_ps", "cT",
                    "bias", "acc", "blank", "chosen", "place_ps", "slots", "owner", "w_ready",
                    "xin0", "xin1", "xt_ps", "xt", "up", "pre", "hT", "hb", "h", "dn", "y", "y_out"] +
             [f"w{e}" for e in range(EXPERTS)] + [f"got{k}" for k in range(4)]}

        def load_expert(sp, e):
            for k, (n, rows_of) in enumerate([("L1_ffn_w1", 2), ("L1_ffn_w2", F1 // P)]):
                sp.dma_start(w_sb[:, e, k, :].rearrange("p (k f) -> p k f", k=rows_of),
                             a[n][e].rearrange("(k p) f -> p k f", p=P)).then_inc(N[f"w{e}"], 16)

        def moe1_sp(sp):
            sp.wait_ge(T["B"], 6 * GROUPS)
            sp.dma_start(router1[:, :, :], a["L1_ffn_gate_w"].rearrange("(k p) e -> p k e", p=P)).then_inc(N["small"], 16)
            sp.dma_start(gate_b[:, :], a["L1_ffn_gate_b"].unsqueeze(0)).then_inc(N["small"], 16)
            sp.dma_start(b2_sb[:, :], a["L1_ffn_b2"]).then_inc(N["small"], 16)
            sp.dma_start(b1_rows[:, :], a["L1_ffn_b1"].rearrange("e (f p) -> (e f) p", p=P)).then_inc(N["small"], 16)
            sp.dma_start(lower[:, :], a["lower"]).then_inc(N["small"], 16)
            sp.dma_start(numbers[:, :], a["numbers"]).then_inc(N["small"], 16)
            sp.wait_ge(L["xn"], 4 * NT)
            sp.dma_start(xn_d.rearrange("(t p) d -> p t d", p=P), xn[:, :, :]).then_inc(N["xn_d"], 16)
            for e in range(2, 4):
                load_expert(sp, e)

            def ready(e):
                sp.wait_ge(N[f"w{e}"], 32)
                sp.sem_inc(N["w_ready"], 1)

            ready(0)
            for e in range(4, EXPERTS):
                ready(e - 3)
                sp.wait_ge(N["xt_ps"], e - 2)
                load_expert(sp, e)
            for e in range(EXPERTS - 3, EXPERTS):
                ready(e)
            sp.sem_inc(N["w_ready"], SLOT_TILES - EXPERTS)
            sp.wait_ge(N["y_out"], 16 * SLOT_TILES)
            rows_of = y_d[0:2 * TOK, :].rearrange("(c p) d -> p c d", p=P)
            for k in range(4):
                sp.dma_start(got[k // 2][:, 4 * (k % 2):4 * (k % 2) + 4, :], rows_of[:, 4 * k:4 * k + 4, :]
                             ).then_inc(N[f"got{k}"], 16)

        def gate1_pe(pe):
            pe.wait_ge(N["small"], 96)
            pe.wait_ge(L["xnT"], 8 + 1)
            nc.tensor.transpose(ps[:, 7, 128:192], b1_rows[:, :], ident[0:64, 0:64])
            nc.tensor.matmul(ps[:, 7, 0:NT * EXPERTS].rearrange("p (t e) -> p t e", e=EXPERTS), ones_row[:, :],
                             gate_b[:, :].unsqueeze(1).to_broadcast([1, NT, EXPERTS]), start=True, stop=False,
                             skip_group_check=True)
            for t in range(NT):
                if t % 4 == 0:
                    pe.wait_ge(L["xnT"], 8 + 2 * (t // 4) + 2)
                for c in range(2):
                    mm = nc.tensor.matmul(ps[:, 7, t * EXPERTS:(t + 1) * EXPERTS], xnT[:, c, t * P:(t + 1) * P],
                                          router1[:, c, :], start=False, stop=(c == 1), skip_group_check=True)
            mm.then_inc(N["lg"], 1)
            pe.wait_ge(N["chosen"], 2)
            nc.tensor.matmul(ps[:, 5, 0:(NT + 1) * EXPERTS], lower_b[:, :], chosen[:, :, :].rearrange("p t e -> p (t e)"),
                             start=True, stop=False, skip_group_check=True)
            for t in range(NT):
                mm = nc.tensor.matmul(ps[:, 5, (t + 1) * EXPERTS:(NT + 1) * EXPERTS].rearrange("p (t e) -> p t e", e=EXPERTS),
                                      ones[:, :], chosen[:, t:t + 1, :].to_broadcast([P, NT - t, EXPERTS]),
                                      start=False, stop=(t == NT - 1), skip_group_check=True)
            mm.then_inc(N["place_ps"], 1)
            pe.wait_ge(N["what"], 1)
            for c in range(2 * NT):
                mm = nc.tensor.matmul(ps[:, 4, 0:3 * (SLOT_TILES + 1)], at_lo[:, c, :],
                                      what[:, c, :, :].rearrange("p g n -> p (g n)"), start=(c == 0), stop=(c == 2 * NT - 1))
            mm.then_inc(N["found_ps"], 1)

        def gate1_act(act):
            nc.scalar.preload_act_table(ACT.Exp)
            act.wait_ge(N["sub"], 1)
            nc.scalar.activation(soft[:, 1, :, :], soft[:, 0, :, :], ACT.Exp).then_inc(N["exp"], 1)

        def gate1_dve(dve):
            v = nc.vector
            lg, ex = (soft[:, k, :, :] for k in range(2))
            msk = chosen[:, 0:NT, :]
            v.memset(ones[:, :], 1.0).then_inc(N["chosen"], 1)
            link(v.memset(chosen[:, NT, :], 0.0))
            dve.wait_ge(N["lg"], 1)
            link(v.tensor_copy(lower_b[:, :], lower[:, :]))
            then(dve, v.tensor_copy(lg, ps[:, 7, 0:NT * EXPERTS].rearrange("p (t e) -> p t e", t=NT)))
            then(dve, v.tensor_reduce(per_tile[:, 0, :], lg, AX.X, ALU.max))
            v.tensor_tensor(lg, lg, by_tile(0), ALU.subtract).then_inc(N["sub"], 1)
            dve.wait_ge(N["exp"], 1)
            then(dve, v.tensor_reduce(per_tile[:, 0, :], ex, AX.X, ALU.add))
            then(dve, v.reciprocal(per_tile[:, 1, :], per_tile[:, 0, :]))
            then(dve, v.tensor_tensor(ex, ex, by_tile(1), ALU.mult))
            top2(dve, ex, msk)
            dve.sem_inc(N["chosen"], 1)
            then(dve, v.tensor_tensor(ex, ex, msk, ALU.mult))
            then(dve, v.tensor_reduce(per_tile[:, 2, :], ex, AX.X, ALU.add))
            then(dve, v.reciprocal(per_tile[:, 3, :], per_tile[:, 2, :]))
            then(dve, v.tensor_scalar(per_tile[:, 3, :], per_tile[:, 3, :], tg[:, 3:4], None, ALU.mult))
            link(v.tensor_tensor(comb[:, :, :], ex, by_tile(3), ALU.mult))
            dve.wait_ge(N["place_ps"], 1)
            then(dve, v.tensor_copy(place[:, :, :], ps[:, 5, 0:(NT + 1) * EXPERTS].rearrange("p (t e) -> p t e", e=EXPERTS)))
            then(dve, v.tensor_scalar(tiles[:, :], place[:, NT, :], 1.0 / P, 63.5 / P, ALU.mult, ALU.add))
            then(dve, v.tensor_scalar(tiles[:, :], tiles[:, :], ROUND, None, ALU.add))
            then(dve, v.tensor_scalar(tiles[:, :], tiles[:, :], ROUND, 1.0, ALU.subtract, ALU.max))
            then(dve, v.tensor_tensor(in_front[:, :, :], before[:, :, :],
                                      tiles[:, :].unsqueeze(1).to_broadcast([P, EXPERTS, EXPERTS]), ALU.mult))
            then(dve, v.tensor_reduce(first[:, :], in_front[:, :, :], AX.X, ALU.add))
            then(dve, v.tensor_scalar(base[:, :], first[:, :], float(P), None, ALU.mult))
            then(dve, v.tensor_tensor(place[:, 0:NT, :], place[:, 0:NT, :],
                                      base[:, :].unsqueeze(1).to_broadcast([P, NT, EXPERTS]), ALU.add))
            link(v.scalar_tensor_tensor(masked[:, 0, :, :], place[:, 0:NT, :], NONE, msk, ALU.subtract, ALU.mult))
            then(dve, v.tensor_tensor(masked[:, 1, :, :], place[:, 0:NT, :], msk, ALU.mult))
            link(v.tensor_reduce(slot_f[:, 0, :], masked[:, 0, :, :], AX.X, ALU.min))
            then(dve, v.tensor_reduce(slot_f[:, 1, :], masked[:, 1, :, :], AX.X, ALU.max))
            then(dve, v.tensor_scalar(slot_f[:, 0, :], slot_f[:, 0, :], NONE, None, ALU.add))
            then(dve, v.tensor_scalar(slot_hi[:, :, :], slot_f[:, :, :], 1.0 / P, -63.5 / P, ALU.mult, ALU.add))
            then(dve, v.tensor_scalar(slot_hi[:, :, :], slot_hi[:, :, :], ROUND, None, ALU.add))
            then(dve, v.tensor_scalar(slot_hi[:, :, :], slot_hi[:, :, :], ROUND, None, ALU.subtract))
            link(v.scalar_tensor_tensor(slot_lo[:, :, :], slot_hi[:, :, :], -float(P), slot_f[:, :, :], ALU.mult, ALU.add))
            tiles_up = SLOT_TILES + 1
            hi_all = slot_hi[:, :, :].rearrange("p k t -> p (k t)").unsqueeze(2).to_broadcast([P, 2 * NT, tiles_up])
            then(dve, v.tensor_tensor(at_hi[:, :, :], hi_all,
                                      count_up[:, 0:tiles_up].unsqueeze(1).to_broadcast([P, 2 * NT, tiles_up]), ALU.is_equal))
            lo_all = slot_lo[:, :, :].rearrange("p k t -> p (k t)")
            link(v.tensor_scalar(what[:, :, 0, :], at_hi[:, :, :], part_no, None, ALU.mult))
            for g, by in ((1, code_no), (2, tile_of)):
                link(v.tensor_tensor(what[:, :, g, :], at_hi[:, :, :],
                                     by.unsqueeze(2).to_broadcast([P, 2 * NT, tiles_up]), ALU.mult))
            for k in range(2):
                link(v.tensor_tensor(at_lo[:, k * NT:(k + 1) * NT, :], lo_all[:, k * NT:(k + 1) * NT].unsqueeze(2).to_broadcast([P, NT, P]),
                                     count_up.unsqueeze(1).to_broadcast([P, NT, P]), ALU.is_equal))
            dve.wait_ge(dve_order, step_count[0])
            dve.sem_inc(N["what"], 1)
            then(dve, v.tensor_tensor(reached[:, :, :], first[0:1, :].unsqueeze(1).to_broadcast([1, SLOT_TILES, EXPERTS]),
                                      count_up[0:1, 0:SLOT_TILES].unsqueeze(2).to_broadcast([1, SLOT_TILES, EXPERTS]),
                                      ALU.is_le))
            then(dve, v.tensor_reduce(owner_f[:, :], reached[:, :, :], AX.X, ALU.add))
            then(dve, v.tensor_scalar(owner[:, :], owner_f[:, :], -1.0, None, ALU.add))
            dve.sem_inc(N["owner"], 1)
            dve.wait_ge(N["found_ps"], 1)
            then(dve, v.tensor_copy(found[:, :, :], ps[:, 4, 0:3 * tiles_up].rearrange("p (g n) -> p g n", g=3)))
            link(v.scalar_tensor_tensor(goes_f[:, 0, :], found[:, 2, :], float(P), found[:, 0, :], ALU.mult, ALU.add))
            link(v.tensor_scalar(goes_f[:, 1, :], found[:, 1, :], 0.0, spare_row, ALU.is_equal, ALU.mult))
            then(dve, v.scalar_tensor_tensor(found[:, 1, :], found[:, 1, :], float(P), found[:, 0, :], ALU.mult, ALU.add))
            link(v.tensor_copy(token_i[:, :], goes_f[:, 0, :]))
            then(dve, v.scalar_tensor_tensor(goes_i[:, :], found[:, 1, :], -float(P), goes_f[:, 1, :], ALU.add, ALU.add))
            dve.sem_inc(N["slots"], 1)
            for k in range(2):
                link(v.scalar_tensor_tensor(hit[:, k, :, :], masked[:, k, :, :], NONE * (1 - k),
                                            slot_f[:, k, :].unsqueeze(2).to_broadcast([P, NT, EXPERTS]),
                                            ALU.add, ALU.is_equal))
            dve.wait_ge(dve_order, step_count[0])
            for k in range(2):
                link(v.tensor_tensor(hit[:, k, :, :], hit[:, k, :, :], comb[:, :, :], ALU.mult))
            dve.wait_ge(dve_order, step_count[0])
            for k in range(2):
                link(v.tensor_reduce(pair_w[:, k, :], hit[:, k, :, :], AX.X, ALU.add))
            link(v.tensor_copy(b1_sb[:, :, :].rearrange("p e f -> p (e f)"), ps[:, 7, 128:192]))
            dve.wait_ge(dve_order, step_count[0])
            dve.sem_inc(N["comb"], 1)

        def bias_pe(pe):
            pe.wait_ge(N["comb"], 1)
            pe.wait_ge(N["y"], SLOT_TILES)
            pe.wait_ge(N["xt"], SLOT_TILES)
            for t in range(NT):
                mm = nc.tensor.transpose(ps[0:EXPERTS, 4 + t // 4, (t % 4) * P:(t % 4 + 1) * P], comb[:, t, :], ident[:, :])
            mm.then_inc(N["cT_ps"], 1)
            pe.wait_ge(N["cT"], 2)
            for t in range(NT):
                mm = nc.tensor.matmul(ps[:, 4 + t // 2, (t % 2) * 256:(t % 2) * 256 + 256], combT[:, t * P:(t + 1) * P],
                                      b2_sb[:, :], start=True, stop=True)
            mm.then_inc(N["bias"], 1)

        def bias_dve(dve):
            dve.wait_ge(N["bias"], 1)
            for t in range(NT):
                nc.vector.tensor_tensor(X[:, t, :], X[:, t, :], ps[:, 4 + t // 2, (t % 2) * 256:(t % 2) * 256 + 256],
                                        ALU.add).then_inc(N["acc"], 1)

        def bias_act(act):
            act.wait_ge(N["cT_ps"], 1)
            for k in range(2):
                nc.scalar.copy(combT[:, k * 512:(k + 1) * 512], ps[0:EXPERTS, 4 + k, :]).then_inc(N["cT"], 1)

        def moe1_pool(pool):
            def gather(i):
                nc.gpsimd.indirect_dma_start(xt_in[:, i % 2, :], None, xn_d[:, :],
                                             bass.IndirectOffsetOnAxis(ap=token_i[:, i:i + 1], axis=0)
                                             ).then_inc(N[f"xin{i % 2}"], 16)

            pool.wait_ge(N["xn_d"], 16)
            pool.wait_ge(N["slots"], 1)
            gather(0)
            gather(1)
            for i in range(2, 4):
                pool.wait_ge(N["xt_ps"], i - 1)
                gather(i)
            for i in range(SLOT_TILES):
                if i + 4 < SLOT_TILES:
                    pool.wait_ge(N["xt_ps"], i + 3)
                    gather(i + 4)
                pool.wait_ge(N["y"], i + 1)
                nc.gpsimd.indirect_dma_start(y_d[:, :], bass.IndirectOffsetOnAxis(ap=goes_i[:, i:i + 1], axis=0),
                                             y_sb[:, :], None).then_inc(N["y_out"], 16)

        def expert_of(tile, engine):
            return nc.values_load(owner[:, tile:tile + 1] if isinstance(tile, int) else owner[:, bass.ds(tile, 1)],
                                  engines=[engine], min_val=0, max_val=EXPERTS - 1,
                                  skip_runtime_bounds_check_because="a count of the experts, from 1, less one")

        def moe1_pe(pe):
            def rows_in(pair, slot):
                pe.wait_ge(N[f"xin{slot}"], 16 * pair + 16)
                for c in range(2):
                    mm = nc.tensor.transpose(ps[:, 6, c * P:(c + 1) * P], xt_in[:, slot, c * P:(c + 1) * P], ident[:, :])
                mm.then_inc(N["xt_ps"], 1)

            def up(i):
                pe.wait_ge(N["xt"], i + 1)
                parts = [(x, w, c) for x, w in ((0, 0), (0, 1), (1, 0)) for c in range(2)]
                for half in range(2):
                    pe.wait_ge(M["w_lo"], EXPERTS + 2 * i + half + 1)
                    for k, (x, w, c) in enumerate(parts):
                        mm = nc.tensor.matmul(ps[:, half, :], xt_r[:, x, c, :], up_r[:, w, c, half * 512:(half + 1) * 512],
                                              start=(k == 0), stop=(k == len(parts) - 1))
                    mm.then_inc(N["up"], 1)

            def turn_hidden(i):
                for half in range(2):
                    pe.wait_ge(N["pre"], 2 * i + half + 1)
                    for q in range(4):
                        f = 4 * half + q
                        mm = nc.tensor.transpose(ps[:, 2 + half, q * P:(q + 1) * P], pre[:, f * P:(f + 1) * P], ident[:, :])
                    mm.then_inc(N["hT"], 1)

            def down(i, e):
                pe.wait_ge(N["h"], 2 * i + 2)
                for f in range(HF):
                    mm = nc.tensor.matmul(ps[:, 4, 0:DM], h1[:, f, :],
                                          w_sb[:, bass.ds(e, 1), 1, f * DM:(f + 1) * DM].rearrange("p o n -> p (o n)"),
                                          start=(f == 0), stop=(f == HF - 1))
                mm.then_inc(N["dn"], 1)

            pe.wait_ge(N["owner"], 1)
            pe.wait_ge(N["slots"], 1)
            rows_in(0, 0)
            up(0)
            rows_in(0, 1)
            turn_hidden(0)

            def turn(i, ups=True, rows=None):
                e = expert_of(i, mybir.EngineType.PE)
                if ups:
                    up(i + 1)
                if rows:
                    rows_in(*rows)
                down(i, e)
                if ups:
                    turn_hidden(i + 1)

            with pe.Fori(0, (SLOT_TILES - 3) // 2) as pair:
                for slot in range(2):
                    turn(2 * pair + slot, rows=(pair + 1, slot))
            turn(SLOT_TILES - 3, rows=((SLOT_TILES - 1) // 2, 0))
            turn(SLOT_TILES - 2)
            turn(SLOT_TILES - 1, ups=False)

        def up_weights(e, half):
            one = w_sb[:, bass.ds(e, 1), 0, :].rearrange("p o (c n) -> p (o c) n", c=2)
            return one[:, :, half * 512:(half + 1) * 512]

        def moe1_act(act):
            def copy_pre(i, half):
                act.wait_ge(N["up"], 2 * i + half + 1)
                nc.scalar.copy(pre[:, half * 512:(half + 1) * 512], ps[:, half, :]).then_inc(N["pre"], 1)

            def split_up(i, half, e):
                nc.scalar.copy(up_r[:, 0, :, half * 512:(half + 1) * 512], up_weights(e, half)).then_inc(M["w_hi"], 1)

            def split_rows(i):
                act.wait_ge(N["xt_ps"], i + 1)
                nc.scalar.copy(xt_r[:, 0, :, :].rearrange("p c n -> p (c n)"), ps[:, 6, 0:DM]).then_inc(M["x_hi"], 1)

            def gelu(i):
                for half in range(2):
                    act.wait_ge(N["hb"], 2 * i + half + 1)
                    part = h1[:, 4 * half:4 * half + 4, :]
                    nc.scalar.activation(part, part, ACT.Gelu_apprx_tanh).then_inc(N["h"], 1)

            nc.scalar.preload_act_table(ACT.Gelu_apprx_tanh)
            act.wait_ge(N["owner"], 1)
            act.wait_ge(N["xn_d"], 16)
            act.wait_ge(N["w_ready"], 1)
            e = expert_of(0, mybir.EngineType.Activation)
            for half in range(2):
                split_up(0, half, e)
            split_rows(0)

            def turn(i):
                e = expert_of(i + 1, mybir.EngineType.Activation)
                copy_pre(i, 0)
                act.wait_ge(N["w_ready"], i + 2)
                split_up(i + 1, 0, e)
                copy_pre(i, 1)
                split_up(i + 1, 1, e)
                split_rows(i + 1)
                gelu(i)

            turn(0)
            with act.Fori(1, SLOT_TILES - 1) as i:
                turn(i)
            for half in range(2):
                copy_pre(SLOT_TILES - 1, half)
            gelu(SLOT_TILES - 1)

        def moe1_dve(dve):
            v = nc.vector

            def low_parts(i):
                e = expert_of(i, mybir.EngineType.DVE)
                for half in range(2):
                    dve.wait_ge(M["w_hi"], EXPERTS + 2 * i + half + 1)
                    at = slice(half * 512, (half + 1) * 512)
                    v.tensor_tensor(up_r[:, 1, :, at], up_weights(e, half), up_r[:, 0, :, at].bitcast(F32), ALU.subtract
                                    ).then_inc(M["w_lo"], 1)
                dve.wait_ge(M["x_hi"], X_SPLITS + 3 * EXPERTS + i + 1)
                v.tensor_tensor(xt_r[:, 1, :, :].rearrange("p c n -> p (c n)"), ps[:, 6, 0:DM],
                                xt_r[:, 0, :, :].rearrange("p c n -> p (c n)").bitcast(F32), ALU.subtract
                                ).then_inc(N["xt"], 1)

            def add_bias(i):
                e = expert_of(i, mybir.EngineType.DVE)
                if not isinstance(i, int) or i:
                    dve.wait_ge(N["dn"], i)
                for half in range(2):
                    dve.wait_ge(N["hT"], 2 * i + half + 1)
                    bias = b1_sb[:, bass.ds(e, 1), 4 * half:4 * half + 4].rearrange("p o f -> p (o f)")
                    v.tensor_tensor(h1[:, 4 * half:4 * half + 4, :],
                                    ps[:, 2 + half, :].rearrange("p (f n) -> p f n", f=4),
                                    bias.unsqueeze(2).to_broadcast([P, 4, P]), ALU.add).then_inc(N["hb"], 1)

            def result(i):
                if not isinstance(i, int) or i:
                    dve.wait_ge(N["y_out"], 16 * i)
                dve.wait_ge(N["dn"], i + 1)
                v.tensor_copy(y_sb[:, :], ps[:, 4, 0:DM]).then_inc(N["y"], 1)

            low_parts(0)
            low_parts(1)
            add_bias(0)
            low_parts(2)
            result(0)
            add_bias(1)
            with dve.Fori(1, SLOT_TILES - 2) as i:
                low_parts(i + 2)
                result(i)
                add_bias(i + 1)
            result(SLOT_TILES - 2)
            add_bias(SLOT_TILES - 1)
            result(SLOT_TILES - 1)

        def results_dve(dve):
            v = nc.vector
            for t in range(NT):
                dve.wait_ge(N[f"got{t // 2}"], 16)
                for k in range(2):
                    dve.wait_ge(N["acc"], NT + 2 * t + k if k else NT)
                    v.scalar_tensor_tensor(X[:, t, :], got[t // 4][:, 2 * (t % 4) + k, :], pair_w[:, k, t:t + 1], X[:, t, :],
                                           ALU.mult, ALU.add).then_inc(N["acc"], 1)
            dve.wait_ge(N["acc"], 3 * NT)

        block = ctx.enter_context(nc.Block())

        @block.sync
        def _(sp):
            sp.dma_start(ident[:, :], a["ident"]).then_inc(ld_const, 16)
            sp.dma_start(ctx_in[:, :, :], a["ctx_1024"].rearrange("b (h p) d -> p (b h) d", p=P)).then_inc(ld_ctx, 16)
            sp.dma_start(in_w[:, :, :], a["L0_xattn_in_proj_w"].rearrange("(e p) d -> p e d", p=P)).then_inc(ld_ssm, 16)
            sp.dma_start(x_w[:, :], a["L0_xattn_x_proj_w"]).then_inc(ld_ssm, 16)
            sp.dma_start(dt_w[:, :, :], a["L0_xattn_dt_proj_w"].rearrange("(e p) d -> p e d", p=P)).then_inc(ld_ssm, 16)
            sp.dma_start(cols[:, :, 0:DC], a["L0_xattn_conv_w"].rearrange("(e p) d -> p e d", p=P)).then_inc(ld_ssm, 16)
            for k, n in enumerate(["conv_b", "dt_proj_b", "D"]):
                sp.dma_start(cols[:, :, DC + k:DC + k + 1],
                             a["L0_xattn_" + n].rearrange("(e p o) -> p e o", p=P, o=1),
                             allow_slow_non_contiguous=True).then_inc(ld_ssm, 16)
            sp.dma_start(a_log[:, :, :], a["L0_xattn_A_log"].rearrange("(e p) d -> p e d", p=P)).then_inc(ld_ssm, 16)
            sp.dma_start(gates[:, 0:2], a["g_xattn"].unsqueeze(0).to_broadcast([P, 2])).then_inc(ld_gate, 16)
            sp.dma_start(gates[:, 2:4], a["g_ffn"].unsqueeze(0).to_broadcast([P, 2])).then_inc(ld_gate, 16)
            sp.dma_start(temp[:, :], a["L0_ffn_temperature"].unsqueeze(0).to_broadcast([P, 1])).then_inc(ld_gate, 16)
            sp.dma_start(rows[:, :], a["rows"]).then_inc(ld_const, 16)
            sp.dma_start(before[:, :, :], a["before"]).then_inc(ld_const, 16)
            sp.dma_start(freq[:, :], a["freq"]).then_inc(ld_const, 16)
            sp.dma_start(X[:, :, :], a["x"].rearrange("b (h p) d -> p (b h) d", p=P)).then_inc(ld_x, 16)
            sp.dma_start(posT[:, :], a["fside_BxSx2_0"].rearrange("b s a -> a (b s)"),
                         allow_slow_non_contiguous=True).then_inc(ld_pos, 16)
            att_sp_weights(sp)
            sp.wait_ge(N["blank"], 1)
            moe0_sp(sp)
            keys_sp(sp)
            att_sp(sp)
            sp.wait_ge(T["X3"], NT)
            moe1_sp(sp)
            out_rows = out.rearrange("b (h p) d -> p (b h) d", p=P)
            for k in range(4):
                sp.wait_ge(N["acc"], NT + 4 * k + 4)
                sp.dma_start(out_rows[:, 2 * k:2 * k + 2, :], X[:, 2 * k:2 * k + 2, :]).then_inc(stored, 16)
            sp.wait_ge(stored, 64)

        @block.vector
        def _(dve):
            nc.vector.memset(minushalf[:, :], -0.5).then_inc(set_up, 1)
            nc.vector.memset(ones_row[:, :], 1.0).then_inc(set_up, 1)
            nc.vector.memset(blank[:, :], 0.0).then_inc(N["blank"], 1)
            ssm_dve(dve)
            ln_dve(dve, 1)
            gate0_dve(dve)
            moe0_dve(dve)
            ln_dve(dve, 2, early=True)
            att_dve(dve)
            ln_dve(dve, 3, early=True)
            gate1_dve(dve)
            moe1_dve(dve)
            bias_dve(dve)
            results_dve(dve)

        @block.gpsimd
        def _(pool):
            pool.wait_ge(set_up, 3)
            ln_pool(pool, 0)
            angles_pool(pool)
            ssm_pool(pool)
            ln_pool(pool, 1)
            keys_pool(pool)
            ln_pool(pool, 2)
            pool.wait_ge(M["acc"], 8 + 8 * EXPERTS)
            pool.wait_ge(L["rstd"], 3)
            blank_rows(pool, 1)
            blank_rows(pool, 2)
            att_pool(pool)
            ln_pool(pool, 3)
            moe1_pool(pool)

        @block.scalar
        def _(act):
            ssm_act(act)
            kv_act(act)
            ln_act(act, 1)
            gate0_act(act)
            moe0_act(act)
            ln_act(act, 2)
            att_act(act)
            ln_act(act, 3)
            gate1_act(act)
            moe1_act(act)
            bias_act(act)

        @block.tensor
        def _(pe):
            ssm_pe(pe)
            kv_pe(pe)
            ln_pe(pe, 1)
            gate0_pe(pe)
            moe0_pe(pe)
            ln_pe(pe, 2)
            att_pe(pe)
            ln_pe(pe, 3)
            gate1_pe(pe)
            moe1_pe(pe)
            bias_pe(pe)


def kernel(**inputs):
    import concourse.bacc as bacc
    from concourse.bass_utils import run_bass_kernel_spmd as run

    nc = bacc.Bacc("TRN2", target_bir_lowering=False, num_devices=1)
    arrays, args = {}, {}
    for name, value in {**inputs, **constants()}.items():
        v = np.ascontiguousarray(value)
        arrays["in_" + name] = v
        args[name] = nc.dram_tensor("in_" + name, v.shape, mybir.dt.from_np(v.dtype), kind="ExternalInput").ap()
    out = nc.dram_tensor("out_x", (BATCH, SEQ, DM), F32, kind="ExternalOutput").ap()
    program(nc, args, out)
    return run(nc, [arrays], core_ids=[0]).results[0]["out_x"]
```
